# Optimizing a Trainium2 kernel written in Bass

```python
import numpy as np
import jax
import jax.numpy as jnp

def _softmax(x, axis=-1):
    return jax.nn.softmax(x, axis=axis)

def _gelu(x):
    return jax.nn.gelu(x, approximate=True)

def _silu(x):
    return jax.nn.silu(x)

def _sigmoid(x):
    return jax.nn.sigmoid(x)

def _layernorm(x, axis=-1, eps=1e-05):
    m = jnp.mean(x, axis=axis, keepdims=True)
    v = jnp.var(x, axis=axis, keepdims=True)
    return (x - m) / jnp.sqrt(v + eps)

def _scatter_add(tgt, idx, src, axis=0):
    return tgt.at[idx].add(src)

def _segment_sum(src, seg, n):
    return jax.ops.segment_sum(src, seg, n)
kernel_name = 'mk_macaron_d1_jaxref_r4_c71fda'

def setup_inputs(seed: int=0):
    np.random.seed(seed)
    _w = jnp.asarray

    def _L0_attn_setup():
        import jax, jax.numpy as jnp
        import numpy as np
        D_MODEL = 256
        key = jax.random.key(seed)
        kx, kq, kk, kv, ko = jax.random.split(key, 5)
        s = 1.0 / np.sqrt(D_MODEL)
        return {'x': jax.random.normal(kx, (4, 1024, D_MODEL), dtype=jnp.float32), 'W_q': jax.random.normal(kq, (D_MODEL, D_MODEL), dtype=jnp.float32) * s, 'W_k': jax.random.normal(kk, (D_MODEL, D_MODEL), dtype=jnp.float32) * s, 'W_v': jax.random.normal(kv, (D_MODEL, D_MODEL), dtype=jnp.float32) * s, 'W_o': jax.random.normal(ko, (D_MODEL, D_MODEL), dtype=jnp.float32) * s}
    _L0_attn_in = _L0_attn_setup()

    def _L0_ffn_setup():
        import jax, jax.numpy as jnp
        import numpy as np
        B, S, H, FF, E = (4, 1024, 256, 1024, 8)
        EPS = 1e-05
        key = jax.random.key(seed)
        ks = jax.random.split(key, 8)
        std = 0.02
        return {'x': jax.random.normal(ks[0], (B, S, H), jnp.float32), 'norm_weight': jnp.ones((H,), jnp.float32), 'router_w': jax.random.normal(ks[1], (E, H), jnp.float32) * std, 'router_b': jnp.zeros((E,), jnp.float32), 'fc1_w': jax.random.normal(ks[2], (E, FF, H), jnp.float32) * std, 'fc1_b': jnp.zeros((E, FF), jnp.float32), 'fc2_w': jax.random.normal(ks[3], (E, H, FF), jnp.float32) * std, 'fc2_b': jnp.zeros((E, H), jnp.float32)}
    _L0_ffn_in = _L0_ffn_setup()
    _d = {'L0_attn_x': _L0_attn_in['x'], 'L0_attn_W_q': _L0_attn_in['W_q'], 'L0_attn_W_k': _L0_attn_in['W_k'], 'L0_attn_W_v': _L0_attn_in['W_v'], 'L0_attn_W_o': _L0_attn_in['W_o'], 'L0_ffn_norm_weight': _L0_ffn_in['norm_weight'], 'L0_ffn_router_w': _L0_ffn_in['router_w'], 'L0_ffn_router_b': _L0_ffn_in['router_b'], 'L0_ffn_fc1_w': _L0_ffn_in['fc1_w'], 'L0_ffn_fc1_b': _L0_ffn_in['fc1_b'], 'L0_ffn_fc2_w': _L0_ffn_in['fc2_w'], 'L0_ffn_fc2_b': _L0_ffn_in['fc2_b']}
    _x0 = _d['L0_attn_x']
    _d['L0_attn_x'] = jax.random.normal(jax.random.fold_in(jax.random.key(seed), 1), (32, 512, 256), dtype=_x0.dtype)
    del _x0
    return _d

def reference(L0_attn_x, L0_attn_W_q, L0_attn_W_k, L0_attn_W_v, L0_attn_W_o, L0_ffn_norm_weight, L0_ffn_router_w, L0_ffn_router_b, L0_ffn_fc1_w, L0_ffn_fc1_b, L0_ffn_fc2_w, L0_ffn_fc2_b):

    def _L0_attn_ref(x, W_q, W_k, W_v, W_o):
        import jax, jax.numpy as jnp
        import numpy as np
        D_MODEL = 256
        B, T, D = x.shape
        q = jnp.einsum('btd,ed->bte', x, W_q)
        k = jnp.einsum('btd,ed->bte', x, W_k)
        v = jnp.einsum('btd,ed->bte', x, W_v)
        scale = 1.0 / jnp.sqrt(jnp.asarray(D, x.dtype))
        scores = jnp.einsum('bqd,bkd->bqk', q, k) * scale
        causal = jnp.tril(jnp.ones((T, T), dtype=bool))
        scores = jnp.where(causal, scores, -jnp.inf)
        att = jax.nn.softmax(scores, axis=-1)
        y = jnp.einsum('bqk,bkd->bqd', att, v)
        out = jnp.einsum('btd,ed->bte', y, W_o)
        return out

    def _L0_ffn_ref(x, norm_weight, router_w, router_b, fc1_w, fc1_b, fc2_w, fc2_b):
        import jax, jax.numpy as jnp
        import numpy as np
        B, S, H, FF, E = (4, 1024, 256, 1024, 8)
        EPS = 1e-05
        b, s, h = x.shape
        T = b * s
        e = router_w.shape[0]
        cap = T // e
        x_flat = x.reshape(T, h)
        xn = x_flat * jax.lax.rsqrt(jnp.mean(x_flat * x_flat, axis=-1, keepdims=True) + EPS) * norm_weight
        logits = xn @ router_w.T + router_b
        probs = jax.nn.softmax(logits, axis=-1)
        gates, idx = jax.lax.top_k(probs.T, cap)
        xe = xn[idx]
        hmid = jnp.einsum('ech,efh->ecf', xe, fc1_w) + fc1_b[:, None, :]
        hmid = jax.nn.gelu(hmid, approximate=False)
        ye = jnp.einsum('ecf,ehf->ech', hmid, fc2_w) + fc2_b[:, None, :]
        flat_idx = idx.reshape(-1)
        weighted = (ye * gates[..., None]).reshape(-1, h)
        out = jnp.zeros((T, h), x.dtype).at[flat_idx].add(weighted)
        gate_sums = jnp.zeros((T, 1), x.dtype).at[flat_idx].add(gates.reshape(-1, 1))
        out = out / jnp.maximum(gate_sums, 1e-09)
        return out.reshape(b, s, h)
    x = L0_attn_x
    x = x + 0.5 * _L0_ffn_ref(_layernorm(x, axis=-1), L0_ffn_norm_weight, L0_ffn_router_w, L0_ffn_router_b, L0_ffn_fc1_w, L0_ffn_fc1_b, L0_ffn_fc2_w, L0_ffn_fc2_b)
    x = x + _L0_attn_ref(_layernorm(x, axis=-1), L0_attn_W_q, L0_attn_W_k, L0_attn_W_v, L0_attn_W_o)
    x = x + 0.5 * _L0_ffn_ref(_layernorm(x, axis=-1), L0_ffn_norm_weight, L0_ffn_router_w, L0_ffn_router_b, L0_ffn_fc1_w, L0_ffn_fc1_b, L0_ffn_fc2_w, L0_ffn_fc2_b)
    return x

_drawn_inputs = setup_inputs


def setup_inputs(seed=0):
    import zlib

    import numpy as np

    out = dict(_drawn_inputs(seed))
    spreads = {'L0_ffn_norm_weight': (1.0, 0.2),
     'L0_ffn_router_b': (0.0, 0.525),
     'L0_ffn_fc1_b': (0.0, 0.276),
     'L0_ffn_fc2_b': (0.0, 0.1)}
    factors = {}
    for name, (base, spread) in spreads.items():
        noise = np.random.default_rng([zlib.crc32(name.encode()), seed]).standard_normal(out[name].shape)
        drawn = base * np.exp(spread * noise) if base else spread * noise
        out[name] = jnp.asarray(drawn.astype(out[name].dtype))
    for name, factor in factors.items():
        out[name] = (out[name] * factor).astype(out[name].dtype)
    return out
```

```python
from contextlib import ExitStack

import concourse.bass as bass
from concourse import mybir
from concourse.alu_op_type import AluOpType as ALU

F32 = mybir.dt.float32
F16 = mybir.dt.float16
BF16 = mybir.dt.bfloat16
I32 = mybir.dt.int32
U32 = mybir.dt.uint32
ACT = mybir.ActivationFunctionType
AX = mybir.AxisListType


class Steps:

    def __init__(self, engine, sem):
        self.engine, self.sem, self.n = engine, sem, 0

    def done(self, instruction):
        instruction.then_inc(self.sem, 1)
        self.n = self.n + 1

    def sync(self):
        self.engine.wait_ge(self.sem, self.n)

    def link(self, instruction):
        self.done(instruction)
        self.sync()


def repeat(engine, steps, body, count, last=None):
    before = steps.n
    body(0)
    per = steps.n - before
    end = count - 1 if last else count
    with engine.Fori(1, end) as i:
        steps.n = i * per + before
        body(i)
    steps.n = before + end * per
    if last:
        last(end)


def wait(engine, sem, value):
    if not isinstance(value, int) or value > 0:
        engine.wait_ge(sem, value)


def macaron(nc, x, wq, wk, wv, wo_t, norm_w, router_t, router_b, fc1_t, fc1_b, fc2_t, fc2_b, out):
    P = 128
    B, S, D = x.shape
    T = B * S
    NE, _, FF = fc1_t.shape
    CAP = T // NE
    NT = T // P
    KD = D // P
    KF = FF // P
    TG = S // P
    NG = T // S
    NC = CAP // S
    SLOTS = CAP // P
    EPS = 1e-5
    WS = 64.0
    HS = 16.0
    YS = WS * HS
    SCORE = 1.0 / (D ** 0.5 * WS)
    BITS = 30
    PER = P // NE
    NV = 5
    QT = P // NC
    assert KD == 2 and TG == 4 and NC == 4 and PER * NE == P and NT == P

    xf = x.rearrange("b s d -> (b s) d")
    outf = out.rearrange("b s d -> (b s) d")
    x1_d = nc.dram_tensor("x1_d", [T, D], F32).ap()
    z_d = nc.dram_tensor("z_d", [T, D], F32).ap()

    def group(d, g):
        return d.rearrange("(g j p) d -> g p j d", p=P, j=TG)[g]

    ctx = ExitStack()
    with ctx:
        def sb(name, shape, dt, stack=ctx):
            return stack.enter_context(nc.sbuf_tensor(name, shape, dt))

        def sem(name):
            return ctx.enter_context(nc.semaphore(name))

        ident = sb("ident", [P, P], F32)
        ident_b = sb("ident_b", [P, P], BF16)
        causal = sb("causal", [P, P], BF16)
        ones = sb("ones", [P, P], F32)
        ones_h = sb("ones_h", [P, P], F16)
        before = sb("before", [P, P], F32)
        apart = sb("apart", [P, P], I32)
        same_expert = sb("same_expert", [P, P], F32)
        iota_i = sb("iota_i", [P, P], I32)
        iota_b = sb("iota_b", [P, P], BF16)
        iota_c = sb("iota_c", [P, SLOTS, P], BF16)
        part_i = sb("part_i", [P, 1], I32)
        part_f = sb("part_f", [P, 1], F32)
        minus_half = sb("minus_half", [P, TG], F32)
        eps = sb("eps", [P, TG], F32)
        pick0 = sb("pick0", [P, 1], F32)
        pick1 = sb("pick1", [P, 1], F32)
        nw = sb("nw", [P, KD], F32)
        nws = sb("nws", [P, KD], F32)
        rb = sb("rb", [P, NE], F32)
        b1 = sb("b1", [P, NE, KF], F32)
        b1_now = sb("b1_now", [P, 2, KF], F32)
        rw = sb("rw", [P, KD, NE], F32)
        rws = sb("rws", [P, KD, NE], F32)
        rw_h = sb("rw_h", [P, KD, NE], F16)
        rw_l = sb("rw_l", [P, KD, NE], F16)
        g_h = sb("g_h", [P, KD, D], F16)
        g_l = sb("g_l", [P, KD, D], F16)
        m_h = sb("m_h", [P, KD, D], F16)
        m_l = sb("m_l", [P, KD, D], F16)
        logits = sb("logits", [P, NT, NE], F32)
        mv = sb("mv", [P, 2, TG, 2], F32)
        bst = sb("bst", [P, TG, 6], F32)
        nt = sb("nt", [P, 6, TG], F32)
        zs = sb("zs", [P, 2, TG], F32)

        ffn = ExitStack()
        w1_st = sb("w1_st", [P, KD, FF], F32, ffn)
        w2_st = sb("w2_st", [P, KF, D], F32, ffn)
        b2_st = sb("b2_st", [P, D], F32, ffn)
        w1_h = sb("w1_h", [P, KD, FF], F16, ffn)
        w1_l = sb("w1_l", [P, KD, FF], F16, ffn)
        w2_h = sb("w2_h", [P, KF, D], F16, ffn)
        w2_l = sb("w2_l", [P, KF, D], F16, ffn)
        b2_h = sb("b2_h", [P, D], F16, ffn)
        b2_l = sb("b2_l", [P, D], F16, ffn)
        b2_r = sb("b2_r", [P, D], F16, ffn)
        rank_r = sb("rank_r", [P, NE, P], F32, ffn)
        rank_c = sb("rank_c", [P, NE, P], BF16, ffn)
        wp = sb("wp", [P, 3, NE, P], BF16, ffn)
        hot_a = sb("hot_a", [P, 2, QT, P], BF16, ffn)
        hot_b = sb("hot_b", [P, NV, SLOTS, P], BF16, ffn)
        found = sb("found", [P, NV, SLOTS], F32, ffn)
        w_next = sb("w_next", [P, SLOTS], F32, ffn)
        w_now = sb("w_now", [P, SLOTS], F32, ffn)
        tok_next = sb("tok_next", [P, SLOTS], I32, ffn)
        tok_now = sb("tok_now", [P, SLOTS], I32, ffn)
        shared = ExitStack()
        xe = sb("xe", [P, 2, TG, D], F32, shared)
        xt_h = sb("xt_h", [P, 2, KD, S], F16, shared)
        xt_l = sb("xt_l", [P, 2, KD, S], F16, shared)
        hf = sb("hf", [P, 2, S], F32, shared)
        hid_h = sb("hid_h", [P, 2, KF, S], F16, shared)
        hid_l = sb("hid_l", [P, 2, KF, S], F16, shared)
        ys = sb("ys", [P, 2, TG, D], F32, shared)
        shared.close()
        rout = ExitStack()
        p_s = sb("p_s", [P, NE, P], F32, rout)
        p_r = sb("p_r", [P, NE, P], F32, rout)
        above = sb("above", [P, NE, P], F32, rout)
        equal = sb("equal", [P, NE, P], F32, rout)
        scan = sb("scan", [P, NE, P], F32, rout)
        scan2 = sb("scan2", [P, NE, P], F32, rout)
        mask = sb("mask", [P, NE, P], F32, rout)
        ranks = sb("ranks", [P, NE, P], I32, rout)
        bits = sb("bits", [P, NE, P], I32, rout)
        weight = sb("weight", [P, NE, P], F32, rout)
        rowv = sb("rowv", [P, 2, P], F32, rout)
        ten = sb("ten", [P, 10, NE], F32, rout)
        thr = sb("thr", [P, 1], I32, rout)
        cand = sb("cand", [P, 1], I32, rout)
        sel = sb("sel", [P, 1], I32, rout)
        bit_i = sb("bit_i", [P, 1], I32, rout)
        bit_f = sb("bit_f", [P, 1], F32, rout)
        count = sb("count", [P, 1], F32, rout)
        thr_m = sb("thr_m", [P, P], F32, rout)
        rout.close()
        ffn.close()

        att = ExitStack()
        wst = sb("wst", [P, 4, KD, D], F32, att)
        xin = sb("xin", [P, 2, TG, D], F32, att)
        zz = sb("zz", [P, 2, TG, D], F32, att)
        zt_h = sb("zt_h", [P, 2, KD, S], F16, att)
        zt_l = sb("zt_l", [P, 2, KD, S], F16, att)
        u_h = sb("u_h", [P, KD, S], F16, att)
        u_l = sb("u_l", [P, KD, S], F16, att)
        v_h = sb("v_h", [P, TG, D], F16, att)
        v_l = sb("v_l", [P, TG, D], F16, att)
        pr = sb("pr", [P, TG, S], F32, att)
        pt_h = sb("pt_h", [P, 2, S], F16, att)
        pt_l = sb("pt_l", [P, 2, S], F16, att)
        x2 = sb("x2", [P, 2, TG, D], F32, att)
        z2 = sb("z2", [P, 2, TG, D], F32, att)
        z2t_h = sb("z2t_h", [P, KD, S], F16, att)
        z2t_l = sb("z2t_l", [P, KD, S], F16, att)
        nmax = sb("nmax", [P, TG], F32, att)
        nbias = sb("nbias", [P, TG], F32, att)
        rsum = sb("rsum", [P, TG], F32, att)
        rinv = sb("rinv", [P, TG], F32, att)
        att.close()

        ps = [ctx.enter_context(nc.psum_tensor(f"ps{i}", [P, 2, 512], F32)) for i in range(4)]

        def bank(i):
            return ps[i // 2][:, i % 2, :]

        s_phase = sem("s_phase")
        s_pool, s_dve, s_act = sem("s_pool"), sem("s_dve"), sem("s_act")
        s_const, s_small, s_split = sem("s_const"), sem("s_small"), sem("s_split")
        s_gm = sem("s_gm")
        s_in = [sem("s_in0"), sem("s_in1")]
        s_mv, s_scale, s_z = sem("s_mv"), sem("s_scale"), sem("s_z")
        s_zst = [sem("s_zst0"), sem("s_zst1")]
        s_x2st = [sem("s_x2st0"), sem("s_x2st1")]
        s_tp, s_th, s_tl = sem("s_tp"), sem("s_th"), sem("s_tl")
        s_lg, s_lge = sem("s_lg"), sem("s_lge")
        s_copy = sem("s_copy")
        s_passed = [sem("s_passed0"), sem("s_passed1")]
        s_exp, s_pt, s_route, s_prr, s_cnt, s_tot = (sem(n) for n in ("s_exp", "s_pt", "s_route", "s_prr", "s_cnt", "s_tot"))
        s_w1d, s_w2d, s_b2d = sem("s_w1d"), sem("s_w2d"), sem("s_b2d")
        s_w1h, s_w1, s_w2h, s_w2 = sem("s_w1h"), sem("s_w1"), sem("s_w2h"), sem("s_w2")
        s_xe = [sem("s_xe0"), sem("s_xe1")]
        s_sc = [sem("s_sc0"), sem("s_sc1")]
        s_xt, s_xth, s_xtl = sem("s_xt"), sem("s_xth"), sem("s_xtl")
        s_h, s_gelu, s_hh, s_hl = sem("s_h"), sem("s_gelu"), sem("s_hh"), sem("s_hl")
        s_y, s_ys = sem("s_y"), sem("s_ys")
        s_hot, s_oh, s_idx, s_now = sem("s_hot"), sem("s_oh"), sem("s_idx"), sem("s_now")
        s_s, s_max, s_prob = sem("s_s"), sem("s_max"), sem("s_prob")
        s_ptp, s_pth, s_ptl = sem("s_ptp"), sem("s_pth"), sem("s_ptl")
        s_o, s_x2 = sem("s_o"), sem("s_x2")
        s_u, s_uh, s_ul = sem("s_u"), sem("s_uh"), sem("s_ul")
        s_v, s_vh, s_vl = sem("s_v"), sem("s_vh"), sem("s_vl")
        s_z2t, s_z2h, s_z2l = sem("s_z2t"), sem("s_z2h"), sem("s_z2l")
        s_aux, s_trp = sem("s_aux"), sem("s_trp")
        s_mv2, s_scale2, s_z2 = sem("s_mv2"), sem("s_scale2"), sem("s_z2")

        block = ctx.enter_context(nc.Block())
        ENGINES = 5

        def stage_end(engine, k):
            engine.drain().then_inc(s_phase, 1)
            engine.wait_ge(s_phase, ENGINES * k)

        @block.sync
        def _(sp):
            steps = Steps(sp, s_phase)
            for dst, src in ((nw[:, :], norm_w), (rb[:, :], router_b.rearrange("(a e) -> a e", a=1).broadcast_to([P, NE])),
                             (b1[:, :, :], fc1_b),
                             (rw[:, :, :], router_t.rearrange("(k p) e -> p k e", p=P)),
                             (wst[:, 0], wq.rearrange("(k p) e -> p k e", p=P)),
                             (wst[:, 1], wk.rearrange("(k p) e -> p k e", p=P)),
                             (wst[:, 2], wv.rearrange("(k p) e -> p k e", p=P)),
                             (wst[:, 3], wo_t.rearrange("(k p) e -> p k e", p=P))):
                sp.dma_start(dst, src).then_inc(s_small, 16)

            def scan_pair(i):
                for u in range(2):
                    g = 2 * i + u
                    wait(sp, s_z, g - 1)
                    sp.dma_start(xin[:, u], group(xf, g)).then_inc(s_in[u], 16)
                for u in range(2):
                    g = 2 * i + u
                    sp.wait_ge(s_z, g + 1)
                    sp.dma_start(group(z_d, g), zz[:, u]).then_inc(s_zst[u], 16)
            repeat(sp, steps, scan_pair, NG // 2)
            steps.n = 0
            sp.dma_start(x1_d.rearrange("(a b) d -> a (b d)", b=8), xf.rearrange("(a b) d -> a (b d)", b=8)).then_inc(s_copy, 16)
            for u in range(2):
                sp.wait_ge(s_zst[u], 16 * (NG // 2))
            stage_end(sp, 1)

            def ffn_loads(layer):
                def load(e):
                    E = e + layer * NE
                    wait(sp, s_w1, E)
                    sp.dma_start(w1_st[:, :, :], fc1_t[e].rearrange("(k p) f -> p k f", p=P)).then_inc(s_w1d, 16)
                    wait(sp, s_w2, E)
                    sp.dma_start(w2_st[:, :, :], fc2_t[e].rearrange("(k p) d -> p k d", p=P)).then_inc(s_w2d, 16)
                    sp.dma_start(b2_st[:, :], fc2_b[e].rearrange("(a d) -> a d", a=1).broadcast_to([P, D])).then_inc(s_b2d, 16)
                repeat(sp, steps, load, NE)
                steps.n = 0

            ffn_loads(0)
            stage_end(sp, 2)

            def att_loads(i):
                for u in range(2):
                    b = 2 * i + u
                    wait(sp, s_x2, TG * (b - 1))
                    sp.dma_start(xin[:, u], group(x1_d, b)).then_inc(s_in[u], 16)
                    store(b - 1, 1 - u)

            def store(b, u):
                if isinstance(b, int) and b < 0:
                    return
                sp.wait_ge(s_x2, TG * (b + 1))
                sp.dma_start(group(outf, b), x2[:, u]).then_inc(s_x2st[u], 16)
                sp.wait_ge(s_z2, b + 1)
                sp.dma_start(group(z_d, b), z2[:, u]).then_inc(s_zst[u], 16)

            repeat(sp, steps, att_loads, NG // 2)
            store(NG - 1, 1)
            for u in range(2):
                sp.wait_ge(s_x2st[u], 16 * (NG // 2))
                sp.wait_ge(s_zst[u], 16 * NG)
            stage_end(sp, 3)
            ffn_loads(1)
            stage_end(sp, 4)

        @block.gpsimd
        def _(pool):
            steps = Steps(pool, s_pool)
            pool.memset(ident[:, :], 0.0)
            pool.memset(ident_b[:, :], 0.0)
            pool.memset(causal[:, :], 0.0)
            pool.memset(ones[:, :], 1.0)
            pool.memset(ones_h[:, :], 1.0)
            pool.memset(before[:, :], 1.0)
            pool.memset(minus_half[:, :], -0.5)
            pool.memset(eps[:, :], EPS)
            pool.memset(pick0[:, :], 0.0)
            pool.memset(pick1[:, :], 0.0)
            pool.iota(iota_i[:, :], pattern=[[1, P]], base=0, channel_multiplier=0)
            steps.link(pool.iota(part_i[:, :], pattern=[[0, 1]], base=0, channel_multiplier=1))
            for m in (ident, ident_b):
                pool.affine_select(out=m[:, :], in_=m[:, :], compare_op=ALU.not_equal, fill=1.0, base=0,
                                   pattern=[[-1, P]], channel_multiplier=1)
            pool.affine_select(out=causal[:, :], in_=causal[:, :], compare_op=ALU.is_ge, fill=-1e30, base=0,
                               pattern=[[-1, P]], channel_multiplier=1)
            pool.affine_select(out=before[:, :], in_=before[:, :], compare_op=ALU.is_gt, fill=0.0, base=0,
                               pattern=[[1, P]], channel_multiplier=-1)
            pool.affine_select(out=pick0[:, :], in_=pick0[:, :], compare_op=ALU.not_equal, fill=1.0, base=0,
                               pattern=[[0, 1]], channel_multiplier=1)
            pool.affine_select(out=pick1[:, :], in_=pick1[:, :], compare_op=ALU.not_equal, fill=1.0, base=-1,
                               pattern=[[0, 1]], channel_multiplier=1)
            pool.iota(apart[:, :], pattern=[[1, P]], base=P, channel_multiplier=-1)
            pool.tensor_copy(part_f[:, :], part_i[:, :])
            pool.tensor_copy(iota_b[:, :], iota_i[:, :])
            pool.iota(iota_c[:, :, :], pattern=[[1, SLOTS], [0, P]], base=0, channel_multiplier=0,
                      allow_small_or_imprecise_dtypes=True).then_inc(s_const, 1)

            def row_scale(turn):
                v = mv[:, turn, :, 1]
                a, r, q, q2, c, r2 = (nt[:, k, :] for k in range(6))
                steps.link(pool.tensor_tensor(a, v, eps[:, :], ALU.add))
                steps.link(pool.tensor_tensor(r, a, minus_half[:, :], ALU.pow))
                steps.link(pool.tensor_tensor(q, v, r, ALU.mult))
                steps.link(pool.tensor_tensor(q2, q, r, ALU.mult))
                steps.link(pool.tensor_tensor(c, q2, eps[:, :], ALU.add))
                steps.link(pool.tensor_tensor(r2, c, minus_half[:, :], ALU.pow))
                return pool.tensor_tensor(zs[:, turn, :], r, r2, ALU.mult)

            def scan_pair(i):
                for u in range(2):
                    g = 2 * i + u
                    pool.wait_ge(s_mv, g + 1)
                    row_scale(0).then_inc(s_scale, 1)
            repeat(pool, steps, scan_pair, NG // 2)
            stage_end(pool, 1)

            def ffn_rows(layer, rows, acc):
                def gather(E, c):
                    n = NC * E + c
                    wait(pool, s_xt, n - 1)
                    pool.sem_inc(s_passed[0], 1)
                    for t in range(TG):
                        k = TG * c + t
                        pool.indirect_dma_start(xe[:, c % 2, t, :], None, rows,
                                                bass.IndirectOffsetOnAxis(ap=tok_next[:, k:k + 1].bitcast(U32), axis=0)).then_inc(s_xe[c % 2], 16)

                def scatter(E, c):
                    n = NC * E + c
                    if c == 0:
                        pool.wait_ge(s_now, E + 1)
                    pool.wait_ge(s_ys, TG * (n + 1))
                    pool.sem_inc(s_passed[0], 1)
                    for t in range(TG):
                        k = TG * c + t
                        pool.indirect_dma_start(acc, bass.IndirectOffsetOnAxis(ap=tok_now[:, k:k + 1].bitcast(U32), axis=0),
                                                ys[:, c % 2, t, :], None, compute_op=ALU.add).then_inc(s_sc[c % 2], 16)

                def expert(e, final=False):
                    E = e + layer * NE
                    gather(E, 2)
                    gather(E, 3)
                    scatter(E, 0)
                    scatter(E, 1)
                    if not final:
                        pool.wait_ge(s_idx, E + 2)
                        gather(E + 1, 0)
                        gather(E + 1, 1)
                    scatter(E, 2)
                    scatter(E, 3)

                pool.wait_ge(s_idx, layer * NE + 1)
                pool.wait_ge(s_copy, 16)
                gather(layer * NE, 0)
                gather(layer * NE, 1)
                repeat(pool, steps, expert, NE, lambda e: expert(e, True))
                for u in range(2):
                    pool.wait_ge(s_sc[u], 16 * TG * (NC // 2) * NE * (layer + 1))

            ffn_rows(0, z_d, x1_d)
            stage_end(pool, 2)

            def att_pair(i):
                for u in range(2):
                    b = 2 * i + u
                    pool.wait_ge(s_mv, NG + b + 1)
                    row_scale(0).then_inc(s_scale, 1)
                    if isinstance(b, int) and b == 0:
                        continue
                    pool.wait_ge(s_mv2, b)
                    row_scale(1).then_inc(s_scale2, 1)
            n0 = steps.n
            att_pair(0)
            per = 2 * 12
            with pool.Fori(1, NG // 2) as i:
                steps.n = i * per + (n0 - 6)
                att_pair(i)
            steps.n = n0 - 6 + per * (NG // 2)
            pool.wait_ge(s_mv2, NG)
            row_scale(1).then_inc(s_scale2, 1)
            stage_end(pool, 3)
            ffn_rows(1, z_d, outf)
            stage_end(pool, 4)

        @block.scalar
        def _(act):
            steps = Steps(act, s_act)

            def copy(dst, src, **kw):
                return act.activation(dst, src, ACT.Copy, **kw)

            act.wait_ge(s_small, 16 * 8)
            act.wait_ge(s_const, 1)
            steps.link(copy(nws[:, :], nw[:, :], scale=WS))
            for k in range(KD):
                steps.link(copy(rws[:, k, :], rw[:, k, :], scale=nws[:, k:k + 1]))
                steps.link(copy(rw_h[:, k, :], rws[:, k, :]))
            act.wait_ge(s_gm, 1)
            for dst, b0 in ((g_h, 0), (m_h, 2)):
                for k in range(KD):
                    steps.link(copy(dst[:, k, :], bank(b0 + k)[:, 0:D], scale=WS))
            copy(nbias[:, 0:1], nws[:, 0:1]).then_inc(s_split, 1)

            def th(g, u):
                act.wait_ge(s_tp, g + 1)
                wait(act, s_lg, g - 1)
                copy(zt_h[:, u], ps[u][:, :, :]).then_inc(s_th, 1)

            def scan_pair(i):
                for u in range(2):
                    th(2 * i + u, u)
            repeat(act, steps, scan_pair, NG // 2)
            stage_end(act, 1)

            def route(layer):
                act.wait_ge(s_route, 3 * layer + 1)
                act.activation(logits[:, :, :], logits[:, :, :], ACT.Exp).then_inc(s_exp, 1)
                act.wait_ge(s_pt, layer + 1)
                copy(p_r[:, :, :].rearrange("p e j -> p (e j)"), ps[0][:, :, :].rearrange("p a b -> p (a b)")).then_inc(s_prr, 1)

            def ffn(layer):
                def xt_hi(E, c):
                    n = NC * E + c
                    act.wait_ge(s_xt, n + 1)
                    wait(act, s_h, KF * (n - 1))
                    copy(xt_h[:, c % 2], ps[0][:, :, :]).then_inc(s_xth, 1)

                def gelu(e, E, c):
                    n = NC * E + c
                    steps.link(copy(b1_now[:, c % 2, :], b1[:, e, :]))
                    wait(act, s_y, TG * (n - 1))
                    for f in range(KF):
                        act.wait_ge(s_h, KF * n + f + 1)
                        wait(act, s_hl, KF * n + f - 1)
                        act.activation(hf[:, f % 2, :], bank(2 + f % 2), ACT.Gelu, bias=b1_now[:, c % 2, f:f + 1],
                                       scale=1.0 / WS).then_inc(s_gelu, 1)
                        act.wait_ge(s_gelu, KF * n + f + 1)
                        copy(hid_h[:, c % 2, f, :], hf[:, f % 2, :], scale=HS).then_inc(s_hh, 1)

                def w1_hi(E):
                    act.wait_ge(s_w1d, 16 * (E + 1))
                    wait(act, s_h, KF * NC * E)
                    for k in range(KD):
                        last = copy(w1_h[:, k, :], w1_st[:, k, :], scale=nws[:, k:k + 1])
                    last.then_inc(s_w1h, 1)

                def w2_hi(E):
                    act.wait_ge(s_w2d, 16 * (E + 1))
                    wait(act, s_y, TG * NC * E)
                    copy(w2_h[:, :, :], w2_st[:, :, :], scale=WS).then_inc(s_w2h, 1)

                def y_out(E, c):
                    n = NC * E + c
                    if c == 0:
                        act.wait_ge(s_now, E + 1)
                    wait(act, s_sc[c % 2], 16 * TG * ((NC // 2) * E + c // 2))
                    for t in range(TG):
                        k = TG * c + t
                        act.wait_ge(s_y, TG * n + t + 1)
                        copy(ys[:, c % 2, t, :], bank(4 + t % 2)[:, 0:D], scale=w_now[:, k:k + 1]).then_inc(s_ys, 1)

                def expert(e, final=False):
                    E = e + layer * NE
                    xt_hi(E, 1)
                    gelu(e, E, 0)
                    w2_hi(E)
                    xt_hi(E, 2)
                    gelu(e, E, 1)
                    y_out(E, 0)
                    xt_hi(E, 3)
                    gelu(e, E, 2)
                    y_out(E, 1)
                    gelu(e, E, 3)
                    if not final:
                        w1_hi(E + 1)
                    y_out(E, 2)
                    if not final:
                        xt_hi(E + 1, 0)
                    y_out(E, 3)

                w1_hi(layer * NE)
                xt_hi(layer * NE, 0)
                repeat(act, steps, expert, NE, lambda e: expert(e, True))

            route(0)
            ffn(0)
            stage_end(act, 2)

            def att_turn(b, u, front=True, back=True, rear=True):
                v = 1 - u
                if back:
                    for q in range(TG):
                        act.wait_ge(s_max, TG * (b - 1) + q + 1)
                        if q == 0:
                            wait(act, s_o, TG * (b - 1))
                            wait(act, s_x2, TG * (b - 1))
                        act.activation(pr[:, q, 0:P * (q + 1)], bank(q)[:, 0:P * (q + 1)], ACT.Exp,
                                       bias=nbias[:, q:q + 1], scale=SCORE, accum_out=rsum[:, q:q + 1]).then_inc(s_prob, 1)
                if rear:
                    act.wait_ge(s_z2t, b - 1)
                    wait(act, s_lg, NG + b - 2)
                    copy(z2t_h[:, :, :], ps[2][:, :, :]).then_inc(s_z2h, 1)
                if back:
                    pth(b, 0)
                    pth(b, 1)
                if front:
                    act.wait_ge(s_tp, NG + b + 1)
                    wait(act, s_v, b - 1)
                    copy(zt_h[:, u], ps[2][:, :, :]).then_inc(s_th, 1)
                if back:
                    pth(b, 2)
                if front:
                    act.wait_ge(s_u, b + 1)
                    copy(u_h[:, :, :], ps[2][:, :, :]).then_inc(s_uh, 1)
                if back:
                    pth(b, 3)
                if front:
                    act.wait_ge(s_v, b + 1)
                    copy(v_h[:, :, :].rearrange("p t d -> p (t d)"), ps[2][:, :, :].rearrange("p a b -> p (a b)")).then_inc(s_vh, 1)

            def pth(b, q):
                act.wait_ge(s_ptp, TG * (b - 1) + q + 1)
                wait(act, s_o, TG * (b - 1) + q - 1)
                copy(pt_h[:, q % 2, 0:P * (q + 1)], bank(6 + q % 2)[:, 0:P * (q + 1)]).then_inc(s_pth, 1)

            att_turn(0, 0, back=False, rear=False)
            att_turn(1, 1, rear=False)
            with act.Fori(1, NG // 2) as i:
                for u in range(2):
                    att_turn(2 * i + u, u)
            att_turn(NG, 0, front=False)
            att_turn(NG + 1, 1, front=False, back=False)
            stage_end(act, 3)
            route(1)
            ffn(1)
            stage_end(act, 4)

        @block.vector
        def _(dve):
            steps = Steps(dve, s_dve)
            link = steps.link
            one = lambda ap: ap.unsqueeze(2)

            def bc_j(ap):
                return ap.unsqueeze(2).broadcast_to([P, NE, P])

            dve.wait_ge(s_split, 1)
            link(dve.tensor_scalar(apart[:, :], apart[:, :], NE - 1, None, ALU.bitwise_and))
            link(dve.tensor_scalar(same_expert[:, :], apart[:, :], 0.0, None, ALU.is_equal))
            for k in range(KD):
                link(dve.tensor_tensor(rw_l[:, k, :], rws[:, k, :], rw_h[:, k, :], ALU.subtract))
            for lo, hi, b0 in ((g_l, g_h, 0), (m_l, m_h, 2)):
                for k in range(KD):
                    link(dve.scalar_tensor_tensor(lo[:, k, :], bank(b0 + k)[:, 0:D], WS, hi[:, k, :], ALU.mult, ALU.subtract))

            def stats(src, turn):
                for t in range(TG):
                    steps.done(dve.bn_stats(bst[:, t, :], src[:, t, :]))
                steps.sync()
                dve.sem_inc(s_passed[1], 1)
                for t in range(TG):
                    last = dve.bn_aggr(mv[:, turn, t, :], bst[:, t, :])
                return last

            def normalise(dst, src, turn):
                for t in range(TG):
                    last = dve.tensor_scalar(dst[:, t, :], src[:, t, :], mv[:, turn, t, 0:1], zs[:, turn, t:t + 1],
                                             ALU.subtract, ALU.mult)
                return last

            def lge(g):
                t0 = g * TG
                dve.scalar_tensor_tensor(logits[:, bass.ds(t0, TG), :], lgb(g)[:, 0:TG * NE].rearrange("p (t e) -> p t e", t=TG), 1.0 / WS,
                                         rb[:, :].unsqueeze(1).broadcast_to([P, TG, NE]), ALU.mult, ALU.add).then_inc(s_lge, 1)

            lgb = lambda g: bank(7)

            def front(g, u):
                dve.wait_ge(s_in[u], 16 * ((g - u) // 2 + 1) if isinstance(g, int) else (g - u) * 8 + 16)
                stats(xin[:, u], 0).then_inc(s_mv, 1)
                dve.wait_ge(s_scale, g + 1)
                if not (isinstance(g, int) and g < 2):
                    dve.wait_ge(s_zst[u], (g - u) * 8)
                wait(dve, s_tp, g - 1)
                normalise(zz[:, u], xin[:, u], 0).then_inc(s_z, 1)

            def tl(g, u):
                dve.wait_ge(s_th, g + 1)
                dve.tensor_tensor(zt_l[:, u], ps[u][:, :, :], zt_h[:, u], ALU.subtract).then_inc(s_tl, 1)

            def scan_logits(g, u):
                dve.wait_ge(s_lg, g + 1)
                lge(g)

            def scan_pair(i):
                for u in range(2):
                    g = 2 * i + u
                    front(g, u)
                    if not (isinstance(g, int) and g < 1):
                        tl(g - 1, 1 - u)
                    if not (isinstance(g, int) and g < 2):
                        scan_logits(g - 2, u)
            repeat(dve, steps, scan_pair, NG // 2)
            tl(NG - 1, 1)
            scan_logits(NG - 2, 0)
            scan_logits(NG - 1, 1)
            stage_end(dve, 1)

            def route(layer):
                by_tile = logits[:, :, :]
                mx, inv = rowv[:, 0, :], rowv[:, 1, :]
                over_e = lambda ap: ap.unsqueeze(2).broadcast_to([P, NT, NE])
                dve.wait_ge(s_lge, NG * (layer + 1))
                link(dve.tensor_reduce(mx, by_tile, AX.X, ALU.max))
                dve.tensor_tensor(by_tile, by_tile, over_e(mx), ALU.subtract).then_inc(s_route, 1)
                dve.wait_ge(s_exp, layer + 1)
                link(dve.tensor_reduce(mx, by_tile, AX.X, ALU.add))
                link(dve.reciprocal(inv, mx))
                dve.tensor_tensor(by_tile, by_tile, over_e(inv), ALU.mult).then_inc(s_route, 1)
                dve.wait_ge(s_pt, layer + 1)
                link(dve.tensor_copy(p_s[:, :, :].rearrange("p a b -> p (a b)"), ps[1][:, :, :].rearrange("p a b -> p (a b)")))
                dve.wait_ge(s_prr, layer + 1)
                dve.memset(thr[:, :], 0)
                dve.memset(bit_i[:, :], 1 << (BITS - 1))
                link(dve.memset(bit_f[:, :], float(1 << (BITS - 1))))

                def search(i):
                    link(dve.tensor_tensor(cand[:, :], thr[:, :], bit_i[:, :], ALU.bitwise_or))
                    dve.tensor_scalar(above[:, :, :].rearrange("p a b -> p (a b)"), p_s[:, :, :].rearrange("p a b -> p (a b)"), cand[:, :].bitcast(F32), 0.0,
                                      ALU.is_ge, ALU.add, accum_out=count[:, :]).then_inc(s_cnt, 1)
                    dve.wait_ge(s_tot, i + (BITS * layer + 1))
                    link(dve.tensor_scalar(sel[:, :], bank(4)[:, 0:1], float(CAP), bit_f[:, :], ALU.is_ge, ALU.mult))
                    steps.done(dve.tensor_tensor(thr[:, :], thr[:, :], sel[:, :], ALU.bitwise_or))
                    link(dve.tensor_scalar(bit_f[:, :], bit_f[:, :], 0.5, None, ALU.mult))
                    link(dve.tensor_copy(bit_i[:, :], bit_f[:, :]))
                repeat(dve, steps, search, BITS)
                dve.tensor_scalar(thr_m[:, :], ones[:, :], thr[:, :].bitcast(F32), None, ALU.mult).then_inc(s_route, 1)
                thr_b, n_above, n_equal, need, eq_before, prev, lim, n_mask, base, _ = (ten[:, k, :] for k in range(10))
                wait_tr(layer, 0)
                link(dve.tensor_copy(thr_b, bank(5)[:, 0:NE]))
                link(dve.tensor_tensor(above[:, :, :], p_r[:, :, :], bc_j(thr_b), ALU.is_gt))
                link(dve.tensor_tensor(equal[:, :, :], p_r[:, :, :], bc_j(thr_b), ALU.is_equal))
                link(dve.tensor_reduce(n_above, above[:, :, :], AX.X, ALU.add))
                dve.tensor_reduce(n_equal, equal[:, :, :], AX.X, ALU.add).then_inc(s_aux, 1)
                flat = lambda a: a[:, :, :].rearrange("p e j -> p (e j)")
                link(dve.tensor_tensor_scan(flat(scan), flat(equal), flat(equal), 0.0, ALU.add, ALU.bypass))
                link(dve.memset(prev[:, 0:1], 0.0))
                link(dve.tensor_copy(prev[:, 1:NE], scan[:, 0:NE - 1, P - 1]))
                wait_tr(layer, 1)
                link(dve.tensor_scalar(need, bank(5)[:, P:P + NE], -1.0, float(CAP), ALU.mult, ALU.add))
                link(dve.tensor_tensor(lim, need, bank(5)[:, P + NE:P + 2 * NE], ALU.subtract))
                link(dve.tensor_tensor(lim, lim, prev, ALU.add))
                link(dve.tensor_tensor(scan2[:, :, :], scan[:, :, :], bc_j(lim), ALU.is_le))
                link(dve.tensor_tensor(scan2[:, :, :], scan2[:, :, :], equal[:, :, :], ALU.mult))
                link(dve.tensor_tensor(mask[:, :, :], scan2[:, :, :], above[:, :, :], ALU.add))
                dve.tensor_reduce(n_mask, mask[:, :, :], AX.X, ALU.add).then_inc(s_aux, 1)
                link(dve.tensor_tensor_scan(flat(scan), flat(mask), flat(mask), 0.0, ALU.add, ALU.bypass))
                link(dve.tensor_copy(prev[:, 1:NE], scan[:, 0:NE - 1, P - 1]))
                wait_tr(layer, 2)
                link(dve.tensor_tensor(base, bank(5)[:, P + 2 * NE:P + 3 * NE], prev, ALU.subtract))
                link(dve.tensor_tensor(scan2[:, :, :], scan[:, :, :], bc_j(base), ALU.add))
                link(dve.tensor_tensor(scan2[:, :, :], scan2[:, :, :], mask[:, :, :], ALU.mult))
                link(dve.tensor_scalar(ranks[:, :, :], scan2[:, :, :], -1.0, None, ALU.add))
                link(dve.tensor_scalar(bits[:, :, :], ranks[:, :, :], P - 1, None, ALU.bitwise_and))
                link(dve.tensor_copy(rank_r[:, :, :], bits[:, :, :]))
                link(dve.tensor_scalar(bits[:, :, :], ranks[:, :, :], 7, None, ALU.arith_shift_right))
                link(dve.tensor_copy(rank_c[:, :, :], bits[:, :, :]))
                link(dve.tensor_tensor(scan[:, :, :], mask[:, :, :], p_r[:, :, :], ALU.mult))
                link(dve.tensor_reduce(rowv[:, 0, :], scan[:, :, :].rearrange("p e j -> p j e"), AX.X, ALU.add))
                link(dve.tensor_scalar(rowv[:, 0, :], rowv[:, 0, :], 1e-9, None, ALU.max))
                link(dve.reciprocal(rowv[:, 1, :], rowv[:, 0, :]))
                link(dve.tensor_scalar(rowv[:, 1, :], rowv[:, 1, :], 0.5 / YS, None, ALU.mult))
                link(dve.tensor_tensor(weight[:, :, :], scan[:, :, :], rowv[:, 1:2, :].broadcast_to([P, NE, P]), ALU.mult))
                link(dve.tensor_copy(wp[:, 0], weight[:, :, :]))
                link(dve.tensor_tensor(scan[:, :, :], weight[:, :, :], wp[:, 0], ALU.subtract))
                link(dve.tensor_copy(wp[:, 1], scan[:, :, :]))
                link(dve.tensor_tensor(wp[:, 2], scan[:, :, :], wp[:, 1], ALU.subtract))

            def wait_tr(layer, k):
                dve.wait_ge(s_trp, 3 * layer + k + 1)

            def hot_values(e, E):
                wait(dve, s_oh, NC * E)
                every_c = lambda ap: ap.unsqueeze(1).broadcast_to([P, SLOTS, P])
                link(dve.tensor_tensor(hot_b[:, 0], iota_c[:, :, :], every_c(rank_c[:, e, :]), ALU.is_equal))
                dve.tensor_tensor(hot_b[:, 1], hot_b[:, 0], every_c(iota_b[:, :]), ALU.mult)
                for v in range(3):
                    dve.tensor_tensor(hot_b[:, 2 + v], hot_b[:, 0], every_c(wp[:, v, e, :]), ALU.mult)
                link(dve.tensor_scalar(hot_b[:, 0], hot_b[:, 0], part_f[:, :], None, ALU.mult))

            def hot_ranks(e, E, q):
                wait(dve, s_oh, NC * E + q - 1)
                for j in range(QT):
                    last = dve.tensor_scalar(hot_a[:, q % 2, j, :], iota_b[:, :], rank_r[:, e, QT * q + j:QT * q + j + 1], None, ALU.is_equal)
                last.then_inc(s_hot, 1)

            def lists(E):
                dve.wait_ge(s_oh, NC * (E + 1))
                for u in range(2):
                    wait(dve, s_xe[u], 16 * TG * (NC // 2) * E)
                link(dve.tensor_copy(found[:, :, :].rearrange("p v c -> p (v c)"), bank(6)[:, 0:NV * SLOTS]))
                link(dve.tensor_tensor(w_next[:, :], found[:, 2, :], found[:, 3, :], ALU.add))
                link(dve.tensor_tensor(w_next[:, :], w_next[:, :], found[:, 4, :], ALU.add))
                dve.scalar_tensor_tensor(tok_next[:, :], found[:, 0, :], float(P), found[:, 1, :], ALU.mult, ALU.add).then_inc(s_idx, 1)

            def ffn(layer):
                def xt_lo(E, c):
                    n = NC * E + c
                    dve.wait_ge(s_xth, n + 1)
                    dve.tensor_tensor(xt_l[:, c % 2], ps[0][:, :, :], xt_h[:, c % 2], ALU.subtract).then_inc(s_xtl, 1)

                def hidden_lo(E, c):
                    n = NC * E + c
                    for f in range(KF):
                        dve.wait_ge(s_hh, KF * n + f + 1)
                        dve.scalar_tensor_tensor(hid_l[:, c % 2, f, :], hf[:, f % 2, :], HS, hid_h[:, c % 2, f, :],
                                                 ALU.mult, ALU.subtract).then_inc(s_hl, 1)

                def w1_lo(E):
                    dve.wait_ge(s_w1h, E + 1)
                    for k in range(KD):
                        last = dve.scalar_tensor_tensor(w1_l[:, k, :], w1_st[:, k, :], nws[:, k:k + 1], w1_h[:, k, :],
                                                        ALU.mult, ALU.subtract)
                    last.then_inc(s_w1, 1)

                def w2_lo(E):
                    dve.wait_ge(s_w2h, E + 1)
                    dve.wait_ge(s_b2d, 16 * (E + 1))
                    link(dve.tensor_scalar(b2_h[:, :], b2_st[:, :], YS, None, ALU.mult))
                    link(dve.scalar_tensor_tensor(b2_l[:, :], b2_st[:, :], YS, b2_h[:, :], ALU.mult, ALU.subtract))
                    link(dve.tensor_scalar(b2_h[:, :], b2_h[:, :], pick0[:, :], None, ALU.mult))
                    dve.scalar_tensor_tensor(b2_r[:, :], b2_l[:, :], pick1[:, :], b2_h[:, :], ALU.mult, ALU.add)
                    dve.scalar_tensor_tensor(w2_l[:, :, :].rearrange("p a b -> p (a b)"), w2_st[:, :, :].rearrange("p a b -> p (a b)"), WS, w2_h[:, :, :].rearrange("p a b -> p (a b)"),
                                             ALU.mult, ALU.subtract).then_inc(s_w2, 1)

                def to_now(E):
                    wait(dve, s_ys, TG * NC * E)
                    for u in range(2):
                        wait(dve, s_sc[u], 16 * TG * (NC // 2) * E)
                    dve.tensor_copy(w_now[:, :], w_next[:, :])
                    dve.tensor_copy(tok_now[:, :], tok_next[:, :]).then_inc(s_now, 1)

                def expert(e, final=False):
                    E = e + layer * NE
                    xt_lo(E, 1)
                    hidden_lo(E, 0)
                    w2_lo(E)
                    xt_lo(E, 2)
                    hidden_lo(E, 1)
                    to_now(E)
                    if not final:
                        hot_values(e + 1, E + 1)
                        hot_ranks(e + 1, E + 1, 0)
                    xt_lo(E, 3)
                    if not final:
                        hot_ranks(e + 1, E + 1, 1)
                    hidden_lo(E, 2)
                    if not final:
                        hot_ranks(e + 1, E + 1, 2)
                        hot_ranks(e + 1, E + 1, 3)
                    hidden_lo(E, 3)
                    if not final:
                        lists(E + 1)
                        w1_lo(E + 1)
                        xt_lo(E + 1, 0)

                E0 = layer * NE
                hot_values(0, E0)
                for q in range(NC):
                    hot_ranks(0, E0, q)
                lists(E0)
                w1_lo(E0)
                xt_lo(E0, 0)
                repeat(dve, steps, expert, NE, lambda e: expert(e, True))

            route(0)
            ffn(0)
            stage_end(dve, 2)

            def att_turn(b, u, front=True, back=True, rear=True):
                v = 1 - u
                a = b - 1
                if back:
                    for q in range(TG):
                        dve.wait_ge(s_s, TG * a + q + 1)
                        if q == 0:
                            wait(dve, s_prob, TG * a)
                        link(dve.tensor_reduce(nmax[:, q:q + 1], bank(q)[:, 0:P * (q + 1)], AX.X, ALU.max, negate=True))
                        dve.tensor_scalar(nbias[:, q:q + 1], nmax[:, q:q + 1], SCORE, None, ALU.mult).then_inc(s_max, 1)
                if rear:
                    dve.wait_ge(s_z2h, b - 1)
                    dve.tensor_tensor(z2t_l[:, :, :], ps[2][:, :, :], z2t_h[:, :, :], ALU.subtract).then_inc(s_z2l, 1)
                if front:
                    dve.wait_ge(s_in[u], 16 * (NG // 2) + (16 * (b // 2 + 1) if isinstance(b, int) else (b - u) * 8 + 16))
                    stats(xin[:, u], 0).then_inc(s_mv, 1)
                    dve.wait_ge(s_scale, NG + b + 1)
                    wait(dve, s_tp, NG + b - 1)
                    normalise(zz[:, u], xin[:, u], 0).then_inc(s_z, 1)
                if back:
                    ptl(a, 0)
                    ptl(a, 1)
                if front:
                    dve.wait_ge(s_th, NG + b + 1)
                    dve.tensor_tensor(zt_l[:, u], ps[2][:, :, :], zt_h[:, u], ALU.subtract).then_inc(s_tl, 1)
                if back:
                    residual(a, 0, v)
                if rear:
                    dve.wait_ge(s_lg, NG + b - 1)
                    lge(b - 2)
                if back:
                    ptl(a, 2)
                    residual(a, 1, v)
                if front:
                    dve.wait_ge(s_uh, b + 1)
                    dve.tensor_tensor(u_l[:, :, :], ps[2][:, :, :], u_h[:, :, :], ALU.subtract).then_inc(s_ul, 1)
                if back:
                    ptl(a, 3)
                    residual(a, 2, v)
                    residual(a, 3, v)
                if front:
                    dve.wait_ge(s_vh, b + 1)
                    dve.tensor_tensor(v_l[:, :, :].rearrange("p t d -> p (t d)"), ps[2][:, :, :].rearrange("p a b -> p (a b)"),
                                      v_h[:, :, :].rearrange("p t d -> p (t d)"), ALU.subtract).then_inc(s_vl, 1)
                if back:
                    dve.wait_ge(s_x2, TG * (a + 1))
                    stats(x2[:, v], 1).then_inc(s_mv2, 1)
                    dve.wait_ge(s_scale2, a + 1)
                    if not (isinstance(a, int) and a < 2):
                        dve.wait_ge(s_zst[v], 16 * (NG // 2) + (a - v) * 8)
                    wait(dve, s_z2t, a - 1)
                    normalise(z2[:, v], x2[:, v], 1).then_inc(s_z2, 1)

            def ptl(a, q):
                dve.wait_ge(s_pth, TG * a + q + 1)
                dve.tensor_tensor(pt_l[:, q % 2, 0:P * (q + 1)], bank(6 + q % 2)[:, 0:P * (q + 1)],
                                  pt_h[:, q % 2, 0:P * (q + 1)], ALU.subtract).then_inc(s_ptl, 1)

            def residual(a, q, v):
                if q == 0:
                    if not (isinstance(a, int) and a < 2):
                        dve.wait_ge(s_x2st[v], (a - v) * 8)
                    dve.wait_ge(s_prob, TG * (a + 1))
                    link(dve.tensor_scalar(rinv[:, :], rsum[:, :], WS, None, ALU.mult))
                    link(dve.reciprocal(rinv[:, :], rinv[:, :]))
                dve.wait_ge(s_o, TG * a + q + 1)
                dve.scalar_tensor_tensor(x2[:, v, q, :], bank(q)[:, 0:D], rinv[:, q:q + 1], xin[:, v, q, :],
                                         ALU.mult, ALU.add).then_inc(s_x2, 1)

            att_turn(0, 0, back=False, rear=False)
            n0 = steps.n
            att_turn(1, 1, rear=False)
            per = steps.n - n0
            with dve.Fori(1, NG // 2) as i:
                for u in range(2):
                    steps.n = i * (2 * per) + (n0 - per + u * per)
                    att_turn(2 * i + u, u)
            steps.n = n0 + per * (NG - 1)
            att_turn(NG, 0, front=False)
            att_turn(NG + 1, 1, front=False, back=False)
            stage_end(dve, 3)
            route(1)
            ffn(1)
            stage_end(dve, 4)

        @block.tensor
        def _(pe):
            def split3(dst, lhs, rhs, first=True, last=True):
                (lh, ll), (rh, rl) = lhs, rhs
                pe.matmul(dst, lh, rh, start=first, stop=False)
                pe.matmul(dst, lh, rl, start=False, stop=False)
                return pe.matmul(dst, ll, rh, start=False, stop=last)

            pe.wait_ge(s_small, 16 * 8)
            pe.wait_ge(s_const, 1)
            for a, c, b0 in ((0, 1, 0), (2, 3, 2)):
                for m in range(KD):
                    for k in range(KD):
                        last = pe.matmul(bank(b0 + m)[:, 0:D], wst[:, a, k, m * P:(m + 1) * P], wst[:, c, k, :],
                                         start=(k == 0), stop=(k == KD - 1))
            last.then_inc(s_gm, 1)

            def transposes(dst, src):
                for k in range(KD):
                    for t in range(TG):
                        last = pe.transpose(dst[:, k, t * P:(t + 1) * P], src[:, t, k * P:(k + 1) * P], ident[:, :])
                return last

            def logit_products(hi, lo):
                for t in range(TG):
                    for k in range(KD):
                        for n, (a, w) in enumerate(((hi, rw_h), (hi, rw_l), (lo, rw_h))):
                            last = pe.matmul(bank(7)[:, t * NE:(t + 1) * NE], a[:, k, t * P:(t + 1) * P], w[:, k, :],
                                             start=(k == 0 and n == 0), stop=(k == KD - 1 and n == 2))
                return last

            pe.wait_ge(s_split, 1)

            def tz(g, u):
                pe.wait_ge(s_z, g + 1)
                wait(pe, s_tl, g - 1)
                transposes(ps[u], zz[:, u]).then_inc(s_tp, 1)

            def lg(g, u):
                pe.wait_ge(s_tl, g + 1)
                wait(pe, s_lge, g)
                logit_products(zt_h[:, u], zt_l[:, u]).then_inc(s_lg, 1)

            def scan_pair(i):
                for u in range(2):
                    g = 2 * i + u
                    tz(g, u)
                    if not (isinstance(g, int) and g < 1):
                        lg(g - 1, 1 - u)
            scan_pair(0)
            with pe.Fori(1, NG // 2) as i:
                scan_pair(i)
            lg(NG - 1, 1)
            stage_end(pe, 1)

            def route(layer):
                pe.wait_ge(s_route, 3 * layer + 2)
                for e in range(NE):
                    pe.transpose(ps[0][:, e // 4, (e % 4) * P:(e % 4 + 1) * P], logits[:, :, e], ident[:, :])
                for b in range(NT // PER):
                    last = pe.transpose(ps[1][:, b // 4, (b % 4) * P:(b % 4 + 1) * P], logits[:, b * PER:(b + 1) * PER, :].rearrange("p t e -> p (t e)"), ident[:, :])
                last.then_inc(s_pt, 1)
                with pe.Fori(0, BITS) as i:
                    pe.wait_ge(s_cnt, i + (BITS * layer + 1))
                    pe.matmul(bank(4)[:, 0:1], same_expert[:, :], count[:, :], start=True, stop=True).then_inc(s_tot, 1)
                pe.wait_ge(s_route, 3 * layer + 3)
                pe.transpose(bank(5)[:, 0:P], thr_m[:, :], ident[:, :]).then_inc(s_trp, 1)
                pe.wait_ge(s_aux, 2 * layer + 1)
                pe.matmul(bank(5)[:, P:P + NE], ones[:, :], ten[:, 1, :], start=True, stop=True)
                pe.matmul(bank(5)[:, P + NE:P + 2 * NE], before[:, :], ten[:, 2, :], start=True, stop=True).then_inc(s_trp, 1)
                pe.wait_ge(s_aux, 2 * layer + 2)
                pe.matmul(bank(5)[:, P + 2 * NE:P + 3 * NE], before[:, :], ten[:, 7, :], start=True, stop=True).then_inc(s_trp, 1)

            def ffn(layer):
                def xt(E, c):
                    n = NC * E + c
                    pe.wait_ge(s_xe[c % 2], 16 * TG * ((NC // 2) * E + c // 2 + 1))
                    wait(pe, s_xtl, n)
                    transposes(ps[0], xe[:, c % 2]).then_inc(s_xt, 1)

                def fc1(E, c):
                    n = NC * E + c
                    pe.wait_ge(s_xtl, n + 1)
                    if c == 0:
                        pe.wait_ge(s_w1, E + 1)
                    for f in range(KF):
                        wait(pe, s_gelu, KF * n + f - 1)
                        for k in range(KD):
                            last = split3(bank(2 + f % 2), (w1_h[:, k, f * P:(f + 1) * P], w1_l[:, k, f * P:(f + 1) * P]),
                                          (xt_h[:, c % 2, k, :], xt_l[:, c % 2, k, :]), k == 0, k == KD - 1)
                        last.then_inc(s_h, 1)

                def fc2(E, c):
                    n = NC * E + c
                    pe.wait_ge(s_hl, KF * (n + 1))
                    if c == 0:
                        pe.wait_ge(s_w2, E + 1)
                    for t in range(TG):
                        wait(pe, s_ys, TG * n + t - 1)
                        dst = bank(4 + t % 2)[:, 0:D]
                        pe.matmul(dst, ones_h[:, :], b2_r[:, :], start=True, stop=False)
                        for f in range(KF):
                            cols = slice(t * P, (t + 1) * P)
                            last = split3(dst, (hid_h[:, c % 2, f, cols], hid_l[:, c % 2, f, cols]), (w2_h[:, f, :], w2_l[:, f, :]),
                                          False, f == KF - 1)
                        last.then_inc(s_y, 1)

                def one_hot(E, q):
                    pe.wait_ge(s_hot, NC * E + q + 1)
                    if q == 0:
                        wait(pe, s_idx, E)
                    for j in range(QT):
                        col = QT * q + j
                        last = pe.matmul(bank(6)[:, 0:NV * SLOTS], hot_a[:, q % 2, j, :],
                                         hot_b[:, :, :, :].rearrange("p v c j -> p (v c) j")[:, :, col],
                                         start=(col == 0), stop=(col == P - 1))
                    last.then_inc(s_oh, 1)

                def expert(e, final=False):
                    E = e + layer * NE
                    xt(E, 1)
                    fc1(E, 0)
                    xt(E, 2)
                    fc1(E, 1)
                    fc2(E, 0)
                    if not final:
                        one_hot(E + 1, 0)
                    xt(E, 3)
                    fc1(E, 2)
                    if not final:
                        one_hot(E + 1, 1)
                    fc2(E, 1)
                    if not final:
                        one_hot(E + 1, 2)
                    fc1(E, 3)
                    if not final:
                        one_hot(E + 1, 3)
                    fc2(E, 2)
                    if not final:
                        xt(E + 1, 0)
                    fc2(E, 3)

                E0 = layer * NE
                for q in range(NC):
                    one_hot(E0, q)
                xt(E0, 0)
                expert(0)
                with pe.Fori(1, NE - 1) as e:
                    expert(e)
                expert(NE - 1, True)

            route(0)
            ffn(0)
            stage_end(pe, 2)

            def scores(a, v, q):
                if q == 0:
                    pe.wait_ge(s_ul, a + 1)
                wait(pe, s_x2, TG * (a - 1) + q + 1)
                dst = bank(q)[:, 0:P * (q + 1)]
                for k in range(KD):
                    cols = slice(q * P, (q + 1) * P)
                    split3(dst, (u_h[:, k, cols], u_l[:, k, cols]),
                           (zt_h[:, v, k, 0:P * (q + 1)], zt_l[:, v, k, 0:P * (q + 1)]), k == 0, False)
                pe.matmul(bank(q)[:, P * q:P * (q + 1)], ident_b[:, :], causal[:, :], start=False, stop=True).then_inc(s_s, 1)

            def pt(a, q):
                pe.wait_ge(s_prob, TG * a + q + 1)
                wait(pe, s_ptl, TG * a + q - 1)
                if q == 1:
                    wait(pe, s_lge, NG + a - 1)
                for k in range(q + 1):
                    last = pe.transpose(bank(6 + q % 2)[:, k * P:(k + 1) * P], pr[:, q, k * P:(k + 1) * P], ident[:, :])
                last.then_inc(s_ptp, 1)

            def values(a, q):
                pe.wait_ge(s_ptl, TG * a + q + 1)
                if q == 0:
                    pe.wait_ge(s_vl, a + 1)
                for k in range(q + 1):
                    cols = slice(k * P, (k + 1) * P)
                    last = split3(bank(q)[:, 0:D], (pt_h[:, q % 2, cols], pt_l[:, q % 2, cols]), (v_h[:, k, :], v_l[:, k, :]),
                                  k == 0, k == q)
                last.then_inc(s_o, 1)

            def att_turn(b, u, front=True, back=True, rear=True):
                v = 1 - u
                a = b - 1
                if back:
                    for q in range(TG):
                        scores(a, v, q)
                if rear:
                    pe.wait_ge(s_z2, b - 1)
                    if back:
                        pe.wait_ge(s_vl, a + 1)
                    transposes(ps[2], z2[:, u]).then_inc(s_z2t, 1)
                if back:
                    pt(a, 0)
                    pt(a, 1)
                if front:
                    pe.wait_ge(s_z, NG + b + 1)
                    if rear:
                        pe.wait_ge(s_z2l, b - 1)
                    elif back:
                        pe.wait_ge(s_vl, b)
                    transposes(ps[2], zz[:, u]).then_inc(s_tp, 1)
                if back:
                    values(a, 0)
                if rear:
                    pe.wait_ge(s_z2l, b - 1)
                    if back:
                        pe.wait_ge(s_ptl, TG * a + 2)
                    logit_products(z2t_h[:, :, :], z2t_l[:, :, :]).then_inc(s_lg, 1)
                if back:
                    pt(a, 2)
                    values(a, 1)
                if front:
                    pe.wait_ge(s_tl, NG + b + 1)
                    for m in range(KD):
                        for k in range(KD):
                            last = split3(ps[2][:, m, :], (g_h[:, k, m * P:(m + 1) * P], g_l[:, k, m * P:(m + 1) * P]),
                                          (zt_h[:, u, k, :], zt_l[:, u, k, :]), k == 0, k == KD - 1)
                    last.then_inc(s_u, 1)
                if back:
                    if rear:
                        pe.wait_ge(s_lge, NG + b - 1)
                    pt(a, 3)
                    values(a, 2)
                    values(a, 3)
                if front:
                    pe.wait_ge(s_ul, b + 1)
                    for t in range(TG):
                        for k in range(KD):
                            cols = slice(t * P, (t + 1) * P)
                            last = split3(ps[2][:, t // 2, (t % 2) * D:(t % 2 + 1) * D], (zt_h[:, u, k, cols], zt_l[:, u, k, cols]),
                                          (m_h[:, k, :], m_l[:, k, :]), k == 0, k == KD - 1)
                    last.then_inc(s_v, 1)

            att_turn(0, 0, back=False, rear=False)
            att_turn(1, 1, rear=False)
            with pe.Fori(1, NG // 2) as i:
                for u in range(2):
                    att_turn(2 * i + u, u)
            att_turn(NG, 0, front=False)
            att_turn(NG + 1, 1, front=False, back=False)
            stage_end(pe, 3)
            route(1)
            ffn(1)
            stage_end(pe, 4)


def kernel(L0_attn_x, L0_attn_W_q, L0_attn_W_k, L0_attn_W_v, L0_attn_W_o, L0_ffn_norm_weight, L0_ffn_router_w,
           L0_ffn_router_b, L0_ffn_fc1_w, L0_ffn_fc1_b, L0_ffn_fc2_w, L0_ffn_fc2_b):
    import numpy as np
    import concourse.bacc as bacc
    from concourse.bass_utils import run_bass_kernel_spmd

    def lay(a):
        return np.ascontiguousarray(a)

    experts, ff, _ = L0_ffn_fc1_w.shape
    arrays = {
        "x": lay(L0_attn_x),
        "wq": lay(L0_attn_W_q),
        "wk": lay(L0_attn_W_k),
        "wv": lay(L0_attn_W_v),
        "wo_t": lay(np.asarray(L0_attn_W_o).T),
        "norm_w": lay(np.asarray(L0_ffn_norm_weight).reshape(-1, 128).T),
        "router_t": lay(np.asarray(L0_ffn_router_w).T),
        "router_b": lay(L0_ffn_router_b),
        "fc1_t": lay(np.asarray(L0_ffn_fc1_w).transpose(0, 2, 1)),
        "fc1_b": lay(np.asarray(L0_ffn_fc1_b).reshape(experts, ff // 128, 128).transpose(2, 0, 1)),
        "fc2_t": lay(np.asarray(L0_ffn_fc2_w).transpose(0, 2, 1)),
        "fc2_b": lay(L0_ffn_fc2_b),
    }
    nc = bacc.Bacc("TRN2", target_bir_lowering=False, num_devices=1)
    args = {n: nc.dram_tensor(n, a.shape, mybir.dt.from_np(a.dtype), kind="ExternalInput").ap() for n, a in arrays.items()}
    out = nc.dram_tensor("out", arrays["x"].shape, F32, kind="ExternalOutput").ap()
    macaron(nc, out=out, **args)
    r = run_bass_kernel_spmd(nc, [arrays], core_ids=[0])
    return r.results[0]["out"]
```

```python
from contextlib import ExitStack

import concourse.bass as bass
from concourse import mybir
from concourse.alu_op_type import AluOpType as ALU

F32 = mybir.dt.float32
F16 = mybir.dt.float16
BF16 = mybir.dt.bfloat16
I32 = mybir.dt.int32
U32 = mybir.dt.uint32
U8 = mybir.dt.uint8
ACT = mybir.ActivationFunctionType
AX = mybir.AxisListType


class Steps:

    def __init__(self, engine, sem):
        self.engine, self.sem, self.n = engine, sem, 0

    def done(self, instruction):
        instruction.then_inc(self.sem, 1)
        self.n = self.n + 1

    def sync(self):
        self.engine.wait_ge(self.sem, self.n)

    def link(self, instruction):
        self.done(instruction)
        self.sync()


def repeat(engine, steps, body, count, last=None):
    before = steps.n
    body(0)
    per = steps.n - before
    end = count - 1 if last else count
    with engine.Fori(1, end) as i:
        steps.n = i * per + before
        body(i)
    steps.n = before + end * per
    if last:
        last(end)


def wait(engine, sem, value):
    if not isinstance(value, int) or value > 0:
        engine.wait_ge(sem, value)


def macaron(nc, x, wq, wk, wv, wo_t, norm_w, router_t, router_b, fc1_t, fc1_b, fc2_t, fc2_b, out):
    P = 128
    B, S, D = x.shape
    T = B * S
    NE, _, FF = fc1_t.shape
    CAP = T // NE
    NT = T // P
    KD = D // P
    KF = FF // P
    TG = S // P
    NG = T // S
    NC = CAP // S
    SLOTS = CAP // P
    FC1 = (2, 3, 7)
    EPS = 1e-5
    WS = 64.0
    HS = 16.0
    YS = WS * HS
    SCORE = 1.0 / (D ** 0.5 * WS)
    BITS = 30
    ROUNDS = ((BITS - 16) // 2, 4, 4)
    SEARCH = sum(ROUNDS)
    MARK = 1024.0
    HF = 4
    PER = P // NE
    NV = 5
    QT = P // NC
    RING = 4
    WIDE = 8
    LEAD = 5
    assert KD == 2 and TG == 4 and NC == 4 and PER * NE == P and NT == P

    xf = x.rearrange("b s d -> (b s) d")
    outf = out.rearrange("b s d -> (b s) d")
    x1_d = nc.dram_tensor("x1_d", [T, D], F32).ap()
    z_d = nc.dram_tensor("z_d", [T, D], F32).ap()

    def group(d, g):
        return d.rearrange("(g j p) d -> g p j d", p=P, j=TG)[g]

    ctx = ExitStack()
    with ctx:
        def sb(name, shape, dt, stack=ctx):
            return stack.enter_context(nc.sbuf_tensor(name, shape, dt))

        def sem(name):
            return ctx.enter_context(nc.semaphore(name))

        ident = sb("ident", [P, P], F32)
        ident_b = sb("ident_b", [P, P], BF16)
        causal = sb("causal", [P, P], BF16)
        ones = sb("ones", [P, P], F32)
        ones_h = sb("ones_h", [P, P], F16)
        before = sb("before", [P, P], F32)
        apart = sb("apart", [P, P], I32)
        same_expert = sb("same_expert", [P, P], F32)
        iota_i = sb("iota_i", [P, P], I32)
        iota_b = sb("iota_b", [P, P], BF16)
        iota_c = sb("iota_c", [P, SLOTS, P], BF16)
        one_two_three = sb("one_two_three", [P, 3], F32)
        part_i = sb("part_i", [P, 1], I32)
        part_f = sb("part_f", [P, 1], F32)
        minus_half = sb("minus_half", [P, 2, TG], F32)
        eps = sb("eps", [P, 2, TG], F32)
        minus_one = sb("minus_one", [P, 2, TG], F32)
        pick0 = sb("pick0", [P, 1], F32)
        pick1 = sb("pick1", [P, 1], F32)
        nw = sb("nw", [P, KD], F32)
        nws = sb("nws", [P, KD], F32)
        rb = sb("rb", [P, NE], F32)
        b1 = sb("b1", [P, NE, KF], F32)
        b1_now = sb("b1_now", [P, KF], F32)
        rw = sb("rw", [P, KD, NE], F32)
        rws = sb("rws", [P, KD, NE], F32)
        rw_h = sb("rw_h", [P, KD, NE], F16)
        rw_l = sb("rw_l", [P, KD, NE], F16)
        g_h = sb("g_h", [P, KD, D], F16)
        g_l = sb("g_l", [P, KD, D], F16)
        m_h = sb("m_h", [P, KD, D], F16)
        m_l = sb("m_l", [P, KD, D], F16)
        logits = sb("logits", [P, NT, NE], F32)
        mv = sb("mv", [P, RING, TG, 2], F32)
        bst = sb("bst", [P, RING, TG, 6], F32)
        nt = sb("nt", [P, 7, RING, TG], F32)
        zs = sb("zs", [P, RING, TG], F32)
        zb = sb("zb", [P, RING, TG], F32)

        ffn = ExitStack()
        w1_st = sb("w1_st", [P, KD, FF], F32, ffn)
        w2_st = sb("w2_st", [P, KF, D], F32, ffn)
        b2_st = sb("b2_st", [P, D], F32, ffn)
        w1_h = sb("w1_h", [P, KD, FF], F16, ffn)
        w1_l = sb("w1_l", [P, KD, FF], F16, ffn)
        w2_h = sb("w2_h", [P, KF, D], F16, ffn)
        w2_l = sb("w2_l", [P, KF, D], F16, ffn)
        b2_h = sb("b2_h", [P, D], F16, ffn)
        b2_l = sb("b2_l", [P, D], F16, ffn)
        b2_r = sb("b2_r", [P, D], F16, ffn)
        rank_r = sb("rank_r", [P, NE, P], F32, ffn)
        rank_c = sb("rank_c", [P, NE, P], BF16, ffn)
        wp = sb("wp", [P, 3, NE, P], BF16, ffn)
        hot_a = sb("hot_a", [P, 2, QT, P], BF16, ffn)
        hot_b = sb("hot_b", [P, NV, SLOTS, P], BF16, ffn)
        found = sb("found", [P, NV, SLOTS], F32, ffn)
        w_next = sb("w_next", [P, SLOTS], F32, ffn)
        w_now = sb("w_now", [P, SLOTS], F32, ffn)
        tok_next = sb("tok_next", [P, SLOTS], I32, ffn)
        tok_now = sb("tok_now", [P, SLOTS], I32, ffn)
        shared = ExitStack()
        xe = sb("xe", [P, 2, TG, D], F32, shared)
        xt_h = sb("xt_h", [P, 2, KD, S], F16, shared)
        xt_l = sb("xt_l", [P, 2, KD, S], F16, shared)
        hf = sb("hf", [P, HF, S], F32, shared)
        hid_h = sb("hid_h", [P, 2, KF, S], F16, shared)
        hid_l = sb("hid_l", [P, 2, KF, S], F16, shared)
        ys = sb("ys", [P, 2, TG, D], F32, shared)
        shared.close()
        rout = ExitStack()
        p_s = sb("p_s", [P, NE, P], F32, rout)
        p_r = sb("p_r", [P, NE, P], F32, rout)
        above = sb("above", [P, NE, P], F32, rout)
        equal = sb("equal", [P, NE, P], F32, rout)
        scan = sb("scan", [P, NE, P], F32, rout)
        scan2 = sb("scan2", [P, NE, P], F32, rout)
        mask = sb("mask", [P, NE, P], F32, rout)
        ranks = sb("ranks", [P, NE, P], I32, rout)
        bits = sb("bits", [P, NE, P], I32, rout)
        weight = sb("weight", [P, NE, P], F32, rout)
        rowv = sb("rowv", [P, 2, P], F32, rout)
        ten = sb("ten", [P, 10, NE], F32, rout)
        thr = sb("thr", [P, 1], I32, rout)
        cand = sb("cand", [P, 3], I32, rout)
        cand_f = sb("cand_f", [P, 3], F32, rout)
        sel = sb("sel", [P, 3], F32, rout)
        count = sb("count", [P, 3], F32, rout)
        steps3 = sb("steps3", [P, 3], F32, rout)
        next3 = sb("next3", [P, 3], F32, rout)
        unit = sb("unit", [P, 3], F32, rout)
        passed = sb("passed", [P, 1], F32, rout)
        found_f = sb("found_f", [P, 1], F32, rout)
        low = sb("low", [P, 1], F32, rout)
        low_i = sb("low_i", [P, 1], I32, rout)
        top = sb("top", [P, NE * P], BF16, rout)
        junk = sb("junk", [P, 3, NE * P], BF16, rout)
        keys = [sb("key_1", [P, NE * P], F16, rout), sb("key_2", [P, NE * P], F16, rout)]
        byte = sb("byte", [P, 2, NE * P], F16, rout)
        thr_m = sb("thr_m", [P, P], F32, rout)
        rout.close()
        ffn.close()

        att = ExitStack()
        wst = sb("wst", [P, 4, KD, D], F32, att)
        xin = sb("xin", [P, WIDE, TG, D], F32, att)
        zz = sb("zz", [P, 2, TG, D], F32, att)
        zt_h = sb("zt_h", [P, 2, KD, S], F16, att)
        zt_l = sb("zt_l", [P, 2, KD, S], F16, att)
        u_h = sb("u_h", [P, KD, S], F16, att)
        u_l = sb("u_l", [P, KD, S], F16, att)
        v_h = sb("v_h", [P, TG, D], F16, att)
        v_l = sb("v_l", [P, TG, D], F16, att)
        pr = sb("pr", [P, TG, S], F32, att)
        pt_h = sb("pt_h", [P, 2, S], F16, att)
        pt_l = sb("pt_l", [P, 2, S], F16, att)
        x2 = sb("x2", [P, 2, TG, D], F32, att)
        z2 = sb("z2", [P, 2, TG, D], F32, att)
        z2t_h = sb("z2t_h", [P, KD, S], F16, att)
        z2t_l = sb("z2t_l", [P, KD, S], F16, att)
        nmax = sb("nmax", [P, TG], F32, att)
        nbias = sb("nbias", [P, TG], F32, att)
        rsum = sb("rsum", [P, 2, TG], F32, att)
        rinv = sb("rinv", [P, TG], F32, att)
        att.close()

        ps = [ctx.enter_context(nc.psum_tensor(f"ps{i}", [P, 2, 512], F32)) for i in range(4)]

        def bank(i):
            return ps[i // 2][:, i % 2, :]

        s_phase = sem("s_phase")
        s_pool, s_dve, s_act = sem("s_pool"), sem("s_dve"), sem("s_act")
        s_const, s_small, s_split = sem("s_const"), sem("s_small"), sem("s_split")
        s_gm = sem("s_gm")
        s_in = [sem(f"s_in{i}") for i in range(WIDE)]
        s_mv, s_scale, s_z = sem("s_mv"), sem("s_scale"), sem("s_z")
        s_zst = [sem("s_zst0"), sem("s_zst1")]
        s_x2st = [sem("s_x2st0"), sem("s_x2st1")]
        s_tp, s_th, s_tl = sem("s_tp"), sem("s_th"), sem("s_tl")
        s_lg, s_lge = sem("s_lg"), sem("s_lge")
        s_copy = sem("s_copy")
        s_passed = [sem("s_passed0"), sem("s_passed1")]
        s_byte_in = sem("s_byte_in")
        s_bytes = sem("s_bytes")
        s_exp, s_pt, s_route, s_prr, s_cnt, s_tot = (sem(n) for n in ("s_exp", "s_pt", "s_route", "s_prr", "s_cnt", "s_tot"))
        s_w1d, s_w2d, s_b2d = sem("s_w1d"), sem("s_w2d"), sem("s_b2d")
        s_w1h, s_w1, s_w2h, s_w2 = sem("s_w1h"), sem("s_w1"), sem("s_w2h"), sem("s_w2")
        s_xe = [sem("s_xe0"), sem("s_xe1")]
        s_sc = [sem("s_sc0"), sem("s_sc1")]
        s_xt, s_xth, s_xtl = sem("s_xt"), sem("s_xth"), sem("s_xtl")
        s_h, s_gelu, s_hh, s_hl = sem("s_h"), sem("s_gelu"), sem("s_hh"), sem("s_hl")
        s_y, s_ys = sem("s_y"), sem("s_ys")
        s_hot, s_oh, s_idx, s_now = sem("s_hot"), sem("s_oh"), sem("s_idx"), sem("s_now")
        s_s, s_max, s_prob = sem("s_s"), sem("s_max"), sem("s_prob")
        s_ptp, s_pth, s_ptl = sem("s_ptp"), sem("s_pth"), sem("s_ptl")
        s_o, s_x2 = sem("s_o"), sem("s_x2")
        s_u, s_uh, s_ul = sem("s_u"), sem("s_uh"), sem("s_ul")
        s_v, s_vh, s_vl = sem("s_v"), sem("s_vh"), sem("s_vl")
        s_z2t, s_z2h, s_z2l = sem("s_z2t"), sem("s_z2h"), sem("s_z2l")
        s_aux, s_trp = sem("s_aux"), sem("s_trp")
        s_mv2, s_scale2, s_z2 = sem("s_mv2"), sem("s_scale2"), sem("s_z2")

        def on(g):
            return not isinstance(g, int) or 0 <= g < NG

        def turns(engine, turn, steps=None):
            for c in range(RING):
                n0 = steps.n if steps else 0
                turn(c, c)
            per = steps.n - n0 if steps else 0
            with engine.Fori(1, NG // RING) as i:
                for u in range(RING):
                    if steps:
                        steps.n = i * (RING * per) + (n0 + (u - RING + 1) * per)
                    turn(RING * i + u, u)
            if steps:
                steps.n = n0 + per * (NG - RING + 1)
            for c in range(NG, NG + RING):
                turn(c, c % RING)

        def flat(t):
            return t.rearrange("p a b -> p (a b)")

        block = ctx.enter_context(nc.Block())
        ENGINES = 5

        def stage_end(engine, k):
            engine.drain().then_inc(s_phase, 1)
            engine.wait_ge(s_phase, ENGINES * k)

        @block.sync
        def _(sp):
            steps = Steps(sp, s_phase)
            for dst, src in ((nw[:, :], norm_w), (rb[:, :], router_b.rearrange("(a e) -> a e", a=1).broadcast_to([P, NE])),
                             (b1[:, :, :], fc1_b),
                             (rw[:, :, :], router_t.rearrange("(k p) e -> p k e", p=P)),
                             (wst[:, 0], wq.rearrange("(k p) e -> p k e", p=P)),
                             (wst[:, 1], wk.rearrange("(k p) e -> p k e", p=P)),
                             (wst[:, 2], wv.rearrange("(k p) e -> p k e", p=P)),
                             (wst[:, 3], wo_t.rearrange("(k p) e -> p k e", p=P))):
                sp.dma_start(dst, src).then_inc(s_small, 16)

            def scan_turns(i):
                for u in range(WIDE):
                    g = WIDE * i + u
                    wait(sp, s_z, g - WIDE + 1)
                    sp.dma_start(xin[:, u], group(xf, g)).then_inc(s_in[u], 16)
                    if on(g - LEAD):
                        z_out(g - LEAD, (u - LEAD) % 2)

            def z_out(g, v):
                sp.wait_ge(s_z, g + 1)
                sp.dma_start(group(z_d, g), zz[:, v]).then_inc(s_zst[v], 16)

            repeat(sp, steps, scan_turns, NG // WIDE)
            for g in range(NG - LEAD, NG):
                z_out(g, g % 2)
            steps.n = 0
            sp.dma_start(x1_d.rearrange("(a b) d -> a (b d)", b=8), xf.rearrange("(a b) d -> a (b d)", b=8)).then_inc(s_copy, 16)
            for u in range(2):
                sp.wait_ge(s_zst[u], 16 * (NG // 2))
            stage_end(sp, 1)

            def ffn_loads(layer):
                def load(e):
                    E = e + layer * NE
                    wait(sp, s_w1, E)
                    sp.dma_start(w1_st[:, :, :], fc1_t[e].rearrange("(k p) f -> p k f", p=P)).then_inc(s_w1d, 16)
                    wait(sp, s_w2, 4 * E)
                    sp.dma_start(w2_st[:, :, :], fc2_t[e].rearrange("(k p) d -> p k d", p=P)).then_inc(s_w2d, 16)
                    sp.dma_start(b2_st[:, :], fc2_b[e].rearrange("(a d) -> a d", a=1).broadcast_to([P, D])).then_inc(s_b2d, 16)
                repeat(sp, steps, load, NE)
                steps.n = 0

            ffn_loads(0)
            stage_end(sp, 2)

            def att_turn(c, u):
                if on(c):
                    wait(sp, s_x2, TG * (c - RING + 1))
                    sp.dma_start(xin[:, u], group(x1_d, c)).then_inc(s_in[u], 16)
                if on(c - 3):
                    v = (u - 3) % 2
                    sp.wait_ge(s_x2, TG * (c - 2))
                    sp.dma_start(group(outf, c - 3), x2[:, v]).then_inc(s_x2st[v], 16)
                if on(c - 4):
                    sp.wait_ge(s_z2, c - 3)
                    sp.dma_start(group(z_d, c - 4), z2[:, u % 2]).then_inc(s_zst[u % 2], 16)

            turns(sp, att_turn)
            for u in range(2):
                sp.wait_ge(s_x2st[u], 16 * (NG // 2))
                sp.wait_ge(s_zst[u], 16 * NG)
            stage_end(sp, 3)
            ffn_loads(1)
            stage_end(sp, 4)

        @block.gpsimd
        def _(pool):
            steps = Steps(pool, s_pool)
            pool.memset(ident[:, :], 0.0)
            pool.memset(ident_b[:, :], 0.0)
            pool.memset(causal[:, :], 0.0)
            pool.memset(ones[:, :], 1.0)
            pool.memset(ones_h[:, :], 1.0)
            pool.memset(before[:, :], 1.0)
            pool.memset(minus_half[:, :, :], -0.5)
            pool.memset(minus_one[:, :, :], -1.0)
            pool.memset(eps[:, :, :], EPS)
            pool.memset(pick0[:, :], 0.0)
            pool.memset(pick1[:, :], 0.0)
            pool.iota(iota_i[:, :], pattern=[[1, P]], base=0, channel_multiplier=0)
            steps.link(pool.iota(part_i[:, :], pattern=[[0, 1]], base=0, channel_multiplier=1))
            for m in (ident, ident_b):
                pool.affine_select(out=m[:, :], in_=m[:, :], compare_op=ALU.not_equal, fill=1.0, base=0,
                                   pattern=[[-1, P]], channel_multiplier=1)
            pool.affine_select(out=causal[:, :], in_=causal[:, :], compare_op=ALU.is_ge, fill=-1e30, base=0,
                               pattern=[[-1, P]], channel_multiplier=1)
            pool.affine_select(out=before[:, :], in_=before[:, :], compare_op=ALU.is_gt, fill=0.0, base=0,
                               pattern=[[1, P]], channel_multiplier=-1)
            pool.affine_select(out=pick0[:, :], in_=pick0[:, :], compare_op=ALU.not_equal, fill=1.0, base=0,
                               pattern=[[0, 1]], channel_multiplier=1)
            pool.affine_select(out=pick1[:, :], in_=pick1[:, :], compare_op=ALU.not_equal, fill=1.0, base=-1,
                               pattern=[[0, 1]], channel_multiplier=1)
            pool.iota(apart[:, :], pattern=[[1, P]], base=P, channel_multiplier=-1)
            pool.tensor_copy(part_f[:, :], part_i[:, :])
            pool.tensor_copy(iota_b[:, :], iota_i[:, :])
            pool.tensor_copy(one_two_three[:, :], iota_i[:, 1:4])
            pool.iota(iota_c[:, :, :], pattern=[[1, SLOTS], [0, P]], base=0, channel_multiplier=0,
                      allow_small_or_imprecise_dtypes=True).then_inc(s_const, 1)

            def row_factors(at, n):
                m, v = mv[:, at:at + n, :, 0], mv[:, at:at + n, :, 1]
                a, r, q, q2, c, r2, minus_m = (nt[:, k, at:at + n, :] for k in range(7))
                steps.done(pool.tensor_tensor(minus_m, m, minus_one[:, 0:n, :], ALU.mult))
                steps.link(pool.tensor_tensor(a, v, eps[:, 0:n, :], ALU.add))
                steps.link(pool.tensor_tensor(r, a, minus_half[:, 0:n, :], ALU.pow))
                steps.link(pool.tensor_tensor(q, v, r, ALU.mult))
                steps.link(pool.tensor_tensor(q2, q, r, ALU.mult))
                steps.link(pool.tensor_tensor(c, q2, eps[:, 0:n, :], ALU.add))
                steps.link(pool.tensor_tensor(r2, c, minus_half[:, 0:n, :], ALU.pow))
                steps.link(pool.tensor_tensor(zs[:, at:at + n, :], r, r2, ALU.mult))
                return pool.tensor_tensor(zb[:, at:at + n, :], minus_m, zs[:, at:at + n, :], ALU.mult)

            def scan_turns(i):
                for w in range(WIDE // 2):
                    pool.wait_ge(s_mv, (WIDE // 2) * i + (w + 1))
                    wait(pool, s_z, WIDE * i + 2 * (w - 1))
                    row_factors(2 * w % RING, 2).then_inc(s_scale, 1)
            repeat(pool, steps, scan_turns, NG // WIDE)
            stage_end(pool, 1)

            def ffn_rows(layer, rows, acc):
                def gather(E, c):
                    n = NC * E + c
                    wait(pool, s_xt, KD * (n - 1))
                    pool.sem_inc(s_passed[0], 1)
                    for t in range(TG):
                        k = TG * c + t
                        pool.indirect_dma_start(xe[:, c % 2, t, :], None, rows,
                                                bass.IndirectOffsetOnAxis(ap=tok_next[:, k:k + 1].bitcast(U32), axis=0)).then_inc(s_xe[c % 2], 16)

                def scatter(E, c):
                    n = NC * E + c
                    if c == 0:
                        pool.wait_ge(s_now, E + 1)
                    pool.wait_ge(s_ys, TG * (n + 1))
                    pool.sem_inc(s_passed[0], 1)
                    for t in range(TG):
                        k = TG * c + t
                        pool.indirect_dma_start(acc, bass.IndirectOffsetOnAxis(ap=tok_now[:, k:k + 1].bitcast(U32), axis=0),
                                                ys[:, c % 2, t, :], None, compute_op=ALU.add).then_inc(s_sc[c % 2], 16)

                def expert(e, final=False):
                    E = e + layer * NE
                    gather(E, 2)
                    gather(E, 3)
                    scatter(E, 0)
                    scatter(E, 1)
                    if not final:
                        pool.wait_ge(s_idx, E + 2)
                        gather(E + 1, 0)
                        gather(E + 1, 1)
                    scatter(E, 2)
                    scatter(E, 3)

                pool.wait_ge(s_idx, layer * NE + 1)
                pool.wait_ge(s_copy, 16)
                gather(layer * NE, 0)
                gather(layer * NE, 1)
                repeat(pool, steps, expert, NE, lambda e: expert(e, True))
                for u in range(2):
                    pool.wait_ge(s_sc[u], 16 * TG * (NC // 2) * NE * (layer + 1))

            ffn_rows(0, z_d, x1_d)
            stage_end(pool, 2)

            def att_turn(c, u):
                if on(c):
                    pool.wait_ge(s_mv, c + (NG // 2 + 1))
                    pool.wait_ge(s_z, c + NG)
                    row_factors(0, 1).then_inc(s_scale, 1)
                a = c - 2
                if on(a):
                    pool.wait_ge(s_mv2, a + 1)
                    wait(pool, s_z2, a)
                    row_factors(1, 1).then_inc(s_scale2, 1)

            turns(pool, att_turn, steps)
            stage_end(pool, 3)
            ffn_rows(1, z_d, outf)
            stage_end(pool, 4)

        @block.scalar
        def _(act):
            steps = Steps(act, s_act)

            def copy(dst, src, **kw):
                return act.activation(dst, src, ACT.Copy, **kw)

            act.wait_ge(s_small, 16 * 8)
            act.wait_ge(s_const, 1)
            steps.link(copy(nws[:, :], nw[:, :], scale=WS))
            for k in range(KD):
                steps.link(copy(rws[:, k, :], rw[:, k, :], scale=nws[:, k:k + 1]))
                steps.link(copy(rw_h[:, k, :], rws[:, k, :]))
            act.wait_ge(s_gm, 1)
            for dst, b0 in ((g_h, 0), (m_h, 2)):
                for k in range(KD):
                    steps.link(copy(dst[:, k, :], bank(b0 + k)[:, 0:D], scale=WS))
            copy(nbias[:, 0:1], nws[:, 0:1]).then_inc(s_split, 1)

            def th(g, u):
                for k in range(KD):
                    act.wait_ge(s_tp, KD * g + (k + 1))
                    if k == 0:
                        wait(act, s_lg, g - 1)
                    copy(zt_h[:, u, k, :], ps[u][:, k, :]).then_inc(s_th, 1)

            def normalise(dst, src, at):
                for t in range(TG):
                    last = act.activation(dst[:, t, :], src[:, t, :], ACT.Identity, bias=zb[:, at, t:t + 1], scale=zs[:, at, t:t + 1])
                return last

            def scan_turns(i):
                for w in range(WIDE // 2):
                    act.wait_ge(s_scale, (WIDE // 2) * i + (w + 1))
                    for v in range(2):
                        g = WIDE * i + (2 * w + v)
                        wait(act, s_tp, KD * (g - 1))
                        wait(act, s_zst[v], 8 * WIDE * i + 16 * w)
                        normalise(zz[:, v], xin[:, 2 * w + v], (2 * w + v) % RING).then_inc(s_z, 1)
                        if on(g - 1):
                            th(g - 1, (v - 1) % 2)
            repeat(act, steps, scan_turns, NG // WIDE)
            th(NG - 1, (NG - 1) % 2)
            stage_end(act, 1)

            def route(layer):
                act.wait_ge(s_route, 3 * layer + 1)
                act.activation(logits[:, :, :], logits[:, :, :], ACT.Exp).then_inc(s_exp, 1)
                act.wait_ge(s_pt, layer + 1)
                copy(p_r[:, :, :].rearrange("p e j -> p (e j)"), ps[0][:, :, :].rearrange("p a b -> p (a b)")).then_inc(s_prr, 1)
                act.wait_ge(s_byte_in, layer + 1)
                octets = p_s[:, :, :].rearrange("p e j -> p (e j)").bitcast(U8).rearrange("p (n four) -> p n four", four=4)
                for k in range(2):
                    last = copy(byte[:, k, :], octets[:, :, 1 - k])
                last.then_inc(s_bytes, 1)

            def ffn(layer):
                def xt_hi(E, c):
                    n = NC * E + c
                    wait(act, s_h, KF * (n - 1))
                    for k in range(KD):
                        act.wait_ge(s_xt, KD * n + (k + 1))
                        copy(xt_h[:, c % 2, k, :], ps[0][:, k, :]).then_inc(s_xth, 1)

                def bias(e, E):
                    wait(act, s_gelu, KF * NC * E)
                    steps.link(copy(b1_now[:, :], b1[:, e, :]))

                def gelu(E, c, f):
                    n = NC * E + c
                    if f == 0:
                        wait(act, s_y, TG * (n - 1))
                    act.wait_ge(s_h, KF * n + f + 1)
                    wait(act, s_hl, KF * n + f - (HF - 1))
                    act.activation(hf[:, f % HF, :], bank(FC1[f % 3]), ACT.Gelu, bias=b1_now[:, f:f + 1],
                                   scale=1.0 / WS).then_inc(s_gelu, 1)
                    act.wait_ge(s_gelu, KF * n + f + 1)
                    copy(hid_h[:, c % 2, f, :], hf[:, f % HF, :], scale=HS).then_inc(s_hh, 1)

                def w1_hi(E):
                    act.wait_ge(s_w1d, 16 * (E + 1))
                    wait(act, s_h, KF * NC * E)
                    for k in range(KD):
                        last = copy(w1_h[:, k, :], w1_st[:, k, :], scale=nws[:, k:k + 1])
                    last.then_inc(s_w1h, 1)

                def w2_hi(E, h):
                    if h == 0:
                        act.wait_ge(s_w2d, 16 * (E + 1))
                        wait(act, s_y, TG * NC * E)
                    part = slice(h * KF // 4, (h + 1) * KF // 4)
                    copy(w2_h[:, part, :], w2_st[:, part, :], scale=WS).then_inc(s_w2h, 1)

                def y_out(E, c):
                    n = NC * E + c
                    if c == 0:
                        act.wait_ge(s_now, E + 1)
                    wait(act, s_sc[c % 2], 16 * TG * ((NC // 2) * E + c // 2))
                    for t in range(TG):
                        k = TG * c + t
                        act.wait_ge(s_y, TG * n + t + 1)
                        copy(ys[:, c % 2, t, :], bank(4 + t % 2)[:, 0:D], scale=w_now[:, k:k + 1]).then_inc(s_ys, 1)

                def expert(e, final=False):
                    E = e + layer * NE
                    bias(e, E)
                    for f in range(KF):
                        gelu(E, 0, f)
                        if f % 2:
                            w2_hi(E, f // 2)
                    xt_hi(E, 2)
                    for f in range(KF):
                        gelu(E, 1, f)
                    xt_hi(E, 3)
                    y_out(E, 0)
                    for f in range(KF):
                        gelu(E, 2, f)
                    y_out(E, 1)
                    for f in range(KF):
                        gelu(E, 3, f)
                    if not final:
                        w1_hi(E + 1)
                        xt_hi(E + 1, 0)
                    y_out(E, 2)
                    if not final:
                        xt_hi(E + 1, 1)
                    y_out(E, 3)

                w1_hi(layer * NE)
                xt_hi(layer * NE, 0)
                xt_hi(layer * NE, 1)
                repeat(act, steps, expert, NE, lambda e: expert(e, True))

            route(0)
            ffn(0)
            stage_end(act, 2)

            def hi_halves(ready, n, dst, done):
                for k in range(KD):
                    act.wait_ge(ready, KD * n + (k + 1))
                    copy(dst[:, k * S:(k + 1) * S], bank(4 + k)).then_inc(done, 1)

            def pth(a, q):
                act.wait_ge(s_ptp, TG * a + (q + 1))
                wait(act, s_o, TG * a + (q - 1))
                copy(pt_h[:, q % 2, 0:P * (q + 1)], bank(6 + q % 2)[:, 0:P * (q + 1)]).then_inc(s_pth, 1)

            def att_turn(c, u):
                f, a, r = c - 1, c - 2, c - 3
                if on(a):
                    for q in range(TG):
                        act.wait_ge(s_max, TG * a + (q + 1))
                        wait(act, s_ptp, TG * (a - 1) + (q + 1))
                        if q == 0:
                            wait(act, s_x2, TG * (a - 1))
                        act.activation(pr[:, q, 0:P * (q + 1)], bank(q)[:, 0:P * (q + 1)], ACT.Exp,
                                       bias=nbias[:, q:q + 1], scale=SCORE, accum_out=rsum[:, u % 2, q:q + 1]).then_inc(s_prob, 1)
                if on(a):
                    pth(a, 0)
                    pth(a, 1)
                if on(f):
                    wait(act, s_s, TG * (f - 1))
                    hi_halves(s_tp, f + NG, flat(zt_h[:, (u - 1) % 2]), s_th)
                if on(a):
                    pth(a, 2)
                    pth(a, 3)
                if on(f):
                    hi_halves(s_u, f, flat(u_h[:, :, :]), s_uh)
                if on(r):
                    v = (u - 3) % 2
                    act.wait_ge(s_scale2, r + 1)
                    wait(act, s_z2t, KD * (r - 1))
                    wait(act, s_zst[v], 16 * (NG // 2) + 8 * (r - v))
                    normalise(z2[:, v], x2[:, v], 1).then_inc(s_z2, 1)
                if on(f):
                    hi_halves(s_v, f, flat(v_h[:, :, :]), s_vh)
                if on(r):
                    hi_halves(s_z2t, r, flat(z2t_h[:, :, :]), s_z2h)
                if on(c):
                    act.wait_ge(s_scale, c + (NG // 2 + 1))
                    wait(act, s_tp, KD * (c + (NG - 1)))
                    normalise(zz[:, u % 2], xin[:, u], 0).then_inc(s_z, 1)

            turns(act, att_turn)
            stage_end(act, 3)
            route(1)
            ffn(1)
            stage_end(act, 4)

        @block.vector
        def _(dve):
            steps = Steps(dve, s_dve)
            link = steps.link
            one = lambda ap: ap.unsqueeze(2)

            def bc_j(ap):
                return ap.unsqueeze(2).broadcast_to([P, NE, P])

            dve.wait_ge(s_split, 1)
            link(dve.tensor_scalar(apart[:, :], apart[:, :], NE - 1, None, ALU.bitwise_and))
            link(dve.tensor_scalar(same_expert[:, :], apart[:, :], 0.0, None, ALU.is_equal))
            for k in range(KD):
                link(dve.tensor_tensor(rw_l[:, k, :], rws[:, k, :], rw_h[:, k, :], ALU.subtract))
            for lo, hi, b0 in ((g_l, g_h, 0), (m_l, m_h, 2)):
                for k in range(KD):
                    link(dve.scalar_tensor_tensor(lo[:, k, :], bank(b0 + k)[:, 0:D], WS, hi[:, k, :], ALU.mult, ALU.subtract))

            def stats(src, turn):
                for t in range(TG):
                    steps.done(dve.bn_stats(bst[:, turn, t, :], src[:, t, :]))
                steps.sync()
                dve.sem_inc(s_passed[1], 1)
                for t in range(TG):
                    last = dve.bn_aggr(mv[:, turn, t, :], bst[:, turn, t, :])
                return last

            def lge(g):
                t0 = g * TG
                dve.scalar_tensor_tensor(logits[:, bass.ds(t0, TG), :], lgb(g)[:, 0:TG * NE].rearrange("p (t e) -> p t e", t=TG), 1.0 / WS,
                                         rb[:, :].unsqueeze(1).broadcast_to([P, TG, NE]), ALU.mult, ALU.add).then_inc(s_lge, 1)

            lgb = lambda g: bank(7)

            def tl(g, u):
                for k in range(KD):
                    dve.wait_ge(s_th, KD * g + (k + 1))
                    dve.tensor_tensor(zt_l[:, u, k, :], ps[u][:, k, :], zt_h[:, u, k, :], ALU.subtract).then_inc(s_tl, 1)

            def group_logits(g, earlier=0):
                dve.wait_ge(s_lg, g + (earlier + 1))
                lge(g)

            def scan_turns(i):
                for w in range(WIDE // 2):
                    g = WIDE * i + 2 * w
                    wait(dve, s_scale, (WIDE // 2) * i + (w - 1))
                    for v in range(2):
                        dve.wait_ge(s_in[2 * w + v], 16 * i + 16)
                        last = stats(xin[:, 2 * w + v], (2 * w + v) % RING)
                    last.then_inc(s_mv, 1)
                    for v in range(2):
                        if on(g + v - 3):
                            group_logits(g + v - 3)
                        if on(g + v - 2):
                            tl(g + v - 2, v)
            repeat(dve, steps, scan_turns, NG // WIDE)
            for g in range(NG, NG + 3):
                group_logits(g - 3)
                if g < NG + 2:
                    tl(g - 2, g % 2)
            stage_end(dve, 1)

            def route(layer):
                by_tile = logits[:, :, :]
                mx, inv = rowv[:, 0, :], rowv[:, 1, :]
                over_e = lambda ap: ap.unsqueeze(2).broadcast_to([P, NT, NE])
                dve.wait_ge(s_lge, NG * (layer + 1))
                link(dve.tensor_reduce(mx, by_tile, AX.X, ALU.max))
                dve.tensor_tensor(by_tile, by_tile, over_e(mx), ALU.subtract).then_inc(s_route, 1)
                dve.wait_ge(s_exp, layer + 1)
                link(dve.tensor_reduce(mx, by_tile, AX.X, ALU.add))
                link(dve.reciprocal(inv, mx))
                dve.tensor_tensor(by_tile, by_tile, over_e(inv), ALU.mult).then_inc(s_route, 1)
                dve.wait_ge(s_pt, layer + 1)
                link(dve.tensor_copy(p_s[:, :, :].rearrange("p a b -> p (a b)"), ps[1][:, :, :].rearrange("p a b -> p (a b)")))
                dve.wait_ge(s_prr, layer + 1)
                flat = lambda a: a[:, :, :].rearrange("p e j -> p (e j)")
                p_top = flat(p_s).bitcast(BF16).rearrange("p (n two) -> p n two", two=2)[:, :, 1]
                dve.tensor_copy(top[:, :], p_top).then_inc(s_byte_in, 1)
                dve.wait_ge(s_byte_in, layer + 1)
                rounds = 0
                key = top
                for part in range(3):
                    floor = 0.0 if part == 0 else MARK
                    step = float(1 << (BITS - 2)) if part == 0 else 64.0
                    dve.memset(found_f[:, :], floor)
                    steps.done(dve.tensor_scalar(steps3[:, :], one_two_three[:, :], step, None, ALU.mult))
                    link(dve.memset(unit[:, :], step))
                    cands = cand if part == 0 else cand_f
                    link(dve.tensor_scalar(cands[:, :], steps3[:, :], floor, None, ALU.add))
                    compare = cand[:, :].bitcast(F32) if part == 0 else cand_f[:, :]
                    for i in range(ROUNDS[part]):
                        for m in range(3):
                            last = dve.tensor_scalar(junk[:, m, :], key[:, :], compare[:, m:m + 1], 0.0, ALU.is_ge, ALU.add,
                                                     accum_out=count[:, m:m + 1])
                        last.then_inc(s_cnt, 1)
                        final = i == ROUNDS[part] - 1
                        if i > 0:
                            steps.sync()
                            steps.done(dve.tensor_scalar(unit[:, :], unit[:, :], 0.25, None, ALU.mult))
                        if not final:
                            link(dve.tensor_scalar(steps3[:, :], steps3[:, :], 0.25, None, ALU.mult))
                            link(dve.tensor_scalar(next3[:, :], steps3[:, :], found_f[:, :], None, ALU.add))
                        rounds += 1
                        dve.wait_ge(s_tot, SEARCH * layer + rounds)
                        link(dve.tensor_scalar(sel[:, :], bank(4)[:, 0:3], float(CAP), 0.0, ALU.is_ge, ALU.add, accum_out=passed[:, :]))
                        if not final:
                            link(dve.scalar_tensor_tensor(cands[:, :], unit[:, :], passed[:, :], next3[:, :], ALU.mult, ALU.add))
                        steps.done(dve.scalar_tensor_tensor(found_f[:, :], unit[:, 0:1], passed[:, :], found_f[:, :], ALU.mult, ALU.add))
                    steps.sync()
                    if part < 2:
                        at = found_f[:, :]
                        if part == 0:
                            link(dve.tensor_copy(thr[:, :], at))
                            at = thr[:, :].bitcast(F32)
                            dve.wait_ge(s_bytes, layer + 1)
                        link(dve.tensor_scalar(junk[:, 0, :], key[:, :], at, None, ALU.is_gt))
                        link(dve.scalar_tensor_tensor(junk[:, 0, :], key[:, :], at, junk[:, 0, :], ALU.is_ge, ALU.add))
                        key = keys[part]
                        link(dve.scalar_tensor_tensor(key[:, :], junk[:, 0, :], MARK, byte[:, part, :], ALU.mult, ALU.add))
                    if part == 1:
                        link(dve.tensor_scalar(low[:, :], found_f[:, :], -MARK, 256.0, ALU.add, ALU.mult))
                link(dve.scalar_tensor_tensor(low_i[:, :], found_f[:, :], -MARK, low[:, :], ALU.add, ALU.add))
                link(dve.tensor_tensor(thr[:, :], thr[:, :], low_i[:, :], ALU.bitwise_or))
                dve.tensor_scalar(thr_m[:, :], ones[:, :], thr[:, :].bitcast(F32), None, ALU.mult).then_inc(s_route, 1)
                thr_b, n_above, n_equal, need, eq_before, prev, lim, n_mask, base, _ = (ten[:, k, :] for k in range(10))
                wait_tr(layer, 0)
                link(dve.tensor_copy(thr_b, bank(5)[:, 0:NE]))
                link(dve.tensor_tensor(above[:, :, :], p_r[:, :, :], bc_j(thr_b), ALU.is_gt))
                link(dve.tensor_tensor(equal[:, :, :], p_r[:, :, :], bc_j(thr_b), ALU.is_equal))
                link(dve.tensor_reduce(n_above, above[:, :, :], AX.X, ALU.add))
                dve.tensor_reduce(n_equal, equal[:, :, :], AX.X, ALU.add).then_inc(s_aux, 1)
                link(dve.tensor_tensor_scan(flat(scan), flat(equal), flat(equal), 0.0, ALU.add, ALU.bypass))
                link(dve.memset(prev[:, 0:1], 0.0))
                link(dve.tensor_copy(prev[:, 1:NE], scan[:, 0:NE - 1, P - 1]))
                wait_tr(layer, 1)
                link(dve.tensor_scalar(need, bank(5)[:, P:P + NE], -1.0, float(CAP), ALU.mult, ALU.add))
                link(dve.tensor_tensor(lim, need, bank(5)[:, P + NE:P + 2 * NE], ALU.subtract))
                link(dve.tensor_tensor(lim, lim, prev, ALU.add))
                link(dve.tensor_tensor(scan2[:, :, :], scan[:, :, :], bc_j(lim), ALU.is_le))
                link(dve.tensor_tensor(scan2[:, :, :], scan2[:, :, :], equal[:, :, :], ALU.mult))
                link(dve.tensor_tensor(mask[:, :, :], scan2[:, :, :], above[:, :, :], ALU.add))
                dve.tensor_reduce(n_mask, mask[:, :, :], AX.X, ALU.add).then_inc(s_aux, 1)
                link(dve.tensor_tensor_scan(flat(scan), flat(mask), flat(mask), 0.0, ALU.add, ALU.bypass))
                link(dve.tensor_copy(prev[:, 1:NE], scan[:, 0:NE - 1, P - 1]))
                wait_tr(layer, 2)
                link(dve.tensor_tensor(base, bank(5)[:, P + 2 * NE:P + 3 * NE], prev, ALU.subtract))
                link(dve.tensor_tensor(scan2[:, :, :], scan[:, :, :], bc_j(base), ALU.add))
                link(dve.tensor_tensor(scan2[:, :, :], scan2[:, :, :], mask[:, :, :], ALU.mult))
                link(dve.tensor_scalar(ranks[:, :, :], scan2[:, :, :], -1.0, None, ALU.add))
                link(dve.tensor_scalar(bits[:, :, :], ranks[:, :, :], P - 1, None, ALU.bitwise_and))
                link(dve.tensor_copy(rank_r[:, :, :], bits[:, :, :]))
                link(dve.tensor_scalar(bits[:, :, :], ranks[:, :, :], 7, None, ALU.arith_shift_right))
                link(dve.tensor_copy(rank_c[:, :, :], bits[:, :, :]))
                link(dve.tensor_tensor(scan[:, :, :], mask[:, :, :], p_r[:, :, :], ALU.mult))
                link(dve.tensor_reduce(rowv[:, 0, :], scan[:, :, :].rearrange("p e j -> p j e"), AX.X, ALU.add))
                link(dve.tensor_scalar(rowv[:, 0, :], rowv[:, 0, :], 1e-9, None, ALU.max))
                link(dve.reciprocal(rowv[:, 1, :], rowv[:, 0, :]))
                link(dve.tensor_scalar(rowv[:, 1, :], rowv[:, 1, :], 0.5 / YS, None, ALU.mult))
                link(dve.tensor_tensor(weight[:, :, :], scan[:, :, :], rowv[:, 1:2, :].broadcast_to([P, NE, P]), ALU.mult))
                link(dve.tensor_copy(wp[:, 0], weight[:, :, :]))
                link(dve.tensor_tensor(scan[:, :, :], weight[:, :, :], wp[:, 0], ALU.subtract))
                link(dve.tensor_copy(wp[:, 1], scan[:, :, :]))
                link(dve.tensor_tensor(wp[:, 2], scan[:, :, :], wp[:, 1], ALU.subtract))

            def wait_tr(layer, k):
                dve.wait_ge(s_trp, 3 * layer + k + 1)

            def hot_values(e, E, v):
                every_c = lambda ap: ap.unsqueeze(1).broadcast_to([P, SLOTS, P])
                if v == 0:
                    wait(dve, s_oh, NC * E)
                    link(dve.tensor_tensor(hot_b[:, 0], iota_c[:, :, :], every_c(rank_c[:, e, :]), ALU.is_equal))
                elif v == 1:
                    steps.done(dve.tensor_tensor(hot_b[:, 1], hot_b[:, 0], every_c(iota_b[:, :]), ALU.mult))
                elif v < NV:
                    steps.done(dve.tensor_tensor(hot_b[:, v], hot_b[:, 0], every_c(wp[:, v - 2, e, :]), ALU.mult))
                else:
                    steps.sync()
                    link(dve.tensor_scalar(hot_b[:, 0], hot_b[:, 0], part_f[:, :], None, ALU.mult))

            def hot_ranks(e, E, q, part=slice(0, QT)):
                if part.start == 0:
                    wait(dve, s_oh, NC * E + q - 1)
                for j in range(part.start, part.stop):
                    last = dve.tensor_scalar(hot_a[:, q % 2, j, :], iota_b[:, :], rank_r[:, e, QT * q + j:QT * q + j + 1], None, ALU.is_equal)
                if part.stop == QT:
                    last.then_inc(s_hot, 1)

            def lists(E):
                dve.wait_ge(s_oh, NC * (E + 1))
                for u in range(2):
                    wait(dve, s_xe[u], 16 * TG * (NC // 2) * E)
                link(dve.tensor_copy(found[:, :, :].rearrange("p v c -> p (v c)"), bank(6)[:, 0:NV * SLOTS]))
                link(dve.tensor_tensor(w_next[:, :], found[:, 2, :], found[:, 3, :], ALU.add))
                link(dve.tensor_tensor(w_next[:, :], w_next[:, :], found[:, 4, :], ALU.add))
                dve.scalar_tensor_tensor(tok_next[:, :], found[:, 0, :], float(P), found[:, 1, :], ALU.mult, ALU.add).then_inc(s_idx, 1)

            def ffn(layer):
                def xt_lo(E, c):
                    n = NC * E + c
                    for k in range(KD):
                        dve.wait_ge(s_xth, KD * n + (k + 1))
                        dve.tensor_tensor(xt_l[:, c % 2, k, :], ps[0][:, k, :], xt_h[:, c % 2, k, :], ALU.subtract).then_inc(s_xtl, 1)

                def hidden_lo(E, c, f):
                    n = NC * E + c
                    dve.wait_ge(s_hh, KF * n + f + 1)
                    dve.scalar_tensor_tensor(hid_l[:, c % 2, f, :], hf[:, f % HF, :], HS, hid_h[:, c % 2, f, :],
                                             ALU.mult, ALU.subtract).then_inc(s_hl, 1)

                def w1_lo(E):
                    dve.wait_ge(s_w1h, E + 1)
                    for k in range(KD):
                        last = dve.scalar_tensor_tensor(w1_l[:, k, :], w1_st[:, k, :], nws[:, k:k + 1], w1_h[:, k, :],
                                                        ALU.mult, ALU.subtract)
                    last.then_inc(s_w1, 1)

                def b2_rows(E):
                    dve.wait_ge(s_b2d, 16 * (E + 1))
                    wait(dve, s_y, TG * NC * E)
                    link(dve.tensor_scalar(b2_h[:, :], b2_st[:, :], YS, None, ALU.mult))
                    link(dve.scalar_tensor_tensor(b2_l[:, :], b2_st[:, :], YS, b2_h[:, :], ALU.mult, ALU.subtract))
                    link(dve.tensor_scalar(b2_h[:, :], b2_h[:, :], pick0[:, :], None, ALU.mult))
                    dve.scalar_tensor_tensor(b2_r[:, :], b2_l[:, :], pick1[:, :], b2_h[:, :], ALU.mult, ALU.add)

                def w2_lo(E, h):
                    dve.wait_ge(s_w2h, 4 * E + h + 1)
                    part = slice(h * KF // 4, (h + 1) * KF // 4)
                    dve.scalar_tensor_tensor(flat(w2_l[:, part, :]), flat(w2_st[:, part, :]), WS, flat(w2_h[:, part, :]),
                                             ALU.mult, ALU.subtract).then_inc(s_w2, 1)

                def to_now(E):
                    wait(dve, s_ys, TG * NC * E)
                    for u in range(2):
                        wait(dve, s_sc[u], 16 * TG * (NC // 2) * E)
                    dve.tensor_copy(w_now[:, :], w_next[:, :])
                    dve.tensor_copy(tok_now[:, :], tok_next[:, :]).then_inc(s_now, 1)

                def expert(e, final=False):
                    E = e + layer * NE
                    for f in range(KF):
                        hidden_lo(E, 0, f)
                        if f == 0:
                            b2_rows(E)
                        elif f % 2:
                            w2_lo(E, f // 2)
                        elif not final:
                            hot_values(e + 1, E + 1, f // 2 - 1)
                    xt_lo(E, 2)
                    for f in range(KF):
                        hidden_lo(E, 1, f)
                        if f < 3 and not final:
                            hot_values(e + 1, E + 1, 3 + f)
                    xt_lo(E, 3)
                    to_now(E)
                    if not final:
                        hot_ranks(e + 1, E + 1, 0)
                        hot_ranks(e + 1, E + 1, 1, slice(0, QT // 2))
                    for f in range(KF):
                        hidden_lo(E, 2, f)
                        if f % 2 == 0 and not final:
                            hot_ranks(e + 1, E + 1, 1, slice(QT // 2 + f * QT // 16, QT // 2 + (f + 2) * QT // 16))
                    if not final:
                        hot_ranks(e + 1, E + 1, 2)
                        hot_ranks(e + 1, E + 1, 3)
                    for f in range(KF):
                        hidden_lo(E, 3, f)
                        if f == 0 and not final:
                            lists(E + 1)
                    if not final:
                        w1_lo(E + 1)
                        xt_lo(E + 1, 0)
                        xt_lo(E + 1, 1)

                E0 = layer * NE
                for v in range(NV + 1):
                    hot_values(0, E0, v)
                for q in range(NC):
                    hot_ranks(0, E0, q)
                lists(E0)
                w1_lo(E0)
                xt_lo(E0, 0)
                xt_lo(E0, 1)
                repeat(dve, steps, expert, NE, lambda e: expert(e, True))

            route(0)
            ffn(0)
            stage_end(dve, 2)

            def lo_halves(ready, n, dst, hi, done):
                for k in range(KD):
                    dve.wait_ge(ready, KD * n + (k + 1))
                    cols = slice(k * S, (k + 1) * S)
                    dve.tensor_tensor(dst[:, cols], bank(4 + k), hi[:, cols], ALU.subtract).then_inc(done, 1)

            def ptl(a, q):
                dve.wait_ge(s_pth, TG * a + (q + 1))
                dve.tensor_tensor(pt_l[:, q % 2, 0:P * (q + 1)], bank(6 + q % 2)[:, 0:P * (q + 1)],
                                  pt_h[:, q % 2, 0:P * (q + 1)], ALU.subtract).then_inc(s_ptl, 1)

            def residual(a, q, v, ring):
                if q == 0:
                    wait(dve, s_z2, a - 1)
                    wait(dve, s_x2st[v], 8 * (a - v))
                    dve.wait_ge(s_prob, TG * (a + 1))
                    link(dve.tensor_scalar(rinv[:, :], rsum[:, v, :], WS, None, ALU.mult))
                    link(dve.reciprocal(rinv[:, :], rinv[:, :]))
                dve.wait_ge(s_o, TG * a + (q + 1))
                dve.scalar_tensor_tensor(x2[:, v, q, :], bank(q)[:, 0:D], rinv[:, q:q + 1], xin[:, ring, q, :],
                                         ALU.mult, ALU.add).then_inc(s_x2, 1)

            def att_turn(c, u):
                f, a, r, v, ring = c - 1, c - 2, c - 3, u % 2, (u - 2) % RING
                if on(a):
                    for q in range(TG):
                        dve.wait_ge(s_s, TG * a + (q + 1))
                        if q == 0:
                            wait(dve, s_prob, TG * a)
                        link(dve.tensor_reduce(nmax[:, q:q + 1], bank(q)[:, 0:P * (q + 1)], AX.X, ALU.max, negate=True))
                        dve.tensor_scalar(nbias[:, q:q + 1], nmax[:, q:q + 1], SCORE, None, ALU.mult).then_inc(s_max, 1)
                if on(r - 1):
                    group_logits(r - 1, NG)
                if on(a):
                    ptl(a, 0)
                    ptl(a, 1)
                if on(f):
                    lo_halves(s_th, f + NG, flat(zt_l[:, (u - 1) % 2]), flat(zt_h[:, (u - 1) % 2]), s_tl)
                if on(a):
                    residual(a, 0, v, ring)
                    ptl(a, 2)
                    residual(a, 1, v, ring)
                    ptl(a, 3)
                if on(c):
                    dve.wait_ge(s_in[u], 16 * (NG // WIDE) + ((c - u) * (16 // RING) + 16))
                    dve.wait_ge(s_scale, c + NG // 2)
                    stats(xin[:, u], 0).then_inc(s_mv, 1)
                if on(f):
                    lo_halves(s_uh, f, flat(u_l[:, :, :]), flat(u_h[:, :, :]), s_ul)
                if on(a):
                    residual(a, 2, v, ring)
                    residual(a, 3, v, ring)
                if on(f):
                    lo_halves(s_vh, f, flat(v_l[:, :, :]), flat(v_h[:, :, :]), s_vl)
                if on(a):
                    dve.wait_ge(s_x2, TG * (a + 1))
                    wait(dve, s_scale2, a)
                    stats(x2[:, v], 1).then_inc(s_mv2, 1)
                if on(r):
                    lo_halves(s_z2h, r, flat(z2t_l[:, :, :]), flat(z2t_h[:, :, :]), s_z2l)

            turns(dve, att_turn, steps)
            stage_end(dve, 3)
            route(1)
            ffn(1)
            stage_end(dve, 4)

        @block.tensor
        def _(pe):
            def split3(dst, lhs, rhs, first=True, last=True):
                (lh, ll), (rh, rl) = lhs, rhs
                pe.matmul(dst, lh, rh, start=first, stop=False)
                pe.matmul(dst, lh, rl, start=False, stop=False)
                return pe.matmul(dst, ll, rh, start=False, stop=last)

            pe.wait_ge(s_small, 16 * 8)
            pe.wait_ge(s_const, 1)
            for a, c, b0 in ((0, 1, 0), (2, 3, 2)):
                for m in range(KD):
                    for k in range(KD):
                        last = pe.matmul(bank(b0 + m)[:, 0:D], wst[:, a, k, m * P:(m + 1) * P], wst[:, c, k, :],
                                         start=(k == 0), stop=(k == KD - 1))
            last.then_inc(s_gm, 1)

            def transposes(dst, src, done, free):
                for k in range(KD):
                    free(k)
                    for t in range(TG):
                        last = pe.transpose(dst[:, k, t * P:(t + 1) * P], src[:, t, k * P:(k + 1) * P], ident[:, :])
                    last.then_inc(done, 1)

            def logit_products(hi, lo):
                for t in range(TG):
                    for k in range(KD):
                        for n, (a, w) in enumerate(((hi, rw_h), (hi, rw_l), (lo, rw_h))):
                            last = pe.matmul(bank(7)[:, t * NE:(t + 1) * NE], a[:, k, t * P:(t + 1) * P], w[:, k, :],
                                             start=(k == 0 and n == 0), stop=(k == KD - 1 and n == 2))
                return last

            pe.wait_ge(s_split, 1)

            def tz(g, v):
                pe.wait_ge(s_z, g + 1)
                transposes(ps[v], zz[:, v], s_tp, lambda k: wait(pe, s_tl, KD * (g - 2) + (k + 1)))

            def lg(g, v):
                pe.wait_ge(s_tl, KD * (g + 1))
                wait(pe, s_lge, g)
                logit_products(zt_h[:, v], zt_l[:, v]).then_inc(s_lg, 1)

            def scan_turns(i):
                for u in range(RING):
                    g = RING * i + u
                    tz(g, u % 2)
                    if on(g - 1):
                        lg(g - 1, (u - 1) % 2)
            scan_turns(0)
            with pe.Fori(1, NG // RING) as i:
                scan_turns(i)
            lg(NG - 1, (NG - 1) % 2)
            stage_end(pe, 1)

            def route(layer):
                pe.wait_ge(s_route, 3 * layer + 2)
                for e in range(NE):
                    pe.transpose(ps[0][:, e // 4, (e % 4) * P:(e % 4 + 1) * P], logits[:, :, e], ident[:, :])
                for b in range(NT // PER):
                    last = pe.transpose(ps[1][:, b // 4, (b % 4) * P:(b % 4 + 1) * P], logits[:, b * PER:(b + 1) * PER, :].rearrange("p t e -> p (t e)"), ident[:, :])
                last.then_inc(s_pt, 1)
                for i in range(SEARCH):
                    pe.wait_ge(s_cnt, SEARCH * layer + i + 1)
                    pe.matmul(bank(4)[:, 0:3], same_expert[:, :], count[:, :], start=True, stop=True).then_inc(s_tot, 1)
                pe.wait_ge(s_route, 3 * layer + 3)
                pe.transpose(bank(5)[:, 0:P], thr_m[:, :], ident[:, :]).then_inc(s_trp, 1)
                pe.wait_ge(s_aux, 2 * layer + 1)
                pe.matmul(bank(5)[:, P:P + NE], ones[:, :], ten[:, 1, :], start=True, stop=True)
                pe.matmul(bank(5)[:, P + NE:P + 2 * NE], before[:, :], ten[:, 2, :], start=True, stop=True).then_inc(s_trp, 1)
                pe.wait_ge(s_aux, 2 * layer + 2)
                pe.matmul(bank(5)[:, P + 2 * NE:P + 3 * NE], before[:, :], ten[:, 7, :], start=True, stop=True).then_inc(s_trp, 1)

            def ffn(layer):
                def xt(E, c):
                    n = NC * E + c
                    pe.wait_ge(s_xe[c % 2], 16 * TG * ((NC // 2) * E + c // 2 + 1))
                    transposes(ps[0], xe[:, c % 2], s_xt, lambda k: wait(pe, s_xtl, KD * (n - 1) + (k + 1)))

                def fc1(E, c):
                    n = NC * E + c
                    pe.wait_ge(s_xtl, KD * (n + 1))
                    if c == 0:
                        pe.wait_ge(s_w1, E + 1)
                    for f in range(KF):
                        wait(pe, s_gelu, KF * n + max(f - 2, 0))
                        for k in range(KD):
                            last = split3(bank(FC1[f % 3]), (w1_h[:, k, f * P:(f + 1) * P], w1_l[:, k, f * P:(f + 1) * P]),
                                          (xt_h[:, c % 2, k, :], xt_l[:, c % 2, k, :]), k == 0, k == KD - 1)
                        last.then_inc(s_h, 1)

                def fc2(E, c):
                    n = NC * E + c
                    pe.wait_ge(s_hl, KF * (n + 1))
                    if c == 0:
                        pe.wait_ge(s_w2, 4 * (E + 1))
                    for t in range(TG):
                        wait(pe, s_ys, TG * n + t - 1)
                        dst = bank(4 + t % 2)[:, 0:D]
                        pe.matmul(dst, ones_h[:, :], b2_r[:, :], start=True, stop=False)
                        for f in range(KF):
                            cols = slice(t * P, (t + 1) * P)
                            last = split3(dst, (hid_h[:, c % 2, f, cols], hid_l[:, c % 2, f, cols]), (w2_h[:, f, :], w2_l[:, f, :]),
                                          False, f == KF - 1)
                        last.then_inc(s_y, 1)

                def one_hot(E, q):
                    pe.wait_ge(s_hot, NC * E + q + 1)
                    if q == 0:
                        wait(pe, s_idx, E)
                    for j in range(QT):
                        col = QT * q + j
                        last = pe.matmul(bank(6)[:, 0:NV * SLOTS], hot_a[:, q % 2, j, :],
                                         hot_b[:, :, :, :].rearrange("p v c j -> p (v c) j")[:, :, col],
                                         start=(col == 0), stop=(col == P - 1))
                    last.then_inc(s_oh, 1)

                def expert(e, final=False):
                    E = e + layer * NE
                    fc1(E, 0)
                    xt(E, 2)
                    fc1(E, 1)
                    xt(E, 3)
                    fc2(E, 0)
                    if not final:
                        one_hot(E + 1, 0)
                    fc1(E, 2)
                    if not final:
                        one_hot(E + 1, 1)
                    fc2(E, 1)
                    if not final:
                        one_hot(E + 1, 2)
                        one_hot(E + 1, 3)
                    fc1(E, 3)
                    if not final:
                        xt(E + 1, 0)
                    fc2(E, 2)
                    if not final:
                        xt(E + 1, 1)
                    fc2(E, 3)

                E0 = layer * NE
                for q in range(NC):
                    one_hot(E0, q)
                xt(E0, 0)
                xt(E0, 1)
                expert(0)
                with pe.Fori(1, NE - 1) as e:
                    expert(e)
                expert(NE - 1, True)

            route(0)
            ffn(0)
            stage_end(pe, 2)

            def scores(a, v, q):
                if q == 0:
                    pe.wait_ge(s_ul, KD * (a + 1))
                wait(pe, s_x2, TG * (a - 1) + q + 1)
                dst = bank(q)[:, 0:P * (q + 1)]
                for k in range(KD):
                    cols = slice(q * P, (q + 1) * P)
                    split3(dst, (u_h[:, k, cols], u_l[:, k, cols]),
                           (zt_h[:, v, k, 0:P * (q + 1)], zt_l[:, v, k, 0:P * (q + 1)]), k == 0, False)
                pe.matmul(bank(q)[:, P * q:P * (q + 1)], ident_b[:, :], causal[:, :], start=False, stop=True).then_inc(s_s, 1)

            def pt(a, q):
                pe.wait_ge(s_prob, TG * a + (q + 1))
                wait(pe, s_ptl, TG * a + (q - 1))
                if q == 1:
                    wait(pe, s_lge, a + (NG - 1))
                for k in range(q + 1):
                    last = pe.transpose(bank(6 + q % 2)[:, k * P:(k + 1) * P], pr[:, q, k * P:(k + 1) * P], ident[:, :])
                last.then_inc(s_ptp, 1)

            def values(a, q):
                pe.wait_ge(s_ptl, TG * a + q + 1)
                if q == 0:
                    pe.wait_ge(s_vl, KD * (a + 1))
                for k in range(q + 1):
                    cols = slice(k * P, (k + 1) * P)
                    last = split3(bank(q)[:, 0:D], (pt_h[:, q % 2, cols], pt_l[:, q % 2, cols]), (v_h[:, k, :], v_l[:, k, :]),
                                  k == 0, k == q)
                last.then_inc(s_o, 1)

            def att_turn(c, u):
                f, a, r = c - 1, c - 2, c - 3
                zf = (u - 1) % 2
                if on(a):
                    for q in range(TG):
                        scores(a, u % 2, q)
                if on(r - 1):
                    wait(pe, s_ptl, TG * (a - 1) + TG if on(a - 1) else TG * NG)
                    pe.wait_ge(s_z2l, KD * r)
                    logit_products(z2t_h[:, :, :], z2t_l[:, :, :]).then_inc(s_lg, 1)
                if on(a):
                    pt(a, 0)
                    pt(a, 1)
                if on(f):
                    def rear_read(k):
                        wait(pe, s_vl, KD * (f - 1) + (k + 1))
                        wait(pe, s_z2l, KD * (r - 1) + (k + 1))
                    pe.wait_ge(s_z, f + (NG + 1))
                    transposes(ps[2], zz[:, zf], s_tp, rear_read)
                if on(a):
                    values(a, 0)
                    pt(a, 2)
                    values(a, 1)
                    pt(a, 3)
                if on(f):
                    pe.wait_ge(s_tl, KD * (f + (NG + 1)))
                    for m in range(KD):
                        for k in range(KD):
                            last = split3(ps[2][:, m, :], (g_h[:, k, m * P:(m + 1) * P], g_l[:, k, m * P:(m + 1) * P]),
                                          (zt_h[:, zf, k, :], zt_l[:, zf, k, :]), k == 0, k == KD - 1)
                        last.then_inc(s_u, 1)
                if on(a):
                    values(a, 2)
                    values(a, 3)
                if on(f):
                    for h in range(2):
                        pe.wait_ge(s_ul, KD * f + (h + 1))
                        for t in (2 * h, 2 * h + 1):
                            for k in range(KD):
                                cols = slice(t * P, (t + 1) * P)
                                last = split3(ps[2][:, h, (t % 2) * D:(t % 2 + 1) * D], (zt_h[:, zf, k, cols], zt_l[:, zf, k, cols]),
                                              (m_h[:, k, :], m_l[:, k, :]), k == 0, k == KD - 1)
                        last.then_inc(s_v, 1)
                if on(r):
                    def front_read(k):
                        pe.wait_ge(s_vl, KD * f + (k + 1) if on(f) else KD * NG)
                        wait(pe, s_z2l, KD * (r - 1) + (k + 1))
                    pe.wait_ge(s_z2, r + 1)
                    transposes(ps[2], z2[:, (u - 3) % 2], s_z2t, front_read)

            turns(pe, att_turn)
            stage_end(pe, 3)
            route(1)
            ffn(1)
            stage_end(pe, 4)


def kernel(L0_attn_x, L0_attn_W_q, L0_attn_W_k, L0_attn_W_v, L0_attn_W_o, L0_ffn_norm_weight, L0_ffn_router_w,
           L0_ffn_router_b, L0_ffn_fc1_w, L0_ffn_fc1_b, L0_ffn_fc2_w, L0_ffn_fc2_b):
    import numpy as np
    import concourse.bacc as bacc
    from concourse.bass_utils import run_bass_kernel_spmd

    def lay(a):
        return np.ascontiguousarray(a)

    experts, ff, _ = L0_ffn_fc1_w.shape
    arrays = {
        "x": lay(L0_attn_x),
        "wq": lay(L0_attn_W_q),
        "wk": lay(L0_attn_W_k),
        "wv": lay(L0_attn_W_v),
        "wo_t": lay(np.asarray(L0_attn_W_o).T),
        "norm_w": lay(np.asarray(L0_ffn_norm_weight).reshape(-1, 128).T),
        "router_t": lay(np.asarray(L0_ffn_router_w).T),
        "router_b": lay(L0_ffn_router_b),
        "fc1_t": lay(np.asarray(L0_ffn_fc1_w).transpose(0, 2, 1)),
        "fc1_b": lay(np.asarray(L0_ffn_fc1_b).reshape(experts, ff // 128, 128).transpose(2, 0, 1)),
        "fc2_t": lay(np.asarray(L0_ffn_fc2_w).transpose(0, 2, 1)),
        "fc2_b": lay(L0_ffn_fc2_b),
    }
    nc = bacc.Bacc("TRN2", target_bir_lowering=False, num_devices=1)
    args = {n: nc.dram_tensor(n, a.shape, mybir.dt.from_np(a.dtype), kind="ExternalInput").ap() for n, a in arrays.items()}
    out = nc.dram_tensor("out", arrays["x"].shape, F32, kind="ExternalOutput").ap()
    macaron(nc, out=out, **args)
    r = run_bass_kernel_spmd(nc, [arrays], core_ids=[0])
    return r.results[0]["out"]
```

```python
from contextlib import ExitStack

import concourse.bass as bass
from concourse import mybir
from concourse.alu_op_type import AluOpType as ALU

F32 = mybir.dt.float32
F16 = mybir.dt.float16
BF16 = mybir.dt.bfloat16
I32 = mybir.dt.int32
U32 = mybir.dt.uint32
U8 = mybir.dt.uint8
ACT = mybir.ActivationFunctionType
AX = mybir.AxisListType


class Steps:

    def __init__(self, engine, sem):
        self.engine, self.sem, self.n = engine, sem, 0

    def done(self, instruction):
        instruction.then_inc(self.sem, 1)
        self.n = self.n + 1

    def sync(self):
        self.engine.wait_ge(self.sem, self.n)

    def link(self, instruction):
        self.done(instruction)
        self.sync()


def repeat(engine, steps, body, count, last=None, once=None):
    start = steps.n
    body(0)
    per = steps.n - start
    if once:
        once()
        start = steps.n - per
    end = count - 1 if last else count
    with engine.Fori(1, end) as i:
        steps.n = i * per + start
        body(i)
    steps.n = start + end * per
    if last:
        last(end)


def wait(engine, sem, value):
    if not isinstance(value, int) or value > 0:
        engine.wait_ge(sem, value)


def macaron(nc, x, wq, wk, wv, wo_t, norm_w, router_t, router_b, fc1_t, fc1_b, fc2_t, fc2_b, out):
    P = 128
    B, S, D = x.shape
    T = B * S
    NE, _, FF = fc1_t.shape
    CAP = T // NE
    NT = T // P
    KD = D // P
    KF = FF // P
    TG = S // P
    NG = T // S
    NC = CAP // S
    SLOTS = CAP // P
    FC1 = (2, 3, 7)
    EPS = 1e-5
    WS = 64.0
    HS = 16.0
    YS = WS * HS
    SCORE = 1.0 / (D ** 0.5 * WS)
    BITS = 30
    ROUNDS = ((BITS - 16) // 2, 4, 4)
    SEARCH = sum(ROUNDS)
    MARK = 1024.0
    ABOVE, EQUAL, CHOSEN = 1, 2, 6
    FAR = 2.0 * CAP
    HF = 4
    PER = P // NE
    NV = 5
    QT = P // NC
    RING = 4
    WIDE = 8
    LEAD = 7
    assert KD == 2 and TG == 4 and NC == 4 and PER * NE == P and NT == P

    xf = x.rearrange("b s d -> (b s) d")
    outf = out.rearrange("b s d -> (b s) d")
    x1_d = nc.dram_tensor("x1_d", [T, D], F32).ap()
    z_d = nc.dram_tensor("z_d", [T, D], F32).ap()

    def group(d, g):
        return d.rearrange("(g j p) d -> g p j d", p=P, j=TG)[g]

    ctx = ExitStack()
    with ctx:
        def sb(name, shape, dt, stack=ctx):
            return stack.enter_context(nc.sbuf_tensor(name, shape, dt))

        def sem(name):
            return ctx.enter_context(nc.semaphore(name))

        ident = sb("ident", [P, P], F32)
        ident_b = sb("ident_b", [P, P], BF16)
        causal = sb("causal", [P, P], BF16)
        ones = sb("ones", [P, P], F32)
        ones_h = sb("ones_h", [P, P], F16)
        before = sb("before", [P, P], F32)
        apart = sb("apart", [P, P], I32)
        same_expert = sb("same_expert", [P, P], F32)
        iota_i = sb("iota_i", [P, P], I32)
        iota_b = sb("iota_b", [P, P], BF16)
        iota_c = sb("iota_c", [P, SLOTS, P], BF16)
        one_two_three = sb("one_two_three", [P, 3], F32)
        part_i = sb("part_i", [P, 1], I32)
        part_f = sb("part_f", [P, 1], F32)
        minus_half = sb("minus_half", [P, 2, TG], F32)
        eps = sb("eps", [P, 2, TG], F32)
        minus_one = sb("minus_one", [P, 2, TG], F32)
        pick0 = sb("pick0", [P, 1], F32)
        pick1 = sb("pick1", [P, 1], F32)
        nw = sb("nw", [P, KD], F32)
        nws = sb("nws", [P, KD], F32)
        rb = sb("rb", [P, NE], F32)
        b1 = sb("b1", [P, NE, KF], F32)
        b1_now = sb("b1_now", [P, KF], F32)
        warm = sb("warm", [P, 1], F32)
        rw = sb("rw", [P, KD, NE], F32)
        rws = sb("rws", [P, KD, NE], F32)
        rw_h = sb("rw_h", [P, KD, NE], F16)
        rw_l = sb("rw_l", [P, KD, NE], F16)
        g_h = sb("g_h", [P, KD, D], F16)
        g_l = sb("g_l", [P, KD, D], F16)
        m_h = sb("m_h", [P, KD, D], F16)
        m_l = sb("m_l", [P, KD, D], F16)
        logits = sb("logits", [P, NT, NE], F32)
        mv = sb("mv", [P, RING, TG, 2], F32)
        bst = sb("bst", [P, RING, TG, 6], F32)
        nt = sb("nt", [P, 7, RING, TG], F32)
        zs = sb("zs", [P, RING, TG], F32)
        zb = sb("zb", [P, RING, TG], F32)

        ffn = ExitStack()
        w1_st = sb("w1_st", [P, KD, FF], F32, ffn)
        w2_st = sb("w2_st", [P, KF, D], F32, ffn)
        b2_st = sb("b2_st", [P, D], F32, ffn)
        w1_h = sb("w1_h", [P, KD, FF], F16, ffn)
        w1_l = sb("w1_l", [P, KD, FF], F16, ffn)
        w2_h = sb("w2_h", [P, KF, D], F16, ffn)
        w2_l = sb("w2_l", [P, KF, D], F16, ffn)
        b2_h = sb("b2_h", [P, D], F16, ffn)
        b2_l = sb("b2_l", [P, D], F16, ffn)
        b2_r = sb("b2_r", [P, D], F16, ffn)
        rank_r = sb("rank_r", [P, NE, P], F32, ffn)
        rank_c = sb("rank_c", [P, NE, P], BF16, ffn)
        wp = sb("wp", [P, 3, NE, P], BF16, ffn)
        hot_a = sb("hot_a", [P, NC, QT, P], BF16, ffn)
        hot_b = sb("hot_b", [P, NV, SLOTS, P], BF16, ffn)
        found = sb("found", [P, NV, SLOTS], F32, ffn)
        w_next = sb("w_next", [P, SLOTS], F32, ffn)
        w_now = sb("w_now", [P, SLOTS], F32, ffn)
        tok_next = sb("tok_next", [P, SLOTS], I32, ffn)
        tok_now = sb("tok_now", [P, SLOTS], I32, ffn)
        shared = ExitStack()
        xe = sb("xe", [P, 2, TG, D], F32, shared)
        xt_h = sb("xt_h", [P, 2, KD, S], F16, shared)
        xt_l = sb("xt_l", [P, 2, KD, S], F16, shared)
        hf = sb("hf", [P, HF, S], F32, shared)
        hid_h = sb("hid_h", [P, 2, KF, S], F16, shared)
        hid_l = sb("hid_l", [P, 2, KF, S], F16, shared)
        ys = sb("ys", [P, 2, TG, D], F32, shared)
        shared.close()
        rout = ExitStack()
        p_r = sb("p_r", [P, NE, P], F32, rout)
        above = sb("above", [P, NE, P], F32, rout)
        equal = sb("equal", [P, NE, P], F32, rout)
        scan = sb("scan", [P, NE, P], F32, rout)
        scan2 = sb("scan2", [P, NE, P], F32, rout)
        mask = sb("mask", [P, NE, P], F32, rout)
        ranks = sb("ranks", [P, NE, P], I32, rout)
        bits = sb("bits", [P, NE, P], I32, rout)
        bits_r = sb("bits_r", [P, NE, P], I32, rout)
        above_out = sb("above_out", [P, NE, P], BF16, rout)
        gate = sb("gate", [P, NE, P], F32, rout)
        gsum = sb("gsum", [P, NE // 2, P], F32, rout)
        rowv = sb("rowv", [P, 2, P], F32, rout)
        per_expert = sb("per_expert", [P, 8, NE], F32, rout)
        thr = sb("thr", [P, 1], I32, rout)
        cand = sb("cand", [P, 3], I32, rout)
        cand_f = sb("cand_f", [P, 3], F32, rout)
        sel = sb("sel", [P, 3], F32, rout)
        count = sb("count", [P, 3], F32, rout)
        steps3 = sb("steps3", [P, 3], F32, rout)
        next3 = sb("next3", [P, 3], F32, rout)
        unit = sb("unit", [P, 3], F32, rout)
        passed = sb("passed", [P, 1], F32, rout)
        found_f = sb("found_f", [P, 1], F32, rout)
        low = sb("low", [P, 1], F32, rout)
        low_i = sb("low_i", [P, 1], I32, rout)
        top = sb("top", [P, NE * P], BF16, rout)
        junk = sb("junk", [P, 3, NE * P], BF16, rout)
        keys = [sb("key_1", [P, NE * P], F16, rout), sb("key_2", [P, NE * P], F16, rout)]
        byte = sb("byte", [P, 2, NE * P], F16, rout)
        thr_m = sb("thr_m", [P, P], F32, rout)
        rout.close()
        ffn.close()

        att = ExitStack()
        wst = sb("wst", [P, 4, KD, D], F32, att)
        xin = sb("xin", [P, WIDE, TG, D], F32, att)
        zz = sb("zz", [P, 2, TG, D], F32, att)
        zt_h = sb("zt_h", [P, 2, KD, S], F16, att)
        zt_l = sb("zt_l", [P, 2, KD, S], F16, att)
        u_h = sb("u_h", [P, KD, S], F16, att)
        u_l = sb("u_l", [P, KD, S], F16, att)
        v_h = sb("v_h", [P, TG, D], F16, att)
        v_l = sb("v_l", [P, TG, D], F16, att)
        pr = sb("pr", [P, TG, S], F32, att)
        pt_h = sb("pt_h", [P, 2, S], F16, att)
        pt_l = sb("pt_l", [P, 2, S], F16, att)
        x2 = sb("x2", [P, 2, TG, D], F32, att)
        z2 = sb("z2", [P, 2, TG, D], F32, att)
        z2t_h = sb("z2t_h", [P, KD, S], F16, att)
        z2t_l = sb("z2t_l", [P, KD, S], F16, att)
        nmax = sb("nmax", [P, TG], F32, att)
        nbias = sb("nbias", [P, TG], F32, att)
        rsum = sb("rsum", [P, 2, TG], F32, att)
        rinv = sb("rinv", [P, TG], F32, att)
        att.close()

        ps = [ctx.enter_context(nc.psum_tensor(f"ps{i}", [P, 2, 512], F32)) for i in range(4)]

        def bank(i):
            return ps[i // 2][:, i % 2, :]

        s_phase = sem("s_phase")
        s_pool, s_dve, s_act = sem("s_pool"), sem("s_dve"), sem("s_act")
        s_const, s_small, s_split = sem("s_const"), sem("s_small"), sem("s_split")
        s_wst = sem("s_wst")
        s_gm, s_gmh = sem("s_gm"), sem("s_gmh")
        s_in = [sem(f"s_in{i}") for i in range(WIDE)]
        s_mv, s_scale, s_z = sem("s_mv"), sem("s_scale"), sem("s_z")
        s_zst = [sem("s_zst0"), sem("s_zst1")]
        s_x2st = [sem("s_x2st0"), sem("s_x2st1")]
        s_tp, s_th, s_tl = sem("s_tp"), sem("s_th"), sem("s_tl")
        s_lg, s_lge = sem("s_lg"), sem("s_lge")
        s_copy = sem("s_copy")
        s_passed = [sem("s_passed0"), sem("s_passed1")]
        s_top = sem("s_top")
        s_above, s_nabove = sem("s_above"), sem("s_nabove")
        s_mask, s_gsum, s_ginv = sem("s_mask"), sem("s_gsum"), sem("s_ginv")
        s_values = sem("s_values")
        s_wp, s_low, s_rank = sem("s_wp"), sem("s_low"), sem("s_rank")
        s_bytes = sem("s_bytes")
        s_exp, s_pt, s_route, s_prr, s_cnt, s_tot = (sem(n) for n in ("s_exp", "s_pt", "s_route", "s_prr", "s_cnt", "s_tot"))
        s_w1d, s_w2d, s_b2d = sem("s_w1d"), sem("s_w2d"), sem("s_b2d")
        s_w1h, s_w1, s_w2h, s_w2 = sem("s_w1h"), sem("s_w1"), sem("s_w2h"), sem("s_w2")
        s_xe = [sem("s_xe0"), sem("s_xe1")]
        s_sc = [sem("s_sc0"), sem("s_sc1")]
        s_xt, s_xth, s_xtl = sem("s_xt"), sem("s_xth"), sem("s_xtl")
        s_h, s_gelu, s_hh, s_hl = sem("s_h"), sem("s_gelu"), sem("s_hh"), sem("s_hl")
        s_y, s_ys = sem("s_y"), sem("s_ys")
        s_hot, s_oh, s_idx, s_now = sem("s_hot"), sem("s_oh"), sem("s_idx"), sem("s_now")
        s_s, s_max, s_prob = sem("s_s"), sem("s_max"), sem("s_prob")
        s_ptp, s_pth, s_ptl = sem("s_ptp"), sem("s_pth"), sem("s_ptl")
        s_o, s_x2 = sem("s_o"), sem("s_x2")
        s_u, s_uh, s_ul = sem("s_u"), sem("s_uh"), sem("s_ul")
        s_v, s_vh, s_vl = sem("s_v"), sem("s_vh"), sem("s_vl")
        s_z2t, s_z2h, s_z2l = sem("s_z2t"), sem("s_z2h"), sem("s_z2l")
        s_aux, s_trp = sem("s_aux"), sem("s_trp")
        s_mv2, s_scale2, s_z2 = sem("s_mv2"), sem("s_scale2"), sem("s_z2")

        def on(g):
            return not isinstance(g, int) or 0 <= g < NG

        def turns(engine, turn, steps=None):
            for c in range(RING):
                n0 = steps.n if steps else 0
                turn(c, c)
            per = steps.n - n0 if steps else 0
            with engine.Fori(1, NG // RING) as i:
                for u in range(RING):
                    if steps:
                        steps.n = i * (RING * per) + (n0 + (u - RING + 1) * per)
                    turn(RING * i + u, u)
            if steps:
                steps.n = n0 + per * (NG - RING + 1)
            for c in range(NG, NG + RING):
                turn(c, c % RING)

        def flat(t):
            return t.rearrange("p a b -> p (a b)")

        block = ctx.enter_context(nc.Block())
        ENGINES = 5

        def stage_end(engine, k):
            engine.drain().then_inc(s_phase, 1)
            engine.wait_ge(s_phase, ENGINES * k)

        @block.sync
        def _(sp):
            steps = Steps(sp, None)
            for dst, src in ((nw[:, :], norm_w), (rb[:, :], router_b.rearrange("(a e) -> a e", a=1).broadcast_to([P, NE])),
                             (b1[:, :, :], fc1_b),
                             (rw[:, :, :], router_t.rearrange("(k p) e -> p k e", p=P))):
                sp.dma_start(dst, src).then_inc(s_small, 16)

            def attention_weights():
                for dst, src in ((wst[:, 0], wq.rearrange("(k p) e -> p k e", p=P)),
                                 (wst[:, 1], wk.rearrange("(k p) e -> p k e", p=P)),
                                 (wst[:, 2], wv.rearrange("(k p) e -> p k e", p=P)),
                                 (wst[:, 3], wo_t.rearrange("(k p) e -> p k e", p=P))):
                    sp.dma_start(dst, src).then_inc(s_wst, 16)

            def scan_turns(i):
                for u in range(WIDE):
                    g = WIDE * i + u
                    wait(sp, s_z, g - WIDE + 1)
                    sp.dma_start(xin[:, u], group(xf, g)).then_inc(s_in[u], 16)
                    if on(g - LEAD):
                        z_out(g - LEAD, (u - LEAD) % 2)

            def z_out(g, v):
                sp.wait_ge(s_z, g + 1)
                sp.dma_start(group(z_d, g), zz[:, v]).then_inc(s_zst[v], 16)

            repeat(sp, steps, scan_turns, NG // WIDE, once=attention_weights)
            for g in range(NG - LEAD, NG):
                z_out(g, g % 2)
            sp.dma_start(x1_d.rearrange("(a b) d -> a (b d)", b=8), xf.rearrange("(a b) d -> a (b d)", b=8)).then_inc(s_copy, 16)
            for u in range(2):
                sp.wait_ge(s_zst[u], 16 * (NG // 2))
            stage_end(sp, 1)

            def ffn_loads(layer):
                def load(e):
                    E = e + layer * NE
                    wait(sp, s_w1, E)
                    sp.dma_start(w1_st[:, :, :], fc1_t[e].rearrange("(k p) f -> p k f", p=P)).then_inc(s_w1d, 16)
                    wait(sp, s_w2, 4 * E)
                    sp.dma_start(w2_st[:, :, :], fc2_t[e].rearrange("(k p) d -> p k d", p=P)).then_inc(s_w2d, 16)
                    sp.dma_start(b2_st[:, :], fc2_b[e].rearrange("(a d) -> a d", a=1).broadcast_to([P, D])).then_inc(s_b2d, 16)
                repeat(sp, steps, load, NE)

            ffn_loads(0)
            stage_end(sp, 2)

            def att_turn(c, u):
                if on(c):
                    wait(sp, s_x2, TG * (c - RING + 1))
                    sp.dma_start(xin[:, u], group(x1_d, c)).then_inc(s_in[u], 16)
                if on(c - 3):
                    v = (u - 3) % 2
                    sp.wait_ge(s_x2, TG * (c - 2))
                    sp.dma_start(group(outf, c - 3), x2[:, v]).then_inc(s_x2st[v], 16)
                if on(c - 4):
                    sp.wait_ge(s_z2, c - 3)
                    sp.dma_start(group(z_d, c - 4), z2[:, u % 2]).then_inc(s_zst[u % 2], 16)

            turns(sp, att_turn)
            for u in range(2):
                sp.wait_ge(s_x2st[u], 16 * (NG // 2))
                sp.wait_ge(s_zst[u], 16 * NG)
            stage_end(sp, 3)
            ffn_loads(1)
            stage_end(sp, 4)

        @block.gpsimd
        def _(pool):
            steps = Steps(pool, s_pool)
            pool.memset(ident[:, :], 0.0)
            pool.memset(ident_b[:, :], 0.0)
            pool.memset(causal[:, :], 0.0)
            pool.memset(ones[:, :], 1.0)
            pool.memset(ones_h[:, :], 1.0)
            pool.memset(before[:, :], 1.0)
            pool.memset(minus_half[:, :, :], -0.5)
            pool.memset(minus_one[:, :, :], -1.0)
            pool.memset(eps[:, :, :], EPS)
            pool.memset(pick0[:, :], 0.0)
            pool.memset(pick1[:, :], 0.0)
            pool.iota(iota_i[:, :], pattern=[[1, P]], base=0, channel_multiplier=0)
            steps.link(pool.iota(part_i[:, :], pattern=[[0, 1]], base=0, channel_multiplier=1))
            for m in (ident, ident_b):
                pool.affine_select(out=m[:, :], in_=m[:, :], compare_op=ALU.not_equal, fill=1.0, base=0,
                                   pattern=[[-1, P]], channel_multiplier=1)
            pool.affine_select(out=causal[:, :], in_=causal[:, :], compare_op=ALU.is_ge, fill=-1e30, base=0,
                               pattern=[[-1, P]], channel_multiplier=1)
            pool.affine_select(out=before[:, :], in_=before[:, :], compare_op=ALU.is_gt, fill=0.0, base=0,
                               pattern=[[1, P]], channel_multiplier=-1)
            pool.affine_select(out=pick0[:, :], in_=pick0[:, :], compare_op=ALU.not_equal, fill=1.0, base=0,
                               pattern=[[0, 1]], channel_multiplier=1)
            pool.affine_select(out=pick1[:, :], in_=pick1[:, :], compare_op=ALU.not_equal, fill=1.0, base=-1,
                               pattern=[[0, 1]], channel_multiplier=1)
            pool.iota(apart[:, :], pattern=[[1, P]], base=P, channel_multiplier=-1)
            pool.tensor_copy(part_f[:, :], part_i[:, :])
            pool.tensor_copy(iota_b[:, :], iota_i[:, :])
            pool.tensor_copy(one_two_three[:, :], iota_i[:, 1:4]).then_inc(s_const, 1)
            pool.iota(iota_c[:, :, :], pattern=[[1, SLOTS], [0, P]], base=0, channel_multiplier=0,
                      allow_small_or_imprecise_dtypes=True)

            def row_factors(at, n):
                m, v = mv[:, at:at + n, :, 0], mv[:, at:at + n, :, 1]
                a, r, q, q2, c, r2, minus_m = (nt[:, k, at:at + n, :] for k in range(7))
                steps.done(pool.tensor_tensor(minus_m, m, minus_one[:, 0:n, :], ALU.mult))
                steps.link(pool.tensor_tensor(a, v, eps[:, 0:n, :], ALU.add))
                steps.link(pool.tensor_tensor(r, a, minus_half[:, 0:n, :], ALU.pow))
                steps.link(pool.tensor_tensor(q, v, r, ALU.mult))
                steps.link(pool.tensor_tensor(q2, q, r, ALU.mult))
                steps.link(pool.tensor_tensor(c, q2, eps[:, 0:n, :], ALU.add))
                steps.link(pool.tensor_tensor(r2, c, minus_half[:, 0:n, :], ALU.pow))
                steps.link(pool.tensor_tensor(zs[:, at:at + n, :], r, r2, ALU.mult))
                return pool.tensor_tensor(zb[:, at:at + n, :], minus_m, zs[:, at:at + n, :], ALU.mult)

            def scan_turns(i):
                for w in range(WIDE // 2):
                    pool.wait_ge(s_mv, (WIDE // 2) * i + (w + 1))
                    wait(pool, s_z, WIDE * i + 2 * (w - 1))
                    row_factors(2 * w % RING, 2).then_inc(s_scale, 1)
            repeat(pool, steps, scan_turns, NG // WIDE)
            stage_end(pool, 1)

            def weights(layer):
                pool.wait_ge(s_mask, layer + 1)
                steps.link(pool.tensor_tensor(gate[:, :, :], mask[:, :, :], p_r[:, :, :], ALU.mult))
                steps.link(pool.tensor_tensor(gsum[:, :, :], gate[:, 0:NE // 2, :], gate[:, NE // 2:NE, :], ALU.add))
                n = NE // 4
                while n > 1:
                    steps.link(pool.tensor_tensor(gsum[:, 0:n, :], gsum[:, 0:n, :], gsum[:, n:2 * n, :], ALU.add))
                    n //= 2
                pool.tensor_tensor(gsum[:, 0, :], gsum[:, 0, :], gsum[:, 1, :], ALU.add).then_inc(s_gsum, 1)
                pool.wait_ge(s_ginv, layer + 1)
                steps.link(pool.tensor_tensor(gate[:, :, :], gate[:, :, :], rowv[:, 1:2, :].broadcast_to([P, NE, P]), ALU.mult))
                for k in range(2):
                    steps.link(pool.tensor_copy(wp[:, k], gate[:, :, :]))
                    if k == 0:
                        steps.link(pool.tensor_tensor(gate[:, :, :], gate[:, :, :], wp[:, k], ALU.subtract))
                pool.tensor_tensor(wp[:, 2], gate[:, :, :], wp[:, 1], ALU.subtract).then_inc(s_wp, 1)

            def ffn_rows(layer, rows, acc):
                def gather(E, c):
                    n = NC * E + c
                    wait(pool, s_xt, KD * (n - 1))
                    pool.sem_inc(s_passed[0], 1)
                    for t in range(TG):
                        k = TG * c + t
                        pool.indirect_dma_start(xe[:, c % 2, t, :], None, rows,
                                                bass.IndirectOffsetOnAxis(ap=tok_next[:, k:k + 1].bitcast(U32), axis=0)).then_inc(s_xe[c % 2], 16)

                def scatter(E, c):
                    n = NC * E + c
                    if c == 0:
                        pool.wait_ge(s_now, E + 1)
                    pool.wait_ge(s_ys, TG * (n + 1))
                    pool.sem_inc(s_passed[0], 1)
                    for t in range(TG):
                        k = TG * c + t
                        pool.indirect_dma_start(acc, bass.IndirectOffsetOnAxis(ap=tok_now[:, k:k + 1].bitcast(U32), axis=0),
                                                ys[:, c % 2, t, :], None, compute_op=ALU.add).then_inc(s_sc[c % 2], 16)

                def expert(e, final=False):
                    E = e + layer * NE
                    gather(E, 3)
                    scatter(E, 0)
                    scatter(E, 1)
                    if not final:
                        pool.wait_ge(s_idx, E + 2)
                        gather(E + 1, 0)
                        gather(E + 1, 1)
                    scatter(E, 2)
                    if not final:
                        gather(E + 1, 2)
                    scatter(E, 3)

                pool.wait_ge(s_idx, layer * NE + 1)
                pool.wait_ge(s_copy, 16)
                for c in range(3):
                    gather(layer * NE, c)
                repeat(pool, steps, expert, NE, lambda e: expert(e, True))
                for u in range(2):
                    pool.wait_ge(s_sc[u], 16 * TG * (NC // 2) * NE * (layer + 1))

            weights(0)
            ffn_rows(0, z_d, x1_d)
            stage_end(pool, 2)

            def att_turn(c, u):
                if on(c):
                    pool.wait_ge(s_mv, c + (NG // 2 + 1))
                    pool.wait_ge(s_z, c + NG)
                    row_factors(0, 1).then_inc(s_scale, 1)
                a = c - 2
                if on(a):
                    pool.wait_ge(s_mv2, a + 1)
                    wait(pool, s_z2, a)
                    row_factors(1, 1).then_inc(s_scale2, 1)

            turns(pool, att_turn, steps)
            stage_end(pool, 3)
            weights(1)
            ffn_rows(1, z_d, outf)
            stage_end(pool, 4)

        @block.scalar
        def _(act):
            steps = Steps(act, s_act)

            def copy(dst, src, **kw):
                return act.activation(dst, src, ACT.Copy, **kw)

            act.wait_ge(s_small, 16 * 4)
            steps.link(copy(nws[:, :], nw[:, :], scale=WS))
            for k in range(KD):
                steps.link(copy(rws[:, k, :], rw[:, k, :], scale=nws[:, k:k + 1]))
                steps.link(copy(rw_h[:, k, :], rws[:, k, :]))
            copy(nbias[:, 0:1], nws[:, 0:1]).then_inc(s_split, 1)

            def attention_weights():
                act.wait_ge(s_gm, 1)
                for n, dst in enumerate((g_h, m_h)):
                    for k in range(KD):
                        last = copy(dst[:, k, :], bank(4 + n)[:, k * D:(k + 1) * D], scale=WS)
                last.then_inc(s_gmh, 1)

            def th(g, u):
                for k in range(KD):
                    act.wait_ge(s_tp, KD * g + (k + 1))
                    if k == 0:
                        wait(act, s_lg, g - 1)
                    copy(zt_h[:, u, k, :], ps[u][:, k, :]).then_inc(s_th, 1)

            def normalise(dst, src, at):
                for t in range(TG):
                    last = act.activation(dst[:, t, :], src[:, t, :], ACT.Identity, bias=zb[:, at, t:t + 1], scale=zs[:, at, t:t + 1])
                return last

            def scan_turns(i):
                for w in range(WIDE // 2):
                    act.wait_ge(s_scale, (WIDE // 2) * i + (w + 1))
                    for v in range(2):
                        g = WIDE * i + (2 * w + v)
                        wait(act, s_tp, KD * (g - 1))
                        wait(act, s_zst[v], 8 * WIDE * i + 16 * w)
                        normalise(zz[:, v], xin[:, 2 * w + v], (2 * w + v) % RING).then_inc(s_z, 1)
                        if on(g - 1):
                            th(g - 1, (v - 1) % 2)
            repeat(act, steps, scan_turns, NG // WIDE, once=attention_weights)
            th(NG - 1, (NG - 1) % 2)
            stage_end(act, 1)

            def route(layer):
                act.wait_ge(s_route, 3 * layer + 1)
                act.activation(logits[:, :, :], logits[:, :, :], ACT.Exp).then_inc(s_exp, 1)
                act.wait_ge(s_top, layer + 1)
                octets = flat(ps[1][:, :, :]).bitcast(U8).rearrange("p (n four) -> p n four", four=4)
                for k in range(2):
                    last = copy(byte[:, k, :], octets[:, :, 1 - k])
                last.then_inc(s_bytes, 1)
                act.wait_ge(s_pt, 2 * layer + 2)
                copy(flat(p_r[:, :, :]), flat(ps[0][:, :, :])).then_inc(s_prr, 1)
                act.wait_ge(s_above, layer + 1)
                for e in range(NE):
                    last = copy(above_out[:, e, :], above[:, e, :], accum_out=per_expert[:, ABOVE, e:e + 1])
                last.then_inc(s_nabove, 1)
                act.wait_ge(s_low, layer + 1)
                copy(rank_r[:, :, :], bits_r[:, :, :]).then_inc(s_rank, 1)

            def ffn(layer):
                def xt_hi(E, c):
                    n = NC * E + c
                    wait(act, s_h, KF * (n - 1))
                    for k in range(KD):
                        act.wait_ge(s_xt, KD * n + (k + 1))
                        copy(xt_h[:, c % 2, k, :], ps[0][:, k, :]).then_inc(s_xth, 1)

                def bias(e, E):
                    wait(act, s_gelu, KF * NC * E)
                    steps.link(copy(b1_now[:, :], b1[:, e, :]))

                def gelu(E, c, f):
                    n = NC * E + c
                    if f == 0:
                        wait(act, s_y, TG * (n - 1))
                    act.wait_ge(s_h, KF * n + f + 1)
                    wait(act, s_hl, KF * n + f - (HF - 1))
                    act.activation(hf[:, f % HF, :], bank(FC1[f % 3]), ACT.Gelu, bias=b1_now[:, f:f + 1],
                                   scale=1.0 / WS).then_inc(s_gelu, 1)
                    act.wait_ge(s_gelu, KF * n + f + 1)
                    copy(hid_h[:, c % 2, f, :], hf[:, f % HF, :], scale=HS).then_inc(s_hh, 1)

                def w1_hi(E):
                    act.wait_ge(s_w1d, 16 * (E + 1))
                    wait(act, s_h, KF * NC * E)
                    for k in range(KD):
                        last = copy(w1_h[:, k, :], w1_st[:, k, :], scale=nws[:, k:k + 1])
                    last.then_inc(s_w1h, 1)

                def w2_hi(E, h):
                    if h == 0:
                        act.wait_ge(s_w2d, 16 * (E + 1))
                        wait(act, s_y, TG * NC * E)
                    part = slice(h * KF // 4, (h + 1) * KF // 4)
                    copy(w2_h[:, part, :], w2_st[:, part, :], scale=WS).then_inc(s_w2h, 1)

                def y_out(E, c):
                    n = NC * E + c
                    if c == 0:
                        act.wait_ge(s_now, E + 1)
                    wait(act, s_sc[c % 2], 16 * TG * ((NC // 2) * E + c // 2))
                    for t in range(TG):
                        k = TG * c + t
                        act.wait_ge(s_y, TG * n + t + 1)
                        copy(ys[:, c % 2, t, :], bank(4 + t % 2)[:, 0:D], scale=w_now[:, k:k + 1]).then_inc(s_ys, 1)

                def expert(e, final=False):
                    E = e + layer * NE
                    bias(e, E)
                    for f in range(KF):
                        gelu(E, 0, f)
                        if f % 4 == 1:
                            w2_hi(E, f // 4)
                    for f in range(KF):
                        gelu(E, 1, f)
                        if f % 4 == 1:
                            w2_hi(E, 2 + f // 4)
                    xt_hi(E, 2)
                    y_out(E, 0)
                    for f in range(KF):
                        gelu(E, 2, f)
                    xt_hi(E, 3)
                    y_out(E, 1)
                    for f in range(KF):
                        gelu(E, 3, f)
                    if not final:
                        w1_hi(E + 1)
                        xt_hi(E + 1, 0)
                    y_out(E, 2)
                    if not final:
                        xt_hi(E + 1, 1)
                    y_out(E, 3)

                act.activation(warm[:, :], nws[:, 0:1], ACT.Gelu)
                w1_hi(layer * NE)
                xt_hi(layer * NE, 0)
                xt_hi(layer * NE, 1)
                repeat(act, steps, expert, NE, lambda e: expert(e, True))

            route(0)
            ffn(0)
            stage_end(act, 2)

            def hi_halves(ready, n, dst, done, b=4):
                for k in range(KD):
                    act.wait_ge(ready, KD * n + (k + 1))
                    copy(dst[:, k * S:(k + 1) * S], bank(b + k)).then_inc(done, 1)

            def pth(a, q):
                act.wait_ge(s_ptp, TG * a + (q + 1))
                wait(act, s_o, TG * a + (q - 1))
                copy(pt_h[:, q % 2, 0:P * (q + 1)], bank(6 + q % 2)[:, 0:P * (q + 1)]).then_inc(s_pth, 1)

            def att_turn(c, u):
                f, a, r = c - 1, c - 2, c - 3
                if on(a):
                    for q in range(TG):
                        act.wait_ge(s_max, TG * a + (q + 1))
                        wait(act, s_ptp, TG * (a - 1) + (q + 1))
                        if q == 0:
                            wait(act, s_x2, TG * (a - 1))
                        act.activation(pr[:, q, 0:P * (q + 1)], bank(q)[:, 0:P * (q + 1)], ACT.Exp,
                                       bias=nbias[:, q:q + 1], scale=SCORE, accum_out=rsum[:, u % 2, q:q + 1]).then_inc(s_prob, 1)
                if on(a):
                    pth(a, 0)
                    pth(a, 1)
                if on(f):
                    wait(act, s_s, TG * (f - 1))
                    hi_halves(s_tp, f + NG, flat(zt_h[:, (u - 1) % 2]), s_th)
                if on(a):
                    pth(a, 2)
                    pth(a, 3)
                if on(r):
                    v = (u - 3) % 2
                    act.wait_ge(s_scale2, r + 1)
                    act.wait_ge(s_lg, r + (NG - 1))
                    wait(act, s_zst[v], 16 * (NG // 2) + 8 * (r - v))
                    normalise(z2[:, v], x2[:, v], 1).then_inc(s_z2, 1)
                if on(f):
                    hi_halves(s_u, f, flat(u_h[:, :, :]), s_uh)
                if on(r):
                    hi_halves(s_z2t, r, flat(z2t_h[:, :, :]), s_z2h, 0)
                if on(f):
                    hi_halves(s_v, f, flat(v_h[:, :, :]), s_vh)
                if on(c):
                    act.wait_ge(s_scale, c + (NG // 2 + 1))
                    wait(act, s_tp, KD * (c + (NG - 1)))
                    normalise(zz[:, u % 2], xin[:, u], 0).then_inc(s_z, 1)

            turns(act, att_turn)
            stage_end(act, 3)
            route(1)
            ffn(1)
            stage_end(act, 4)

        @block.vector
        def _(dve):
            steps = Steps(dve, s_dve)
            link = steps.link

            def bc_j(ap):
                return ap.unsqueeze(2).broadcast_to([P, NE, P])

            dve.wait_ge(s_const, 1)
            dve.wait_ge(s_split, 1)
            link(dve.tensor_scalar(apart[:, :], apart[:, :], NE - 1, None, ALU.bitwise_and))
            link(dve.tensor_scalar(same_expert[:, :], apart[:, :], 0.0, None, ALU.is_equal))
            for k in range(KD):
                link(dve.tensor_tensor(rw_l[:, k, :], rws[:, k, :], rw_h[:, k, :], ALU.subtract))

            def attention_weights():
                dve.wait_ge(s_gmh, 1)
                for n, (lo, hi) in enumerate(((g_l, g_h), (m_l, m_h))):
                    for k in range(KD):
                        dve.scalar_tensor_tensor(lo[:, k, :], bank(4 + n)[:, k * D:(k + 1) * D], WS, hi[:, k, :], ALU.mult, ALU.subtract)

            def stats(src, turn):
                for t in range(TG):
                    steps.done(dve.bn_stats(bst[:, turn, t, :], src[:, t, :]))
                steps.sync()
                dve.sem_inc(s_passed[1], 1)
                for t in range(TG):
                    last = dve.bn_aggr(mv[:, turn, t, :], bst[:, turn, t, :])
                return last

            def tl(g, u):
                for k in range(KD):
                    dve.wait_ge(s_th, KD * g + (k + 1))
                    dve.tensor_tensor(zt_l[:, u, k, :], ps[u][:, k, :], zt_h[:, u, k, :], ALU.subtract).then_inc(s_tl, 1)

            def group_logits(g, b, earlier=0):
                dve.wait_ge(s_lg, g + (earlier + 1))
                dve.scalar_tensor_tensor(logits[:, bass.ds(g * TG, TG), :], bank(b)[:, 0:TG * NE].rearrange("p (t e) -> p t e", t=TG), 1.0 / WS,
                                         rb[:, :].unsqueeze(1).broadcast_to([P, TG, NE]), ALU.mult, ALU.add).then_inc(s_lge, 1)

            def scan_turns(i):
                for w in range(WIDE // 2):
                    g = WIDE * i + 2 * w
                    wait(dve, s_scale, (WIDE // 2) * i + (w - 1))
                    for v in range(2):
                        dve.wait_ge(s_in[2 * w + v], 16 * i + 16)
                        last = stats(xin[:, 2 * w + v], (2 * w + v) % RING)
                    last.then_inc(s_mv, 1)
                    for v in range(2):
                        if on(g + v - 6):
                            group_logits(g + v - 6, 6 + v)
                        if on(g + v - 4):
                            tl(g + v - 4, v)
            repeat(dve, steps, scan_turns, NG // WIDE)
            attention_weights()
            for g in range(NG, NG + 6):
                group_logits(g - 6, 6 + g % 2)
                if g < NG + 4:
                    tl(g - 4, g % 2)
            stage_end(dve, 1)

            def route(layer):
                by_tile = logits[:, :, :]
                mx, inv = rowv[:, 0, :], rowv[:, 1, :]
                over_e = lambda ap: ap.unsqueeze(2).broadcast_to([P, NT, NE])
                dve.wait_ge(s_lge, NG * (layer + 1))
                link(dve.tensor_reduce(mx, by_tile, AX.X, ALU.max))
                dve.tensor_tensor(by_tile, by_tile, over_e(mx), ALU.subtract).then_inc(s_route, 1)
                dve.wait_ge(s_exp, layer + 1)
                link(dve.tensor_reduce(mx, by_tile, AX.X, ALU.add))
                link(dve.reciprocal(inv, mx))
                dve.tensor_tensor(by_tile, by_tile, over_e(inv), ALU.mult).then_inc(s_route, 1)
                dve.wait_ge(s_pt, 2 * layer + 1)
                p_top = flat(ps[1][:, :, :]).bitcast(BF16).rearrange("p (n two) -> p n two", two=2)[:, :, 1]
                dve.tensor_copy(top[:, :], p_top).then_inc(s_top, 1)
                dve.wait_ge(s_top, layer + 1)
                rounds = 0
                key = top
                for part in range(3):
                    floor = 0.0 if part == 0 else MARK
                    step = float(1 << (BITS - 2)) if part == 0 else 64.0
                    dve.memset(found_f[:, :], floor)
                    steps.done(dve.tensor_scalar(steps3[:, :], one_two_three[:, :], step, None, ALU.mult))
                    link(dve.memset(unit[:, :], step))
                    cands = cand if part == 0 else cand_f
                    link(dve.tensor_scalar(cands[:, :], steps3[:, :], floor, None, ALU.add))
                    compare = cand[:, :].bitcast(F32) if part == 0 else cand_f[:, :]
                    for i in range(ROUNDS[part]):
                        for m in range(3):
                            last = dve.tensor_scalar(junk[:, m, :], key[:, :], compare[:, m:m + 1], 0.0, ALU.is_ge, ALU.add,
                                                     accum_out=count[:, m:m + 1])
                        last.then_inc(s_cnt, 1)
                        final = i == ROUNDS[part] - 1
                        if i > 0:
                            steps.sync()
                            steps.done(dve.tensor_scalar(unit[:, :], unit[:, :], 0.25, None, ALU.mult))
                        if not final:
                            link(dve.tensor_scalar(steps3[:, :], steps3[:, :], 0.25, None, ALU.mult))
                            link(dve.tensor_scalar(next3[:, :], steps3[:, :], found_f[:, :], None, ALU.add))
                        rounds += 1
                        dve.wait_ge(s_tot, SEARCH * layer + rounds)
                        link(dve.tensor_scalar(sel[:, :], bank(4)[:, 0:3], float(CAP), 0.0, ALU.is_ge, ALU.add, accum_out=passed[:, :]))
                        if not final:
                            link(dve.scalar_tensor_tensor(cands[:, :], unit[:, :], passed[:, :], next3[:, :], ALU.mult, ALU.add))
                        steps.done(dve.scalar_tensor_tensor(found_f[:, :], unit[:, 0:1], passed[:, :], found_f[:, :], ALU.mult, ALU.add))
                    steps.sync()
                    if part < 2:
                        at = found_f[:, :]
                        if part == 0:
                            link(dve.tensor_copy(thr[:, :], at))
                            at = thr[:, :].bitcast(F32)
                            dve.wait_ge(s_bytes, layer + 1)
                        link(dve.tensor_scalar(junk[:, 0, :], key[:, :], at, None, ALU.is_gt))
                        link(dve.scalar_tensor_tensor(junk[:, 0, :], key[:, :], at, junk[:, 0, :], ALU.is_ge, ALU.add))
                        key = keys[part]
                        link(dve.scalar_tensor_tensor(key[:, :], junk[:, 0, :], MARK, byte[:, part, :], ALU.mult, ALU.add))
                    if part == 1:
                        link(dve.tensor_scalar(low[:, :], found_f[:, :], -MARK, 256.0, ALU.add, ALU.mult))
                link(dve.scalar_tensor_tensor(low_i[:, :], found_f[:, :], -MARK, low[:, :], ALU.add, ALU.add))
                link(dve.tensor_tensor(thr[:, :], thr[:, :], low_i[:, :], ALU.bitwise_or))
                dve.tensor_scalar(thr_m[:, :], ones[:, :], thr[:, :].bitcast(F32), None, ALU.mult).then_inc(s_route, 1)
                thr_b, _, n_equal, need, prev, lim, n_mask, base = (per_expert[:, k, :] for k in range(8))
                dve.wait_ge(s_prr, layer + 1)
                wait_tr(layer, 0)
                link(dve.tensor_copy(thr_b, bank(5)[:, 0:NE]))
                dve.tensor_tensor(above[:, :, :], p_r[:, :, :], bc_j(thr_b), ALU.is_gt).then_inc(s_above, 1)
                link(dve.tensor_tensor(equal[:, :, :], p_r[:, :, :], bc_j(thr_b), ALU.is_equal))
                link(dve.tensor_tensor_scan(flat(scan[:, :, :]), flat(equal[:, :, :]), flat(equal[:, :, :]), 0.0, ALU.add, ALU.bypass))
                link(dve.memset(prev[:, 0:1], 0.0))
                link(dve.tensor_copy(prev[:, 1:NE], scan[:, 0:NE - 1, P - 1]))
                dve.tensor_tensor(n_equal, scan[:, :, P - 1], prev, ALU.subtract).then_inc(s_aux, 1)
                wait_tr(layer, 1)
                link(dve.tensor_scalar(need, bank(5)[:, P:P + NE], -1.0, float(CAP), ALU.mult, ALU.add))
                link(dve.tensor_tensor(lim, need, bank(5)[:, P + NE:P + 2 * NE], ALU.subtract))
                link(dve.tensor_tensor(lim, lim, prev, ALU.add))
                link(dve.tensor_tensor(scan2[:, :, :], scan[:, :, :], bc_j(lim), ALU.is_le))
                link(dve.tensor_tensor(scan2[:, :, :], scan2[:, :, :], equal[:, :, :], ALU.mult))
                dve.tensor_tensor(mask[:, :, :], scan2[:, :, :], above[:, :, :], ALU.add).then_inc(s_mask, 1)
                dve.wait_ge(s_mask, layer + 1)
                link(dve.tensor_tensor_scan(flat(scan[:, :, :]), flat(mask[:, :, :]), flat(mask[:, :, :]), 0.0, ALU.add, ALU.bypass))
                link(dve.tensor_copy(prev[:, 1:NE], scan[:, 0:NE - 1, P - 1]))
                dve.tensor_tensor(n_mask, scan[:, :, P - 1], prev, ALU.subtract).then_inc(s_aux, 1)
                wait_tr(layer, 2)
                link(dve.tensor_tensor(base, bank(5)[:, P + 2 * NE:P + 3 * NE], prev, ALU.subtract))
                link(dve.tensor_scalar(base, base, FAR - 1.0, None, ALU.add))
                link(dve.tensor_tensor(scan2[:, :, :], scan[:, :, :], bc_j(base), ALU.add))
                link(dve.scalar_tensor_tensor(ranks[:, :, :], mask[:, :, :], -FAR, scan2[:, :, :], ALU.mult, ALU.add))
                dve.tensor_scalar(bits_r[:, :, :], ranks[:, :, :], P - 1, None, ALU.bitwise_and).then_inc(s_low, 1)
                link(dve.tensor_scalar(bits[:, :, :], ranks[:, :, :], 7, None, ALU.arith_shift_right))
                link(dve.tensor_copy(rank_c[:, :, :], bits[:, :, :]))
                dve.wait_ge(s_gsum, layer + 1)
                link(dve.tensor_scalar(rowv[:, 0, :], gsum[:, 0, :], 1e-9, None, ALU.max))
                link(dve.reciprocal(rowv[:, 1, :], rowv[:, 0, :]))
                dve.tensor_scalar(rowv[:, 1, :], rowv[:, 1, :], 0.5 / YS, None, ALU.mult).then_inc(s_ginv, 1)

            def wait_tr(layer, k):
                dve.wait_ge(s_trp, 3 * layer + k + 1)

            def hot_values(e, E, v):
                every_c = lambda ap: ap.unsqueeze(1).broadcast_to([P, SLOTS, P])
                if v == 0:
                    wait(dve, s_oh, NC * E)
                    link(dve.tensor_tensor(hot_b[:, 0], iota_c[:, :, :], every_c(rank_c[:, e, :]), ALU.is_equal))
                elif v == 1:
                    steps.done(dve.tensor_tensor(hot_b[:, 1], hot_b[:, 0], every_c(iota_b[:, :]), ALU.mult))
                elif v < NV:
                    steps.done(dve.tensor_tensor(hot_b[:, v], hot_b[:, 0], every_c(wp[:, v - 2, e, :]), ALU.mult))
                else:
                    steps.sync()
                    dve.tensor_scalar(hot_b[:, 0], hot_b[:, 0], part_f[:, :], None, ALU.mult).then_inc(s_values, 1)

            def hot_ranks(e, E, q, part=slice(0, QT)):
                if part.start == 0:
                    wait(dve, s_oh, NC * (E - 1) + q + 1)
                for j in range(part.start, part.stop):
                    last = dve.tensor_scalar(hot_a[:, q, j, :], iota_b[:, :], rank_r[:, e, QT * q + j:QT * q + j + 1], None, ALU.is_equal)
                if part.stop == QT:
                    last.then_inc(s_hot, 1)

            def lists(E):
                dve.wait_ge(s_oh, NC * (E + 1))
                for u in range(2):
                    wait(dve, s_xe[u], 16 * TG * (NC // 2) * E)
                link(dve.tensor_copy(found[:, :, :].rearrange("p v c -> p (v c)"), bank(6)[:, 0:NV * SLOTS]))
                link(dve.tensor_tensor(w_next[:, :], found[:, 2, :], found[:, 3, :], ALU.add))
                link(dve.tensor_tensor(w_next[:, :], w_next[:, :], found[:, 4, :], ALU.add))
                dve.scalar_tensor_tensor(tok_next[:, :], found[:, 0, :], float(P), found[:, 1, :], ALU.mult, ALU.add).then_inc(s_idx, 1)

            def ffn(layer):
                def xt_lo(E, c):
                    n = NC * E + c
                    for k in range(KD):
                        dve.wait_ge(s_xth, KD * n + (k + 1))
                        dve.tensor_tensor(xt_l[:, c % 2, k, :], ps[0][:, k, :], xt_h[:, c % 2, k, :], ALU.subtract).then_inc(s_xtl, 1)

                def hidden_lo(E, c, f):
                    n = NC * E + c
                    dve.wait_ge(s_hh, KF * n + f + 1)
                    dve.scalar_tensor_tensor(hid_l[:, c % 2, f, :], hf[:, f % HF, :], HS, hid_h[:, c % 2, f, :],
                                             ALU.mult, ALU.subtract).then_inc(s_hl, 1)

                def w1_lo(E):
                    dve.wait_ge(s_w1h, E + 1)
                    for k in range(KD):
                        last = dve.scalar_tensor_tensor(w1_l[:, k, :], w1_st[:, k, :], nws[:, k:k + 1], w1_h[:, k, :],
                                                        ALU.mult, ALU.subtract)
                    last.then_inc(s_w1, 1)

                def b2_rows(E):
                    dve.wait_ge(s_b2d, 16 * (E + 1))
                    wait(dve, s_y, TG * NC * E)
                    link(dve.tensor_scalar(b2_h[:, :], b2_st[:, :], YS, None, ALU.mult))
                    link(dve.scalar_tensor_tensor(b2_l[:, :], b2_st[:, :], YS, b2_h[:, :], ALU.mult, ALU.subtract))
                    link(dve.tensor_scalar(b2_h[:, :], b2_h[:, :], pick0[:, :], None, ALU.mult))
                    dve.scalar_tensor_tensor(b2_r[:, :], b2_l[:, :], pick1[:, :], b2_h[:, :], ALU.mult, ALU.add)

                def w2_lo(E, h):
                    dve.wait_ge(s_w2h, 4 * E + h + 1)
                    part = slice(h * KF // 4, (h + 1) * KF // 4)
                    dve.scalar_tensor_tensor(flat(w2_l[:, part, :]), flat(w2_st[:, part, :]), WS, flat(w2_h[:, part, :]),
                                             ALU.mult, ALU.subtract).then_inc(s_w2, 1)

                def to_now(E):
                    wait(dve, s_ys, TG * NC * E)
                    for u in range(2):
                        wait(dve, s_sc[u], 16 * TG * (NC // 2) * E)
                    dve.tensor_copy(w_now[:, :], w_next[:, :])
                    dve.tensor_copy(tok_now[:, :], tok_next[:, :]).then_inc(s_now, 1)

                def expert(e, final=False):
                    E = e + layer * NE
                    for f in range(KF):
                        hidden_lo(E, 0, f)
                        if f == 0:
                            b2_rows(E)
                        elif f % 4 == 1:
                            w2_lo(E, f // 4)
                        elif f % 2 == 0 and not final:
                            hot_values(e + 1, E + 1, f // 2 - 1)
                    for f in range(KF):
                        hidden_lo(E, 1, f)
                        if f % 4 == 1:
                            w2_lo(E, 2 + f // 4)
                        elif f in (0, 2, 4) and not final:
                            hot_values(e + 1, E + 1, 3 + f // 2)
                    xt_lo(E, 2)
                    to_now(E)
                    if not final:
                        hot_ranks(e + 1, E + 1, 0)
                        hot_ranks(e + 1, E + 1, 1, slice(0, QT // 2))
                    for f in range(KF):
                        hidden_lo(E, 2, f)
                        at = f % (KF // 2) * QT // KF
                        if not final:
                            if f < KF // 2:
                                hot_ranks(e + 1, E + 1, 1, slice(QT // 2 + at, QT // 2 + at + QT // KF))
                            else:
                                hot_ranks(e + 1, E + 1, 2, slice(at, at + QT // KF))
                    xt_lo(E, 3)
                    if not final:
                        hot_ranks(e + 1, E + 1, 2, slice(QT // 2, QT))
                        hot_ranks(e + 1, E + 1, 3)
                    if not final:
                        lists(E + 1)
                    for f in range(KF):
                        hidden_lo(E, 3, f)
                    if not final:
                        w1_lo(E + 1)
                        xt_lo(E + 1, 0)
                        xt_lo(E + 1, 1)

                E0 = layer * NE
                hot_values(0, E0, 0)
                hot_values(0, E0, 1)
                dve.wait_ge(s_rank, layer + 1)
                hot_ranks(0, E0, 0)
                hot_ranks(0, E0, 1)
                dve.wait_ge(s_wp, layer + 1)
                for v in range(2, NV + 1):
                    hot_values(0, E0, v)
                hot_ranks(0, E0, 2)
                hot_ranks(0, E0, 3)
                lists(E0)
                w1_lo(E0)
                xt_lo(E0, 0)
                xt_lo(E0, 1)
                repeat(dve, steps, expert, NE, lambda e: expert(e, True))

            route(0)
            ffn(0)
            stage_end(dve, 2)

            def lo_halves(ready, n, dst, hi, done, b=4):
                for k in range(KD):
                    dve.wait_ge(ready, KD * n + (k + 1))
                    cols = slice(k * S, (k + 1) * S)
                    dve.tensor_tensor(dst[:, cols], bank(b + k), hi[:, cols], ALU.subtract).then_inc(done, 1)

            def ptl(a, q):
                dve.wait_ge(s_pth, TG * a + (q + 1))
                dve.tensor_tensor(pt_l[:, q % 2, 0:P * (q + 1)], bank(6 + q % 2)[:, 0:P * (q + 1)],
                                  pt_h[:, q % 2, 0:P * (q + 1)], ALU.subtract).then_inc(s_ptl, 1)

            def residual(a, q, v, ring):
                if q == 0:
                    wait(dve, s_z2, a - 1)
                    wait(dve, s_x2st[v], 8 * (a - v))
                    dve.wait_ge(s_prob, TG * (a + 1))
                    link(dve.tensor_scalar(rinv[:, :], rsum[:, v, :], WS, None, ALU.mult))
                    link(dve.reciprocal(rinv[:, :], rinv[:, :]))
                dve.wait_ge(s_o, TG * a + (q + 1))
                dve.scalar_tensor_tensor(x2[:, v, q, :], bank(q)[:, 0:D], rinv[:, q:q + 1], xin[:, ring, q, :],
                                         ALU.mult, ALU.add).then_inc(s_x2, 1)

            def att_turn(c, u):
                f, a, r, v, ring = c - 1, c - 2, c - 3, u % 2, (u - 2) % RING
                def biases(q):
                    dve.wait_ge(s_s, TG * a + (q + 1))
                    if q == 0:
                        wait(dve, s_prob, TG * a)
                    link(dve.tensor_reduce(nmax[:, q:q + 1], bank(q)[:, 0:P * (q + 1)], AX.X, ALU.max, negate=True))
                    dve.tensor_scalar(nbias[:, q:q + 1], nmax[:, q:q + 1], SCORE, None, ALU.mult).then_inc(s_max, 1)

                if on(a):
                    for q in range(TG):
                        biases(q)
                if on(r - 1):
                    group_logits(r - 1, 7, NG)
                if on(a):
                    ptl(a, 0)
                    ptl(a, 1)
                if on(f):
                    lo_halves(s_th, f + NG, flat(zt_l[:, (u - 1) % 2]), flat(zt_h[:, (u - 1) % 2]), s_tl)
                if on(a):
                    residual(a, 0, v, ring)
                    ptl(a, 2)
                    residual(a, 1, v, ring)
                    ptl(a, 3)
                if on(c):
                    dve.wait_ge(s_in[u], 16 * (NG // WIDE) + ((c - u) * (16 // RING) + 16))
                    dve.wait_ge(s_scale, c + NG // 2)
                    stats(xin[:, u], 0).then_inc(s_mv, 1)
                if on(f):
                    lo_halves(s_uh, f, flat(u_l[:, :, :]), flat(u_h[:, :, :]), s_ul)
                if on(r):
                    lo_halves(s_z2h, r, flat(z2t_l[:, :, :]), flat(z2t_h[:, :, :]), s_z2l, 0)
                if on(a):
                    residual(a, 2, v, ring)
                    residual(a, 3, v, ring)
                if on(a):
                    dve.wait_ge(s_x2, TG * (a + 1))
                    wait(dve, s_scale2, a)
                    stats(x2[:, v], 1).then_inc(s_mv2, 1)
                if on(f):
                    lo_halves(s_vh, f, flat(v_l[:, :, :]), flat(v_h[:, :, :]), s_vl)

            turns(dve, att_turn, steps)
            stage_end(dve, 3)
            route(1)
            ffn(1)
            stage_end(dve, 4)

        @block.tensor
        def _(pe):
            def split3(dst, lhs, rhs, first=True, last=True):
                (lh, ll), (rh, rl) = lhs, rhs
                pe.matmul(dst, lh, rh, start=first, stop=False)
                pe.matmul(dst, lh, rl, start=False, stop=False)
                return pe.matmul(dst, ll, rh, start=False, stop=last)

            pe.wait_ge(s_const, 1)

            def attention_weights():
                pe.wait_ge(s_wst, 16 * 4)
                for a, c, b in ((0, 1, 4), (2, 3, 5)):
                    for m in range(KD):
                        for k in range(KD):
                            last = pe.matmul(bank(b)[:, m * D:(m + 1) * D], wst[:, a, k, m * P:(m + 1) * P], wst[:, c, k, :],
                                             start=(k == 0), stop=(k == KD - 1))
                last.then_inc(s_gm, 1)

            def transposes(dst, src, done, free):
                for k in range(KD):
                    free(k)
                    for t in range(TG):
                        last = pe.transpose(dst[:, k, t * P:(t + 1) * P], src[:, t, k * P:(k + 1) * P], ident[:, :])
                    last.then_inc(done, 1)

            def logit_products(b, hi, lo):
                for t in range(TG):
                    for k in range(KD):
                        for n, (a, w) in enumerate(((hi, rw_h), (hi, rw_l), (lo, rw_h))):
                            last = pe.matmul(bank(b)[:, t * NE:(t + 1) * NE], a[:, k, t * P:(t + 1) * P], w[:, k, :],
                                             start=(k == 0 and n == 0), stop=(k == KD - 1 and n == 2))
                return last

            pe.wait_ge(s_split, 1)

            def tz(g, v):
                pe.wait_ge(s_z, g + 1)
                transposes(ps[v], zz[:, v], s_tp, lambda k: wait(pe, s_tl, KD * (g - 2) + (k + 1)))

            def lg(g, v):
                pe.wait_ge(s_tl, KD * (g + 1))
                wait(pe, s_lge, g - 1)
                logit_products(6 + v, zt_h[:, v], zt_l[:, v]).then_inc(s_lg, 1)

            def scan_turns(i):
                for u in range(RING):
                    g = RING * i + u
                    tz(g, u % 2)
                    if on(g - 1):
                        lg(g - 1, (u - 1) % 2)
            scan_turns(0)
            attention_weights()
            with pe.Fori(1, NG // RING) as i:
                scan_turns(i)
            lg(NG - 1, (NG - 1) % 2)
            stage_end(pe, 1)

            def route(layer):
                pe.wait_ge(s_route, 3 * layer + 2)
                for b in range(NT // PER):
                    last = pe.transpose(ps[1][:, b // 4, (b % 4) * P:(b % 4 + 1) * P], logits[:, b * PER:(b + 1) * PER, :].rearrange("p t e -> p (t e)"), ident[:, :])
                last.then_inc(s_pt, 1)
                for e in range(NE):
                    last = pe.transpose(ps[0][:, e // 4, (e % 4) * P:(e % 4 + 1) * P], logits[:, :, e], ident[:, :])
                last.then_inc(s_pt, 1)
                for i in range(SEARCH):
                    pe.wait_ge(s_cnt, SEARCH * layer + i + 1)
                    pe.matmul(bank(4)[:, 0:3], same_expert[:, :], count[:, :], start=True, stop=True).then_inc(s_tot, 1)
                pe.wait_ge(s_route, 3 * layer + 3)
                pe.transpose(bank(5)[:, 0:P], thr_m[:, :], ident[:, :]).then_inc(s_trp, 1)
                pe.wait_ge(s_aux, 2 * layer + 1)
                pe.wait_ge(s_nabove, layer + 1)
                pe.matmul(bank(5)[:, P:P + NE], ones[:, :], per_expert[:, ABOVE, :], start=True, stop=True)
                pe.matmul(bank(5)[:, P + NE:P + 2 * NE], before[:, :], per_expert[:, EQUAL, :], start=True, stop=True).then_inc(s_trp, 1)
                pe.wait_ge(s_aux, 2 * layer + 2)
                pe.matmul(bank(5)[:, P + 2 * NE:P + 3 * NE], before[:, :], per_expert[:, CHOSEN, :], start=True, stop=True).then_inc(s_trp, 1)

            def ffn(layer):
                def xt(E, c):
                    n = NC * E + c
                    pe.wait_ge(s_xe[c % 2], 16 * TG * ((NC // 2) * E + c // 2 + 1))
                    transposes(ps[0], xe[:, c % 2], s_xt, lambda k: wait(pe, s_xtl, KD * (n - 1) + (k + 1)))

                def fc1(E, c):
                    n = NC * E + c
                    pe.wait_ge(s_xtl, KD * (n + 1))
                    if c == 0:
                        pe.wait_ge(s_w1, E + 1)
                    for f in range(KF):
                        wait(pe, s_gelu, KF * n + (f - 2 if f > 2 else (-1, 0, -2)[f]))
                        for k in range(KD):
                            last = split3(bank(FC1[f % 3]), (w1_h[:, k, f * P:(f + 1) * P], w1_l[:, k, f * P:(f + 1) * P]),
                                          (xt_h[:, c % 2, k, :], xt_l[:, c % 2, k, :]), k == 0, k == KD - 1)
                        last.then_inc(s_h, 1)

                def fc2(E, c):
                    n = NC * E + c
                    pe.wait_ge(s_hl, KF * (n + 1))
                    if c == 0:
                        pe.wait_ge(s_w2, 4 * (E + 1))
                    for t in range(TG):
                        wait(pe, s_ys, TG * n + t - 1)
                        dst = bank(4 + t % 2)[:, 0:D]
                        pe.matmul(dst, ones_h[:, :], b2_r[:, :], start=True, stop=False)
                        for f in range(KF):
                            cols = slice(t * P, (t + 1) * P)
                            last = split3(dst, (hid_h[:, c % 2, f, cols], hid_l[:, c % 2, f, cols]), (w2_h[:, f, :], w2_l[:, f, :]),
                                          False, f == KF - 1)
                        last.then_inc(s_y, 1)

                def one_hot(E, q):
                    pe.wait_ge(s_hot, NC * E + q + 1)
                    if q == 0:
                        pe.wait_ge(s_values, E + 1)
                        wait(pe, s_idx, E)
                    for j in range(QT):
                        col = QT * q + j
                        last = pe.matmul(bank(6)[:, 0:NV * SLOTS], hot_a[:, q, j, :],
                                         hot_b[:, :, :, :].rearrange("p v c j -> p (v c) j")[:, :, col],
                                         start=(col == 0), stop=(col == P - 1))
                    last.then_inc(s_oh, 1)

                def expert(e, final=False):
                    E = e + layer * NE
                    fc1(E, 0)
                    fc1(E, 1)
                    xt(E, 2)
                    fc2(E, 0)
                    if not final:
                        one_hot(E + 1, 0)
                    fc1(E, 2)
                    if not final:
                        one_hot(E + 1, 1)
                    xt(E, 3)
                    fc2(E, 1)
                    if not final:
                        one_hot(E + 1, 2)
                        one_hot(E + 1, 3)
                    fc1(E, 3)
                    if not final:
                        xt(E + 1, 0)
                    fc2(E, 2)
                    if not final:
                        xt(E + 1, 1)
                    fc2(E, 3)

                E0 = layer * NE
                for q in range(NC):
                    one_hot(E0, q)
                xt(E0, 0)
                xt(E0, 1)
                expert(0)
                with pe.Fori(1, NE - 1) as e:
                    expert(e)
                expert(NE - 1, True)

            route(0)
            ffn(0)
            stage_end(pe, 2)

            def scores(a, v, q):
                if q == 0:
                    pe.wait_ge(s_ul, KD * (a + 1))
                wait(pe, s_x2, TG * (a - 1) + q + 1)
                if q < KD:
                    wait(pe, s_z2l, KD * (a - 2) + (q + 1))
                dst = bank(q)[:, 0:P * (q + 1)]
                for k in range(KD):
                    cols = slice(q * P, (q + 1) * P)
                    split3(dst, (u_h[:, k, cols], u_l[:, k, cols]),
                           (zt_h[:, v, k, 0:P * (q + 1)], zt_l[:, v, k, 0:P * (q + 1)]), k == 0, False)
                pe.matmul(bank(q)[:, P * q:P * (q + 1)], ident_b[:, :], causal[:, :], start=False, stop=True).then_inc(s_s, 1)

            def pt(a, q):
                pe.wait_ge(s_prob, TG * a + (q + 1))
                wait(pe, s_ptl, TG * a + (q - 1))
                if q == 1:
                    wait(pe, s_lge, a + (NG - 1))
                for k in range(q + 1):
                    last = pe.transpose(bank(6 + q % 2)[:, k * P:(k + 1) * P], pr[:, q, k * P:(k + 1) * P], ident[:, :])
                last.then_inc(s_ptp, 1)

            def values(a, q):
                pe.wait_ge(s_ptl, TG * a + q + 1)
                if q == 0:
                    pe.wait_ge(s_vl, KD * (a + 1))
                for k in range(q + 1):
                    cols = slice(k * P, (k + 1) * P)
                    last = split3(bank(q)[:, 0:D], (pt_h[:, q % 2, cols], pt_l[:, q % 2, cols]), (v_h[:, k, :], v_l[:, k, :]),
                                  k == 0, k == q)
                last.then_inc(s_o, 1)

            def att_turn(c, u):
                f, a, r = c - 1, c - 2, c - 3
                zf = (u - 1) % 2
                if on(a):
                    for q in range(TG):
                        scores(a, u % 2, q)
                if on(r - 1):
                    wait(pe, s_ptl, TG * (a - 1) + TG if on(a - 1) else TG * NG)
                    pe.wait_ge(s_z2l, KD * r)
                    logit_products(7, z2t_h[:, :, :], z2t_l[:, :, :]).then_inc(s_lg, 1)
                if on(a):
                    pt(a, 0)
                if on(f):
                    def rear_read(k):
                        wait(pe, s_vl, KD * (f - 1) + (k + 1))
                    pe.wait_ge(s_z, f + (NG + 1))
                    transposes(ps[2], zz[:, zf], s_tp, rear_read)
                if on(a):
                    pt(a, 1)
                    values(a, 0)
                    pt(a, 2)
                    values(a, 1)
                    pt(a, 3)
                if on(f):
                    pe.wait_ge(s_tl, KD * (f + (NG + 1)))
                    for m in range(KD):
                        for k in range(KD):
                            last = split3(ps[2][:, m, :], (g_h[:, k, m * P:(m + 1) * P], g_l[:, k, m * P:(m + 1) * P]),
                                          (zt_h[:, zf, k, :], zt_l[:, zf, k, :]), k == 0, k == KD - 1)
                        last.then_inc(s_u, 1)
                if on(r):
                    def front_read(k):
                        pe.wait_ge(s_x2, TG * a + (k + 1) if on(a) else TG * NG)
                    pe.wait_ge(s_z2, r + 1)
                    transposes(ps[0], z2[:, (u - 3) % 2], s_z2t, front_read)
                if on(a):
                    values(a, 2)
                    values(a, 3)
                if on(f):
                    for h in range(2):
                        pe.wait_ge(s_ul, KD * f + (h + 1))
                        for t in (2 * h, 2 * h + 1):
                            for k in range(KD):
                                cols = slice(t * P, (t + 1) * P)
                                last = split3(ps[2][:, h, (t % 2) * D:(t % 2 + 1) * D], (zt_h[:, zf, k, cols], zt_l[:, zf, k, cols]),
                                              (m_h[:, k, :], m_l[:, k, :]), k == 0, k == KD - 1)
                        last.then_inc(s_v, 1)

            turns(pe, att_turn)
            stage_end(pe, 3)
            route(1)
            ffn(1)
            stage_end(pe, 4)


def kernel(L0_attn_x, L0_attn_W_q, L0_attn_W_k, L0_attn_W_v, L0_attn_W_o, L0_ffn_norm_weight, L0_ffn_router_w,
           L0_ffn_router_b, L0_ffn_fc1_w, L0_ffn_fc1_b, L0_ffn_fc2_w, L0_ffn_fc2_b):
    import numpy as np
    import concourse.bacc as bacc
    from concourse.bass_utils import run_bass_kernel_spmd

    def lay(a):
        return np.ascontiguousarray(a)

    experts, ff, _ = L0_ffn_fc1_w.shape
    arrays = {
        "x": lay(L0_attn_x),
        "wq": lay(L0_attn_W_q),
        "wk": lay(L0_attn_W_k),
        "wv": lay(L0_attn_W_v),
        "wo_t": lay(np.asarray(L0_attn_W_o).T),
        "norm_w": lay(np.asarray(L0_ffn_norm_weight).reshape(-1, 128).T),
        "router_t": lay(np.asarray(L0_ffn_router_w).T),
        "router_b": lay(L0_ffn_router_b),
        "fc1_t": lay(np.asarray(L0_ffn_fc1_w).transpose(0, 2, 1)),
        "fc1_b": lay(np.asarray(L0_ffn_fc1_b).reshape(experts, ff // 128, 128).transpose(2, 0, 1)),
        "fc2_t": lay(np.asarray(L0_ffn_fc2_w).transpose(0, 2, 1)),
        "fc2_b": lay(L0_ffn_fc2_b),
    }
    nc = bacc.Bacc("TRN2", target_bir_lowering=False, num_devices=1)
    args = {n: nc.dram_tensor(n, a.shape, mybir.dt.from_np(a.dtype), kind="ExternalInput").ap() for n, a in arrays.items()}
    out = nc.dram_tensor("out", arrays["x"].shape, F32, kind="ExternalOutput").ap()
    macaron(nc, out=out, **args)
    r = run_bass_kernel_spmd(nc, [arrays], core_ids=[0])
    return r.results[0]["out"]
```
